# Optimizing a Trainium2 kernel written in Bass

```python
import numpy as np
import jax
import jax.numpy as jnp

def _softmax(x, axis=-1):
    return jax.nn.softmax(x, axis=axis)

def _gelu(x):
    return jax.nn.gelu(x, approximate=True)

def _silu(x):
    return jax.nn.silu(x)

def _sigmoid(x):
    return jax.nn.sigmoid(x)

def _layernorm(x, axis=-1, eps=1e-05):
    m = jnp.mean(x, axis=axis, keepdims=True)
    v = jnp.var(x, axis=axis, keepdims=True)
    return (x - m) / jnp.sqrt(v + eps)

def _scatter_add(tgt, idx, src, axis=0):
    return tgt.at[idx].add(src)

def _segment_sum(src, seg, n):
    return jax.ops.segment_sum(src, seg, n)
kernel_name = 'mk_gnn_resnorm_d2_gnn_r8_042810'

def setup_inputs(seed: int=0):
    np.random.seed(seed)
    _w = jnp.asarray

    def _rec_inputs():
        import jax
        import jax.numpy as jnp
        _gk = jax.random.key(seed)
        x = -0.0001006 + 1 * jax.random.normal(jax.random.fold_in(_gk, 1), (12500, 96), jnp.float32)
        _s = jax.random.randint(jax.random.fold_in(_gk, 2), (200000,), 0, 12500, jnp.int32)
        _d = jax.random.randint(jax.random.fold_in(_gk, 3), (200000,), 0, 12500, jnp.int32)
        _loop = jnp.arange(12500, dtype=jnp.int32)
        src = jnp.concatenate([_s, _d, _loop])
        dst = jnp.concatenate([_d, _s, _loop])
        _o = jnp.argsort(dst, stable=True)
        src = src[_o]
        dst = dst[_o]
        edge_attr_4 = 0.000714719 + 1.00021 * jax.random.normal(jax.random.fold_in(_gk, 11), (412500, 4), jnp.float32)
        edge_weight1 = 0.000614103 + 0.999867 * jax.random.normal(jax.random.fold_in(_gk, 13), (412500, 1), jnp.float32)
        return (x, src, dst, edge_attr_4, edge_weight1)
    x, src, dst, edge_attr_4, edge_weight1 = _rec_inputs()

    def _L0_gnn_setup():
        import jax, jax.numpy as jnp
        import numpy as np
        N = 6250
        E = 100000
        C = 96

        def _lin_params(key, fan_in, fan_out):
            k1, k2 = jax.random.split(key)
            bound = 1.0 / np.sqrt(fan_in)
            W = jax.random.uniform(k1, (fan_in, fan_out), minval=-bound, maxval=bound, dtype=jnp.float32)
            b = jax.random.uniform(k2, (fan_out,), minval=-bound, maxval=bound, dtype=jnp.float32)
            return (W, b)

        def _gine_conv(x, src, dst, e, W1, b1, W2, b2):
            msg = jax.nn.relu(x[src] + e)
            agg = jax.ops.segment_sum(msg, dst, num_segments=x.shape[0])
            h = x + agg
            h = jax.nn.relu(h @ W1 + b1)
            h = jax.nn.relu(h @ W2 + b2)
            return h
        key = jax.random.key(seed)
        ks = jax.random.split(key, 10)
        x = jax.random.normal(ks[0], (N, C), dtype=jnp.float32)
        edge_index = jax.random.randint(ks[1], (2, E), 0, N, dtype=jnp.int64)
        edge_attr = jax.random.normal(ks[2], (E, 1), dtype=jnp.float32)
        W_l0, b_l0 = _lin_params(ks[3], 1, C)
        W_l1, b_l1 = _lin_params(ks[4], C, C)
        W00, b00 = _lin_params(ks[5], C, C)
        W01, b01 = _lin_params(ks[6], C, C)
        W10, b10 = _lin_params(ks[7], C, C)
        W11, b11 = _lin_params(ks[8], C, C)
        return {'x': x, 'edge_index': edge_index, 'edge_attr': edge_attr, 'W_l0': W_l0, 'b_l0': b_l0, 'W_l1': W_l1, 'b_l1': b_l1, 'W00': W00, 'b00': b00, 'W01': W01, 'b01': b01, 'W10': W10, 'b10': b10, 'W11': W11, 'b11': b11}
    _L0_gnn_all = _L0_gnn_setup()
    _L0_gnn_in = {k: v for k, v in _L0_gnn_all.items() if k in ('W_l0', 'b_l0', 'W_l1', 'b_l1', 'W00', 'b00', 'W01', 'b01', 'W10', 'b10', 'W11', 'b11')}
    del _L0_gnn_all

    def _L1_gnn_setup():
        import jax, jax.numpy as jnp
        import numpy as np
        EPS = 1e-05

        def _mlp(h, W, b, gamma, beta):
            h = jax.nn.relu(h @ W + b)
            mu = jnp.mean(h, axis=0)
            var = jnp.mean(jnp.square(h - mu), axis=0)
            return gamma * (h - mu) * jax.lax.rsqrt(var + EPS) + beta
        key = jax.random.key(seed)
        ks = jax.random.split(key, 10)
        N, E, C_in, C_out, E_dim = (6250, 100000, 96, 96, 4)
        x = jax.random.normal(ks[0], (N, C_in), dtype=jnp.float32)
        edge_index = jax.random.randint(ks[1], (2, E), 0, N, dtype=jnp.int64)
        edge_attr = jax.random.normal(ks[2], (E, E_dim), dtype=jnp.float32)
        s = lambda fan_in: 1.0 / np.sqrt(fan_in)
        W_node = jax.random.uniform(ks[3], (C_in, C_out), jnp.float32, -s(C_in), s(C_in))
        b_node = jnp.zeros((C_out,), jnp.float32)
        g_node = jnp.ones((C_out,), jnp.float32)
        beta_node = jnp.zeros((C_out,), jnp.float32)
        W_edge = jax.random.uniform(ks[4], (E_dim, C_out), jnp.float32, -s(E_dim), s(E_dim))
        b_edge = jnp.zeros((C_out,), jnp.float32)
        g_edge = jnp.ones((C_out,), jnp.float32)
        beta_edge = jnp.zeros((C_out,), jnp.float32)
        M_in = 2 * C_in + C_out
        W_msg = jax.random.uniform(ks[5], (M_in, C_out), jnp.float32, -s(M_in), s(M_in))
        b_msg = jnp.zeros((C_out,), jnp.float32)
        g_msg = jnp.ones((C_out,), jnp.float32)
        beta_msg = jnp.zeros((C_out,), jnp.float32)
        return dict(x=x, edge_index=edge_index, edge_attr=edge_attr, W_node=W_node, b_node=b_node, g_node=g_node, beta_node=beta_node, W_edge=W_edge, b_edge=b_edge, g_edge=g_edge, beta_edge=beta_edge, W_msg=W_msg, b_msg=b_msg, g_msg=g_msg, beta_msg=beta_msg)
    _L1_gnn_all = _L1_gnn_setup()
    _L1_gnn_in = {k: v for k, v in _L1_gnn_all.items() if k in ('W_node', 'b_node', 'g_node', 'beta_node', 'W_edge', 'b_edge', 'g_edge', 'beta_edge', 'W_msg', 'b_msg', 'g_msg', 'beta_msg')}
    del _L1_gnn_all
    return {'x': x, 'src': src, 'dst': dst, 'edge_attr_4': edge_attr_4, 'edge_weight1': edge_weight1, 'L0_gnn_W_l0': _L0_gnn_in['W_l0'], 'L0_gnn_b_l0': _L0_gnn_in['b_l0'], 'L0_gnn_W_l1': _L0_gnn_in['W_l1'], 'L0_gnn_b_l1': _L0_gnn_in['b_l1'], 'L0_gnn_W00': _L0_gnn_in['W00'], 'L0_gnn_b00': _L0_gnn_in['b00'], 'L0_gnn_W01': _L0_gnn_in['W01'], 'L0_gnn_b01': _L0_gnn_in['b01'], 'L0_gnn_W10': _L0_gnn_in['W10'], 'L0_gnn_b10': _L0_gnn_in['b10'], 'L0_gnn_W11': _L0_gnn_in['W11'], 'L0_gnn_b11': _L0_gnn_in['b11'], 'L1_gnn_W_node': _L1_gnn_in['W_node'], 'L1_gnn_b_node': _L1_gnn_in['b_node'], 'L1_gnn_g_node': _L1_gnn_in['g_node'], 'L1_gnn_beta_node': _L1_gnn_in['beta_node'], 'L1_gnn_W_edge': _L1_gnn_in['W_edge'], 'L1_gnn_b_edge': _L1_gnn_in['b_edge'], 'L1_gnn_g_edge': _L1_gnn_in['g_edge'], 'L1_gnn_beta_edge': _L1_gnn_in['beta_edge'], 'L1_gnn_W_msg': _L1_gnn_in['W_msg'], 'L1_gnn_b_msg': _L1_gnn_in['b_msg'], 'L1_gnn_g_msg': _L1_gnn_in['g_msg'], 'L1_gnn_beta_msg': _L1_gnn_in['beta_msg']}

def reference(x, src, dst, edge_attr_4, edge_weight1, L0_gnn_W_l0, L0_gnn_b_l0, L0_gnn_W_l1, L0_gnn_b_l1, L0_gnn_W00, L0_gnn_b00, L0_gnn_W01, L0_gnn_b01, L0_gnn_W10, L0_gnn_b10, L0_gnn_W11, L0_gnn_b11, L1_gnn_W_node, L1_gnn_b_node, L1_gnn_g_node, L1_gnn_beta_node, L1_gnn_W_edge, L1_gnn_b_edge, L1_gnn_g_edge, L1_gnn_beta_edge, L1_gnn_W_msg, L1_gnn_b_msg, L1_gnn_g_msg, L1_gnn_beta_msg):
    import jax
    import jax.numpy as jnp

    def _L0_gnn_ref(x, edge_index, edge_attr, W_l0, b_l0, W_l1, b_l1, W00, b00, W01, b01, W10, b10, W11, b11):
        import jax, jax.numpy as jnp
        import numpy as np
        N = 6250
        E = 100000
        C = 96

        def _lin_params(key, fan_in, fan_out):
            k1, k2 = jax.random.split(key)
            bound = 1.0 / np.sqrt(fan_in)
            W = jax.random.uniform(k1, (fan_in, fan_out), minval=-bound, maxval=bound, dtype=jnp.float32)
            b = jax.random.uniform(k2, (fan_out,), minval=-bound, maxval=bound, dtype=jnp.float32)
            return (W, b)

        def _gine_conv(x, src, dst, e, W1, b1, W2, b2):
            msg = jax.nn.relu(x[src] + e)
            agg = jax.ops.segment_sum(msg, dst, num_segments=x.shape[0])
            h = x + agg
            h = jax.nn.relu(h @ W1 + b1)
            h = jax.nn.relu(h @ W2 + b2)
            return h
        src, dst = (edge_index[0], edge_index[1])
        e = jax.nn.relu(edge_attr @ W_l0 + b_l0) @ W_l1 + b_l1
        h = _gine_conv(x, src, dst, e, W00, b00, W01, b01)
        h = jax.nn.relu(h)
        h = _gine_conv(h, src, dst, e, W10, b10, W11, b11)
        h = jax.nn.relu(h)
        return h

    def _L1_gnn_ref(x, edge_index, edge_attr, W_node, b_node, g_node, beta_node, W_edge, b_edge, g_edge, beta_edge, W_msg, b_msg, g_msg, beta_msg):
        import jax, jax.numpy as jnp
        import numpy as np
        EPS = 1e-05

        def _mlp(h, W, b, gamma, beta):
            h = jax.nn.relu(h @ W + b)
            mu = jnp.mean(h, axis=0)
            var = jnp.mean(jnp.square(h - mu), axis=0)
            return gamma * (h - mu) * jax.lax.rsqrt(var + EPS) + beta
        node_feat = _mlp(x, W_node, b_node, g_node, beta_node)
        edge_feat = _mlp(edge_attr, W_edge, b_edge, g_edge, beta_edge)
        row, col = (edge_index[0], edge_index[1])
        message = jnp.concatenate([x[row], x[col], edge_feat], axis=1)
        message = _mlp(message, W_msg, b_msg, g_msg, beta_msg)
        agg = jax.ops.segment_sum(message, col, num_segments=node_feat.shape[0])
        return agg + node_feat
    edge_index = jnp.stack([src, dst])
    x = _layernorm(x + _L0_gnn_ref(x, edge_index, edge_weight1, L0_gnn_W_l0, L0_gnn_b_l0, L0_gnn_W_l1, L0_gnn_b_l1, L0_gnn_W00, L0_gnn_b00, L0_gnn_W01, L0_gnn_b01, L0_gnn_W10, L0_gnn_b10, L0_gnn_W11, L0_gnn_b11), axis=-1)
    x = _layernorm(x + _L1_gnn_ref(x, edge_index, edge_attr_4, L1_gnn_W_node, L1_gnn_b_node, L1_gnn_g_node, L1_gnn_beta_node, L1_gnn_W_edge, L1_gnn_b_edge, L1_gnn_g_edge, L1_gnn_beta_edge, L1_gnn_W_msg, L1_gnn_b_msg, L1_gnn_g_msg, L1_gnn_beta_msg), axis=-1)
    return x

_drawn_inputs = setup_inputs


def setup_inputs(seed=0):
    import zlib

    import numpy as np

    out = dict(_drawn_inputs(seed))
    spreads = {'L1_gnn_b_node': (0.0, 0.1),
     'L1_gnn_g_node': (1.0, 0.6),
     'L1_gnn_beta_node': (0.0, 0.633),
     'L1_gnn_b_edge': (0.0, 0.1),
     'L1_gnn_g_edge': (1.0, 0.2),
     'L1_gnn_beta_edge': (0.0, 0.1),
     'L1_gnn_b_msg': (0.0, 0.1),
     'L1_gnn_g_msg': (1.0, 0.2),
     'L1_gnn_beta_msg': (0.0, 0.1)}
    factors = {'L0_gnn_b00': 3.708, 'L0_gnn_b10': 8.0, 'L0_gnn_b11': 8.0}
    for name, (base, spread) in spreads.items():
        noise = np.random.default_rng([zlib.crc32(name.encode()), seed]).standard_normal(out[name].shape)
        drawn = base * np.exp(spread * noise) if base else spread * noise
        out[name] = jnp.asarray(drawn.astype(out[name].dtype))
    for name, factor in factors.items():
        out[name] = (out[name] * factor).astype(out[name].dtype)
    return out
```

```python
from contextlib import ExitStack

import concourse.bass as bass
from concourse import mybir

F32 = mybir.dt.float32
BF16 = mybir.dt.bfloat16
I32 = mybir.dt.int32
ALU = mybir.AluOpType
ACT = mybir.ActivationFunctionType
AX_X = mybir.AxisListType.X

P = 128
T = 26
W = 112
R = 32
CH = 4
CHUNKS = [(t, min(CH, T - t)) for t in range(0, T, CH)]
NC_ = len(CHUNKS)
U = 2
Q = U * NC_
NODE_TILES = 2
UN = 10
EPS = 1e-5


def slabs_of(edges):
    return -(-edges // (T * P * U)) * U


def chunk(q):
    t0, nt = CHUNKS[q % NC_]
    return q // NC_, q % NC_, t0, nt


def gnn_kernel(nc, a, out):
    NPAD, C = a["x_rows"].shape
    N = a["nodes"]
    E = a["edges"]
    S = slabs_of(E)
    ITERS = S // U
    STEP = NODE_TILES * P
    STEPS = NPAD // STEP
    TILES = NPAD // P
    EPAD = S * T * P
    C1 = C + 1
    D = a["ea_nat"].shape[0]
    KW = a["w_hid0"].shape[0]
    KE = a["w_hid1"].shape[0]
    HEADS = S * NC_
    COLS = EPAD // P
    PIECE = COLS // ITERS
    assert STEPS % UN == 0 and COLS % ITERS == 0 and S <= P and N < NPAD and C + R <= P

    ctx = ExitStack()
    with ctx:
        def sb(name, shape, dt=F32, where=ctx):
            return where.enter_context(nc.sbuf_tensor(name, shape, dt))

        stage = [0]

        def pools(where, **banks):
            stage[0] += 1
            return {n: [where.enter_context(nc.psum_tensor(f"ps{stage[0]}_{n}{i}", [P, 512], F32)) for i in range(k)]
                    for n, k in banks.items()}

        def sems(where, *names):
            return {n: where.enter_context(nc.semaphore(n)) for n in names}

        sums = sb("sums", [C1, NPAD])
        rel = sb("rel", [P, S * T])
        head_i = sb("head_i", [1, HEADS], I32)
        base_i = sb("base_i", [1, S], I32)
        base_all = sb("base_all", [P, S])
        fits = sb("fits", [1, 1], I32)
        ident = sb("ident", [P, P])
        node_row = sb("node_row", [P, P])
        node_col = sb("node_col", [P, 1])
        first = sb("first", [P, TILES])
        ones = sb("ones", [P, P])
        eps = sb("eps", [P, 1])
        w_hid0 = sb("w_hid0", [KW, C], BF16)
        w_hid1 = sb("w_hid1", [KE + 1, C + R], BF16)
        w_e0 = sb("w_e0", [C1, C])
        w_e1 = sb("w_e1", [C, C])
        w_conv = [[sb(f"w_conv{l}_{i}", [C1, C]) for i in range(2)] for l in range(2)]
        b_conv = [[sb(f"b_conv{l}_{i}", [C, 1]) for i in range(2)] for l in range(2)]
        w_wide = sb("w_wide", [C1, 3 * C])
        w_msg_e = sb("w_msg_e", [C, C])
        b_msg = sb("b_msg", [C1, C])
        gb_edge = sb("gb_edge", [C, 2])
        gb_msg = sb("gb_msg", [C, 2])
        gb_node = sb("gb_node", [P, 2 * C])
        w_fin = sb("w_fin", [C1, C])
        sumsq = sb("sumsq", [P, CH * C])
        slab_mv = sb("slab_mv", [C, S * 2])
        tmp = sb("tmp", [P, 16])
        lift = sb("lift", [C, C1])

        h1_rows = nc.dram_tensor("h1_rows", (NPAD, C), F32, kind="Internal").ap()
        p_rows = nc.dram_tensor("p_rows", (NPAD, C), F32, kind="Internal").ap()
        q_rows = nc.dram_tensor("q_rows", (NPAD, C), F32, kind="Internal").ap()
        w_parts = nc.dram_tensor("w_parts", (4, EPAD), BF16, kind="Internal").ap()
        ea_parts = nc.dram_tensor("ea_parts", (3 * D + 1, EPAD), BF16, kind="Internal").ap()
        near = nc.dram_tensor("near", (S, T * P), BF16, kind="Internal").ap()

        def chain(eng, sem):
            count = [0]

            def go(ins):
                count[0] += 1
                ins.then_inc(sem, 1)
                return count[0]

            def done():
                eng.wait_ge(sem, count[0])
            return go, done

        def split(go, done, v, x, parts):
            for i, part in enumerate(parts):
                go(v.tensor_copy(part, x))
                done()
                if i < 2:
                    go(v.tensor_tensor(x, x, part, ALU.subtract))
                    done()

        with ExitStack() as st:
            dst_i = sb("dst_i", [P, S * T], I32, st)
            dst_n = sb("dst_n", [S, T * P], I32, st)
            near_f = sb("near_f", [S, T * P], F32, st)
            near_b = sb("near_b", [S, T * P], BF16, st)
            inside = sb("inside", [P, T * P], F32, st)
            heads = sb("heads", [1, HEADS], I32, st)
            heads_s = sb("heads_s", [S, NC_], I32, st)
            head_s = sb("head_s", [S, NC_], F32, st)
            head_f = sb("head_f", [1, HEADS], F32, st)
            base_f = sb("base_f", [1, S], F32, st)
            hid_f = [sb(f"hid_f{i}", [k, C], F32, st) for i, k in enumerate((KW, KE))]
            pick = [sb(f"pick{i}", [k, 3], F32, st) for i, k in enumerate((KW, KE))]
            hid_p = [sb(f"hid_p{i}", [KE, C], BF16, st) for i in range(3)]
            hid_t = sb("hid_t", [KE, C], F32, st)
            tail_f = sb("tail_f", [KE + 1, R], F32, st)
            ps = pools(st, base=1, count=1)
            s = sems(st, "u_dst", "u_near", "u_heads", "u_const", "u_dve", "u_base", "u_cnt", "u_pe", "u_nearout", "u_ones")
            loads = [(ident, a["ident"]), (node_row, a["node_row"]), (node_col, a["node_col"]), (first, a["first"]),
                     (hid_f[0], a["w_hid0"]), (w_e0, a["w_e0"]), (hid_f[1], a["w_hid1"]),
                     (pick[0], a["pick0"]), (pick[1], a["pick1"]), (tail_f, a["tail"]),
                     (w_msg_e, a["w_msg_e"]), (b_msg[C:C1, :], a["b_msg"]), (gb_edge, a["gb_edge"]),
                     (gb_msg, a["gb_msg"]), (w_wide, a["w_wide"]), (sums[0:C, :], a["x_cols"]),
                     (gb_node, a["gb_node"].to_broadcast([P, 2 * C]))]
            for l in range(2):
                for i in range(2):
                    loads += [(w_conv[l][i], a[f"w_conv{l}_{i}"]), (b_conv[l][i], a[f"b_conv{l}_{i}"])]
            block = st.enter_context(nc.Block())

            @block.sync
            def _(sp):
                sp.dma_start(heads[:], a["heads"]).then_inc(s["u_heads"], 16)
                sp.dma_start(heads_s[:], a["heads_s"]).then_inc(s["u_heads"], 16)
                sp.dma_start(dst_i[:], a["dst_t"]).then_inc(s["u_dst"], 16)
                sp.dma_start(dst_n[:], a["dst_n"]).then_inc(s["u_near"], 16)
                for to, src in loads:
                    sp.dma_start(to[:] if not isinstance(to, bass.AP) else to, src).then_inc(s["u_const"], 16)
                sp.wait_ge(s["u_const"], 16 * len(loads))
                sp.wait_ge(s["u_near"], 32)
                sp.dma_start(near, near_b[:]).then_inc(s["u_nearout"], 16)
                sp.wait_ge(s["u_nearout"], 16)

            @block.scalar
            def _(act):
                act.dma_start(w_parts[3:4, :], a["is_edge"]).then_inc(s["u_ones"], 16)
                act.dma_start(ea_parts[3 * D:3 * D + 1, :], a["is_edge"]).then_inc(s["u_ones"], 16)
                act.wait_ge(s["u_ones"], 32)

            @block.tensor
            def _(pe):
                pe.wait_ge(s["u_base"], 1)
                pe.matmul(ps["base"][0][:, 0:S], ones[0:1, :], base_f[:], start=True, stop=True).then_inc(s["u_pe"], 1)
                pe.wait_ge(s["u_cnt"], 1)
                pe.matmul(ps["count"][0][:, 0:2], ones[:], tmp[:, 0:2], start=True, stop=True).then_inc(s["u_pe"], 1)

            @block.vector
            def _(v):
                go, done = chain(v, s["u_dve"])
                go(v.memset(ones[:], 1.0))
                go(v.memset(eps[:], EPS))
                go(v.memset(lift[:], 0.0))
                go(v.memset(sumsq[:], 0.0))
                go(v.memset(tmp[:], 0.0))
                go(v.memset(w_hid1[:], 0.0))
                v.wait_ge(s["u_heads"], 32)
                go(v.tensor_scalar(base_f[:], heads[:].rearrange("p (s c) -> p s c", c=NC_)[:, :, 0],
                                   float(N - W), 0.0, ALU.min, ALU.max))
                go(v.tensor_scalar(head_f[:], heads[:], float(N - R), 0.0, ALU.min, ALU.max))
                go(v.tensor_scalar(head_s[:], heads_s[:], float(N - R), 0.0, ALU.min, ALU.max))
                done()
                v.drain().then_inc(s["u_base"], 1)
                go(v.tensor_copy(base_i[:], base_f[:]))
                go(v.tensor_copy(head_i[:], head_f[:]))
                v.wait_ge(s["u_dst"], 16)
                go(v.tensor_copy(rel[:], dst_i[:]))
                v.wait_ge(s["u_pe"], 1)
                go(v.tensor_copy(base_all[:], ps["base"][0][:, 0:S]))
                done()
                rel3 = rel[:].rearrange("p (s t) -> p s t", t=T)
                go(v.tensor_tensor(rel3, rel3, base_all[:].unsqueeze(2).to_broadcast([P, S, T]), ALU.subtract))
                done()
                seen = inside[:, 0:S * T]
                go(v.tensor_scalar(seen, rel[:], 0.0, None, ALU.is_ge))
                done()
                go(v.scalar_tensor_tensor(out=seen, in0=rel[:], scalar=float(W), in1=seen,
                                          op0=ALU.is_lt, op1=ALU.mult, accum_out=tmp[:, 0:1]))
                v.wait_ge(s["u_near"], 16)
                for c, (t0, nt) in enumerate(CHUNKS):
                    go(v.tensor_scalar(near_f[:, t0 * P:(t0 + nt) * P], dst_n[:, t0 * P:(t0 + nt) * P],
                                       head_s[:, c:c + 1], None, ALU.subtract))
                done()
                go(v.tensor_scalar(inside[0:S, :], near_f[:], 0.0, None, ALU.is_ge))
                v.tensor_copy(near_b[:], near_f[:]).then_inc(s["u_near"], 16)
                done()
                go(v.scalar_tensor_tensor(out=inside[0:S, :], in0=near_f[:], scalar=float(R), in1=inside[0:S, :],
                                          op0=ALU.is_lt, op1=ALU.mult, accum_out=tmp[0:S, 1:2]))
                done()
                v.drain().then_inc(s["u_cnt"], 1)
                v.wait_ge(s["u_const"], 16 * len(loads))
                for x, m, to in ((hid_f[0], pick[0], w_hid0[:]), (hid_f[1], pick[1], w_hid1[0:KE, 0:C])):
                    K = x.shape[0]
                    split(go, done, v, x[:], [h[0:K, :] for h in hid_p])
                    go(v.tensor_scalar(hid_t[0:K, :], hid_p[0][0:K, :], m[:, 0:1], None, ALU.mult))
                    done()
                    go(v.scalar_tensor_tensor(out=hid_t[0:K, :], in0=hid_p[1][0:K, :], scalar=m[:, 1:2], in1=hid_t[0:K, :],
                                              op0=ALU.mult, op1=ALU.add))
                    done()
                    go(v.scalar_tensor_tensor(out=to, in0=hid_p[2][0:K, :], scalar=m[:, 2:3], in1=hid_t[0:K, :],
                                              op0=ALU.mult, op1=ALU.add))
                    done()
                go(v.tensor_copy(w_hid1[:, C:C + R], tail_f[:]))
                go(v.memset(sums[C:C1, :], 0.0))
                v.wait_ge(s["u_pe"], 2)
                go(v.tensor_scalar(tmp[0:1, 2:3], ps["count"][0][0:1, 0:1], ps["count"][0][0:1, 1:2], float(2 * E),
                                   ALU.add, ALU.is_equal))
                done()
                go(v.tensor_copy(fits[:], tmp[0:1, 2:3]))
                done()

        def edge_pass(name, table, split_edges=False, stats=False, last=False):
            K = KE + 1 if last else KW
            HC = C + R if last else C
            M = C1 if last else C
            with ExitStack() as st:
                idx = [sb(f"{name}_idx{j}", [P, T], I32, st) for j in range(U)]
                got = [sb(f"{name}_got{j}", [P, T * C], F32, st) for j in range(U)]
                row = [sb(f"{name}_row{j}", [K, T * P], BF16, st) for j in range(U)]
                hid = [sb(f"{name}_hid{i}", [P, CH * P], F32, st) for i in range(2)]
                msg = [sb(f"{name}_msg{i}", [P, CH * C1], F32, st) for i in range(2)]
                hot = [sb(f"{name}_hot{i}", [P, CH * P], F32, st) for i in range(2)]
                dst = sb(f"{name}_dst", [P, T], F32, st)
                off = sb(f"{name}_off", [P, CH], F32, st)
                if last:
                    w_q = [sb(f"{name}_w_q{j}", [P, NC_ * C], F32, st) for j in range(U)]
                    sq = [sb(f"{name}_sq{i}", [P, CH * C], F32, st) for i in range(2)]
                    q_idx = sb(f"{name}_q_idx", [P, T], I32, st)
                if stats:
                    srow = [sb(f"{name}_srow{j}", [KE, T * P], BF16, st) for j in range(U)]
                    feat = [sb(f"{name}_feat{i}", [C, CH * P], F32, st) for i in range(2)]
                    parts = sb(f"{name}_parts", [C, NC_ * 6], F32, st)
                    mv1 = sb(f"{name}_mv1", [C, 2], F32, st)
                if split_edges:
                    w_f = sb(f"{name}_w_f", [P, COLS], F32, st)
                    w_p = [sb(f"{name}_w_p{i}", [P, COLS], BF16, st) for i in range(3)]
                    e_f = [sb(f"{name}_e_f{i}", [P, D * PIECE], F32, st) for i in range(2)]
                    e_p = [sb(f"{name}_e_p{i}", [P, 3 * D * PIECE], BF16, st) for i in range(2)]
                ps = pools(st, hid=2, pre=2, win=2, **(dict(feat=2) if stats else {}))
                names = ["row0", "row1", "idx0", "idx1", "got0", "got1", "win0", "win1", "hid", "rhid", "pre", "add", "msg",
                         "hot", "seg", "init", "slab", "dst", "off"]
                names += ["wf", "wcut", "wout", "ef", "ecut", "estep", "eout"] if split_edges else []
                names += ["srow0", "srow1", "f", "rf", "bn", "flush", "keep"] if stats else []
                names += ["q0", "q1", "hot_t", "sq", "sumsq", "qidx", "qadd"] if last else []
                s = dict(zip(names, sems(st, *[f"{name}_{n}" for n in names]).values()))
                block = st.enter_context(nc.Block())

                def left(k, q, depth=2):
                    return Q * k + max(0, q + 1 - depth)

                def load_rows(sp, j, slab):
                    src, n = (ea_parts, 3 * D + 1) if last else (w_parts, 4)
                    at = bass.ds(slab * (T * P), T * P)
                    for i in range(3):
                        sp.dma_start(row[j][i * n:(i + 1) * n, :], src[:, at]).then_inc(s[f"row{j}"], 16)
                    if last:
                        sp.dma_start(row[j][KE:KE + 1, :], near[bass.ds(slab, 1), :]).then_inc(s[f"row{j}"], 16)
                    if stats:
                        for i in range(3):
                            n = 3 * D + 1
                            sp.dma_start(srow[j][i * n:(i + 1) * n, :], ea_parts[:, at]).then_inc(s[f"srow{j}"], 16)
                ROWS = 16 * (4 if last else 3)

                def load_idx(sp, j, slab):
                    sp.dma_start(idx[j][:], a["src_t"][bass.ds(slab, 1)].rearrange("s p t -> (s p) t")).then_inc(s[f"idx{j}"], 16)

                def hidden(pe, j, q, b, n, free):
                    t0, nt = CHUNKS[q % NC_]
                    pe.wait_ge(s["rhid"], free)
                    if last:
                        pe.wait_ge(s["hot_t"], free)
                    pe.matmul(ps["hid"][b][0:HC, 0:nt * P], (w_hid1 if last else w_hid0)[:], row[j][:, t0 * P:(t0 + nt) * P],
                              start=True, stop=True).then_inc(s["hid"], 1)

                def features(pe, j, q, b, n, free):
                    t0, nt = CHUNKS[q % NC_]
                    pe.wait_ge(s["rf"], free)
                    pe.matmul(ps["feat"][b][0:C, 0:nt * P], w_hid1[0:KE, 0:C], srow[j][:, t0 * P:(t0 + nt) * P],
                              start=True, stop=True).then_inc(s["f"], 1)

                def relu_hidden(act, q, b, n, free):
                    nt = CHUNKS[q % NC_][1]
                    act.wait_ge(s["hid"], n + 1)
                    act.wait_ge(s["pre"], free)
                    act.activation(hid[b][0:C, 0:nt * P], ps["hid"][b][0:C, 0:nt * P], ACT.Relu).then_inc(s["rhid"], 1)

                def relu_features(act, q, b, n, free):
                    nt = CHUNKS[q % NC_][1]
                    act.wait_ge(s["f"], n + 1)
                    act.wait_ge(s["bn"], free)
                    act.activation(feat[b][:, 0:nt * P], ps["feat"][b][0:C, 0:nt * P], ACT.Relu).then_inc(s["rf"], 1)

                def relu_message(act, j, q, b, n, free):
                    t0, nt = CHUNKS[q % NC_]
                    m3 = msg[b][:].rearrange("p (t c) -> p t c", c=C1)[:, 0:nt, 0:C]
                    act.wait_ge(s["add"], n + 1)
                    act.wait_ge(s["seg"], free)
                    act.activation(m3, got[j][:, t0 * C:(t0 + nt) * C].rearrange("p (t c) -> p t c", c=C),
                                   ACT.Relu).then_inc(s["msg"], 1)

                def square_message(act, q, b, n, sq_free):
                    nt = CHUNKS[q % NC_][1]
                    m3 = msg[b][:].rearrange("p (t c) -> p t c", c=C1)[:, 0:nt, 0:C]
                    act.wait_ge(s["msg"], n + 1)
                    act.wait_ge(s["sumsq"], sq_free)
                    act.activation(sq[b][:, 0:nt * C].rearrange("p (t c) -> p t c", c=C), m3,
                                   ACT.Square).then_inc(s["sq"], 1)

                def batch_statistics(v, slab, q, b, n):
                    nt = CHUNKS[q % NC_][1]
                    c = q % NC_
                    v.wait_ge(s["rf"], n + 1)
                    if c == 0:
                        v.wait_ge(s["flush"], slab)
                    v.bn_stats(parts[:, c * 6:(c + 1) * 6], feat[b][:, 0:nt * P]).then_inc(s["bn"], 1)
                    if c == NC_ - 1:
                        v.wait_ge(s["bn"], n + 1)
                        v.wait_ge(s["keep"], slab)
                        v.nop(nofuse=True)
                        v.bn_aggr(mv1[:], parts[:]).then_inc(s["flush"], 1)
                        v.wait_ge(s["flush"], slab + 1)
                        v.tensor_copy(slab_mv[:, bass.ds(slab * 2, 2)], mv1[:]).then_inc(s["keep"], 1)

                def add_gathered(v, j, q, b, n, inc=True):
                    t0, nt = CHUNKS[q % NC_]
                    v.wait_ge(s["pre"], n + 1)
                    at = got[j][:, t0 * C:(t0 + nt) * C]
                    ins = v.tensor_tensor(at, at, ps["pre"][b][:, 0:nt * C], ALU.add)
                    return ins.then_inc(s["add"], 1) if inc else ins

                def add_squares(v, q, b, n):
                    nt = CHUNKS[q % NC_][1]
                    v.wait_ge(s["sq"], n + 1)
                    v.wait_ge(s["sumsq"], n)
                    v.tensor_tensor(sumsq[:, 0:nt * C], sumsq[:, 0:nt * C], sq[b][:, 0:nt * C], ALU.add).then_inc(s["sumsq"], 1)

                def prepare(v):
                    for i in range(2):
                        v.memset(hid[i][64:P, :], 1.0)
                        v.memset(msg[i][:], 1.0)
                    if last:
                        for j in range(U):
                            v.tensor_copy(w_q[j][0:C, :].rearrange("p (k c) -> p k c", c=C),
                                          w_e1[:].unsqueeze(1).to_broadcast([C, NC_, C]))
                    v.drain().then_inc(s["init"], 1)
                    if split_edges:
                        v.wait_ge(s["wf"], 16)
                        go, done = chain(v, s["wcut"])
                        split(go, done, v, w_f[:], [x[:] for x in w_p])

                def sync_windows(sp):
                    with sp.Fori(0, ITERS) as k:
                        for j in range(U):
                            sp.wait_ge(s[f"got{j}"], 16 * T * k)
                            sp.nop(nofuse=True)
                            load_idx(sp, j, k * U + j)
                        if split_edges:
                            sp.wait_ge(s["estep"], k)
                            sp.nop(nofuse=True)
                            sp.dma_start(e_f[0][:].rearrange("p (d i) -> p d i", d=D),
                                         a["ea_nat"][:, :, bass.ds(k * PIECE, PIECE)].rearrange("d p i -> p d i")).then_inc(s["ef"], 16)
                            sp.wait_ge(s["wout"], 48)
                        for j in range(U):
                            sp.wait_ge(s[f"win{j}"], k)
                            sp.nop(nofuse=True)
                            load_rows(sp, j, k * U + j)
                            if last:
                                for c in range(NC_):
                                    h = sp.value_load(head_i[0:1, bass.ds((k * U + j) * NC_ + c, 1)], min_val=0, max_val=N - R)
                                    sp.dma_start(w_q[j][C:C + R, c * C:(c + 1) * C], q_rows[bass.ds(h, R), :]).then_inc(s[f"q{j}"], 16)
                        if split_edges:
                            sp.wait_ge(s["estep"], k + 1)
                            sp.nop(nofuse=True)
                            store_parts(sp, k)
                    if split_edges:
                        sp.wait_ge(s["eout"], 48 * ITERS)

                def store_parts(sp, k):
                    for i in range(3):
                        sp.dma_start(ea_parts[i * D:(i + 1) * D, :].rearrange("d (p i) -> p d i", p=P)[:, :, bass.ds(k * PIECE, PIECE)],
                                     e_p[0][:, i * D * PIECE:(i + 1) * D * PIECE].rearrange("p (d i) -> p d i", d=D)
                                     ).then_inc(s["eout"], 16)

                def split_piece(v, k):
                    v.wait_ge(s["ef"], 16 * (k + 1))
                    v.wait_ge(s["eout"], 48 * k)
                    n = D * PIECE
                    for i in range(3):
                        part = e_p[0][:, i * n:(i + 1) * n]
                        ins = v.tensor_copy(part, e_f[0][:])
                        ins.then_inc(s["estep"] if i == 2 else s["ecut"], 1)
                        if i < 2:
                            v.wait_ge(s["ecut"], 4 * k + 2 * i + 1)
                            v.tensor_tensor(e_f[0][:], e_f[0][:], part, ALU.subtract).then_inc(s["ecut"], 1)
                            v.wait_ge(s["ecut"], 4 * k + 2 * i + 2)

                def gpsimd_windows(gp):
                    with gp.Fori(0, ITERS) as k:
                        for j in range(U):
                            gp.wait_ge(s[f"win{j}"], k)
                            gp.wait_ge(s[f"idx{j}"], 16 * (k + 1))
                            gp.nop(nofuse=True)
                            for t in range(T):
                                gp.indirect_dma_start(got[j][:, t * C:(t + 1) * C], None, table,
                                                      bass.IndirectOffsetOnAxis(idx[j][:, t:t + 1], 0)).then_inc(s[f"got{j}"], 16)

                def tensor_windows(pe):
                    def pre(k, q):
                        j, c, t0, nt = chunk(q)
                        pe.wait_ge(s["rhid"], Q * k + q + 1)
                        pe.wait_ge(s["add"], left(k, q))
                        if last:
                            pe.wait_ge(s["hot_t"], Q * k + q + 1)
                            if c == 0:
                                pe.wait_ge(s[f"q{j}"], 16 * NC_ * (k + 1))
                        for t in range(nt):
                            mm = pe.matmul(ps["pre"][q % 2][:, t * C:(t + 1) * C], hid[q % 2][0:P if last else C1, t * P:(t + 1) * P],
                                           w_q[j][:, c * C:(c + 1) * C] if last else w_e0[:], start=True, stop=True)
                        mm.then_inc(s["pre"], 1)

                    def segment(k, q):
                        j, c, t0, nt = chunk(q)
                        if c == 0:
                            pe.wait_ge(s[f"win{j}"], k)
                        pe.wait_ge(s["msg"], Q * k + q + 1)
                        pe.wait_ge(s["hot"], Q * k + q + 1)
                        for t in range(nt):
                            mm = pe.matmul(ps["win"][j][0:M, 0:W], msg[q % 2][:, t * C1:t * C1 + M],
                                           hot[q % 2][:, t * W:(t + 1) * W],
                                           start=(t0 + t == 0), stop=(t0 + t == T - 1))
                        mm.then_inc(s["seg"], 1)

                    with pe.Fori(0, ITERS) as k:
                        for q in range(Q + 2):
                            if q < Q:
                                j, c, t0, nt = chunk(q)
                                if c == 0:
                                    pe.wait_ge(s[f"row{j}"], ROWS * (k + 1))
                                hidden(pe, j, q, q % 2, Q * k + q, left(k, q))
                                if stats:
                                    if c == 0:
                                        pe.wait_ge(s[f"srow{j}"], 48 * (k + 1))
                                    features(pe, j, q, q % 2, Q * k + q, left(k, q))
                            if 1 <= q <= Q:
                                pre(k, q - 1)
                            if q >= 2:
                                segment(k, q - 2)

                def scalar_windows(act):
                    with act.Fori(0, ITERS) as k:
                        for q in range(Q + 1):
                            if q < Q:
                                relu_hidden(act, q, q % 2, Q * k + q, left(k, q))
                                if stats:
                                    relu_features(act, q, q % 2, Q * k + q, left(k, q))
                            if q >= 1:
                                p = q - 1
                                relu_message(act, chunk(p)[0], p, p % 2, Q * k + p, left(k, p))
                                if last:
                                    square_message(act, p, p % 2, Q * k + p, left(k, p))

                def vector_windows(v):
                    with v.Fori(0, ITERS) as k:
                        if split_edges:
                            split_piece(v, k)
                        for q in range(Q + 3):
                            if q < Q:
                                j, c, t0, nt = chunk(q)
                                if last:
                                    v.wait_ge(s["hid"], Q * k + q + 1)
                                    v.wait_ge(s["pre"], left(k, q))
                                    v.tensor_scalar(hid[q % 2][C:C + R, 0:nt * P], ps["hid"][q % 2][C:C + R, 0:nt * P],
                                                    0.0, None, ALU.is_equal).then_inc(s["hot_t"], 1)
                            if 3 <= q and (q - 3) % NC_ == NC_ - 1:
                                i = (q - 3) // NC_
                                b = v.value_load(base_i[0:1, bass.ds(k * U + i, 1)], min_val=0, max_val=N - W)
                                v.wait_ge(s["seg"], Q * k + q - 2)
                                v.wait_ge(s[f"win{1 - i}"], k + i)
                                at = sums[0:M, bass.ds(b, W)]
                                v.tensor_tensor(at, at, ps["win"][i][0:M, 0:W], ALU.add).then_inc(s[f"win{i}"], 1)
                            if q < Q:
                                v.wait_ge(s["seg"], left(k, q))
                                v.tensor_tensor(hot[q % 2][:, 0:nt * W].rearrange("p (t w) -> p t w", w=W),
                                                node_row[:, 0:W].unsqueeze(1).to_broadcast([P, nt, W]),
                                                rel[:, bass.ds((k * U + j) * T + t0, nt)].unsqueeze(2).to_broadcast([P, nt, W]),
                                                ALU.is_equal).then_inc(s["hot"], 1)
                                if stats:
                                    batch_statistics(v, k * U + j, q, q % 2, Q * k + q)
                            if 1 <= q <= Q:
                                p = q - 1
                                i, c, _, _ = chunk(p)
                                if c == 0:
                                    v.wait_ge(s[f"got{i}"], 16 * T * (k + 1))
                                add_gathered(v, i, p, p % 2, Q * k + p)
                            if last and 2 <= q <= Q + 1:
                                add_squares(v, q - 2, q % 2, Q * k + q - 2)

                NW = TILES

                def sync_general(sp):
                    if split_edges:
                        sp.wait_ge(s["wout"], 48)
                        with sp.Fori(0, ITERS) as k:
                            sp.wait_ge(s["estep"], k)
                            sp.nop(nofuse=True)
                            sp.dma_start(e_f[0][:].rearrange("p (d i) -> p d i", d=D),
                                         a["ea_nat"][:, :, bass.ds(k * PIECE, PIECE)].rearrange("d p i -> p d i")).then_inc(s["ef"], 16)
                            sp.wait_ge(s["estep"], k + 1)
                            sp.nop(nofuse=True)
                            store_parts(sp, k)
                        sp.wait_ge(s["eout"], 48 * ITERS)
                    with sp.Fori(0, S) as k:
                        sp.wait_ge(s["slab"], k)
                        sp.nop(nofuse=True)
                        load_idx(sp, 0, k)
                        load_rows(sp, 0, k)

                def gpsimd_general(gp):
                    with gp.Fori(0, S) as k:
                        gp.wait_ge(s["slab"], k)
                        if last:
                            gp.wait_ge(s["qidx"], k + 1)
                        gp.wait_ge(s["idx0"], 16 * (k + 1))
                        gp.nop(nofuse=True)
                        for t in range(T):
                            gp.indirect_dma_start(got[0][:, t * C:(t + 1) * C], None, table,
                                                  bass.IndirectOffsetOnAxis(idx[0][:, t:t + 1], 0)).then_inc(s["got0"], 16)
                            if last:
                                gp.indirect_dma_start(got[1][:, t * C:(t + 1) * C], None, q_rows,
                                                      bass.IndirectOffsetOnAxis(q_idx[:, t:t + 1], 0)).then_inc(s["got1"], 16)

                def tensor_general(pe):
                    with pe.Fori(0, S) as k:
                        pe.wait_ge(s["row0"], ROWS * (k + 1))
                        if stats:
                            pe.wait_ge(s["srow0"], 48 * (k + 1))
                        for c, (t0, nt) in enumerate(CHUNKS):
                            n = k * NC_ + c
                            hidden(pe, 0, c, 0, n, n)
                            if stats:
                                features(pe, 0, c, 0, n, n)
                            pe.wait_ge(s["rhid"], n + 1)
                            pe.wait_ge(s["add"], n)
                            for t in range(nt):
                                mm = pe.matmul(ps["pre"][0][:, t * C:(t + 1) * C], hid[0][0:C if last else C1, t * P:(t + 1) * P],
                                               (w_e1 if last else w_e0)[:], start=True, stop=True)
                            mm.then_inc(s["pre"], 1)
                            pe.wait_ge(s["msg"], n + 1)
                            pe.nop(nofuse=True)
                            with pe.Fori(0, NW) as w:
                                pe.wait_ge(s["hot"], n * NW + w + 1)
                                pe.wait_ge(s["win0"], n * NW + w)
                                for t in range(nt):
                                    mm = pe.matmul(ps["win"][0][0:M, 0:P], msg[0][:, t * C1:t * C1 + M],
                                                   hot[0][:, t * P:(t + 1) * P], start=(t == 0), stop=(t == nt - 1))
                                mm.then_inc(s["win1"], 1)
                            pe.drain().then_inc(s["seg"], 1)

                def scalar_general(act):
                    with act.Fori(0, S) as k:
                        for c in range(NC_):
                            n = k * NC_ + c
                            relu_hidden(act, c, 0, n, n)
                            if stats:
                                relu_features(act, c, 0, n, n)
                            relu_message(act, 0, c, 0, n, n)
                            if last:
                                square_message(act, c, 0, n, n)

                def vector_general(v):
                    if split_edges:
                        with v.Fori(0, ITERS) as k:
                            split_piece(v, k)
                    with v.Fori(0, S) as k:
                        v.wait_ge(s["slab"], k)
                        v.tensor_scalar(dst[:], rel[:, bass.ds(k * T, T)], base_all[:, bass.ds(k, 1)], None,
                                        ALU.add).then_inc(s["dst"], 1)
                        v.wait_ge(s["dst"], k + 1)
                        if last:
                            v.tensor_scalar(q_idx[:], dst[:], 0.0, None, ALU.max).then_inc(s["qidx"], 1)
                        for c, (t0, nt) in enumerate(CHUNKS):
                            n = k * NC_ + c
                            if last:
                                v.wait_ge(s["hid"], n + 1)
                                v.sem_inc(s["hot_t"], 1)
                            if stats:
                                batch_statistics(v, k, c, 0, n)
                            if c == 0:
                                v.wait_ge(s["got0"], 16 * T * (k + 1))
                            if last:
                                if c == 0:
                                    v.wait_ge(s["got1"], 16 * T * (k + 1))
                                at = got[0][:, t0 * C:(t0 + nt) * C]
                                v.tensor_tensor(at, at, got[1][:, t0 * C:(t0 + nt) * C], ALU.add).then_inc(s["qadd"], 1)
                                v.wait_ge(s["qadd"], n + 1)
                            add_gathered(v, 0, c, 0, n)
                            with v.Fori(0, NW) as w:
                                v.wait_ge(s["win1"], n * NW + w)
                                v.tensor_scalar(off[:, 0:nt], dst[:, t0:t0 + nt], first[:, bass.ds(w, 1)], None,
                                                ALU.subtract).then_inc(s["off"], 1)
                                v.wait_ge(s["off"], n * NW + w + 1)
                                v.tensor_tensor(hot[0][:, 0:nt * P].rearrange("p (t w) -> p t w", w=P),
                                                node_row[:].unsqueeze(1).to_broadcast([P, nt, P]),
                                                off[:, 0:nt].unsqueeze(2).to_broadcast([P, nt, P]),
                                                ALU.is_equal).then_inc(s["hot"], 1)
                                v.wait_ge(s["win1"], n * NW + w + 1)
                                v.wait_ge(s["win0"], n * NW + w)
                                at = sums[0:M, bass.ds(w * P, P)]
                                v.tensor_tensor(at, at, ps["win"][0][0:M, 0:P], ALU.add).then_inc(s["win0"], 1)
                            if last:
                                add_squares(v, c, 0, n)
                        v.drain().then_inc(s["slab"], 1)

                def both(eng, windows, general):
                    flag = eng.value_load(fits[:], min_val=0, max_val=1)
                    with eng.If(flag == 1):
                        windows(eng)
                    with eng.Else():
                        general(eng)

                @block.sync
                def _(sp):
                    if split_edges:
                        sp.dma_start(w_f[:], a["w_nat"].rearrange("o p i -> (o p) i")).then_inc(s["wf"], 16)
                    both(sp, sync_windows, sync_general)

                @block.gpsimd
                def _(gp):
                    both(gp, gpsimd_windows, gpsimd_general)

                @block.tensor
                def _(pe):
                    pe.wait_ge(s["init"], 1)
                    both(pe, tensor_windows, tensor_general)

                @block.scalar
                def _(act):
                    act.wait_ge(s["init"], 1)
                    if split_edges:
                        act.wait_ge(s["wcut"], 5)
                        for i in range(3):
                            act.dma_start(w_parts[i:i + 1, :].rearrange("o (p i) -> (o p) i", p=P), w_p[i][:]).then_inc(s["wout"], 16)
                    both(act, scalar_windows, scalar_general)

                @block.vector
                def _(v):
                    prepare(v)
                    both(v, vector_windows, vector_general)

        def node_mlp(l, y=None, mv=None):
            with ExitStack() as st:
                z = [sb(f"n{l}_z{i}", [C1, STEP], F32, st) for i in range(2)]
                ps = pools(st, a=2, b=2, c=2)
                s = sems(st, *[f"n{l}_{n}" for n in ("init", "a", "z", "b", "c", "row", "col", "out0", "out1", "st", "x")])
                s = {n[3:]: x for n, x in s.items()}
                if l == 0:
                    rows_out = [sb(f"n0_rows{i}", [P, NODE_TILES * C], F32, st) for i in range(2)]
                else:
                    parts = sb("n1_parts", [P, UN * NODE_TILES * 6], F32, st)
                    some = sb("n1_some", [P, UN * NODE_TILES * 2], F32, st)
                block = st.enter_context(nc.Block())

                def left(k, q):
                    return UN * k + max(0, q - 1)

                @block.tensor
                def _(pe):
                    pe.wait_ge(s["init"], 1)
                    with pe.Fori(0, STEPS // UN) as k:
                        for q in range(UN + 1):
                            if q < UN:
                                pe.wait_ge(s["z"], left(k, q))
                                pe.matmul(ps["a"][q % 2][0:C, 0:STEP], w_conv[l][0][0:C, :],
                                          sums[0:C, bass.ds((k * UN + q) * STEP, STEP)], start=True, stop=True).then_inc(s["a"], 1)
                            if q >= 1:
                                p = q - 1
                                pe.wait_ge(s["z"], UN * k + p + 1)
                                pe.wait_ge(s["row"], left(k, p))
                                for t in range(NODE_TILES):
                                    mm = pe.matmul(ps["b"][p % 2][:, t * C:(t + 1) * C], z[p % 2][:, t * P:(t + 1) * P],
                                                   w_conv[l][1][:], start=True, stop=True)
                                mm.then_inc(s["b"], 1)
                                if l == 0:
                                    pe.wait_ge(s["col"], left(k, p))
                                    pe.matmul(ps["c"][p % 2][0:C, 0:STEP], w_conv[l][1][0:C, :], z[p % 2][0:C, :],
                                              start=True, stop=True).then_inc(s["c"], 1)

                @block.scalar
                def _(act):
                    with act.Fori(0, STEPS // UN) as k:
                        for q in range(UN + 1):
                            if q < UN:
                                act.wait_ge(s["a"], UN * k + q + 1)
                                act.wait_ge(s["c"] if l == 0 else s["b"], left(k, q))
                                act.activation(z[q % 2][0:C, :], ps["a"][q % 2][0:C, 0:STEP], ACT.Relu,
                                               bias=b_conv[l][0][:]).then_inc(s["z"], 1)
                            if q >= 1 and l == 0:
                                p = q - 1
                                act.wait_ge(s["c"], UN * k + p + 1)
                                act.activation(sums[0:C, bass.ds((k * UN + p) * STEP, STEP)], ps["c"][p % 2][0:C, 0:STEP],
                                               ACT.Relu, bias=b_conv[l][1][:]).then_inc(s["col"], 1)

                @block.vector
                def _(v):
                    for i in range(2):
                        v.memset(z[i][C:C1, :], 1.0)
                    v.drain().then_inc(s["init"], 1)
                    if l == 1:
                        v.wait_ge(s["x"], 16)
                    with v.Fori(0, STEPS // UN) as k:
                        for q in range(UN):
                            v.wait_ge(s["b"], UN * k + q + 1)
                            if l == 0:
                                v.wait_ge(s[f"out{q % 2}"], (UN // 2 * k + q // 2) * 16)
                                v.tensor_scalar(rows_out[q % 2][:], ps["b"][q % 2][:, 0:NODE_TILES * C], 0.0, None,
                                                ALU.max).then_inc(s["row"], 1)
                            else:
                                at = y[:, bass.ds((k * UN + q) * NODE_TILES * C, NODE_TILES * C)]
                                v.scalar_tensor_tensor(out=at, in0=ps["b"][q % 2][:, 0:NODE_TILES * C], scalar=0.0, in1=at,
                                                       op0=ALU.max, op1=ALU.add).then_inc(s["row"], 1)
                        if l == 1:
                            moments(v, s["row"], UN * (k + 1), s["st"], k, y, parts, some, mv)

                if l == 0:
                    @block.sync
                    def _(sp):
                        with sp.Fori(0, STEPS // UN) as k:
                            for q in range(UN):
                                sp.wait_ge(s["row"], UN * k + q + 1)
                                sp.dma_start(h1_rows[bass.ds((k * UN + q) * STEP, STEP), :].rearrange("(t p) c -> p t c", p=P),
                                             rows_out[q % 2][:].rearrange("p (t c) -> p t c", c=C)).then_inc(s[f"out{q % 2}"], 16)
                        for i in range(2):
                            sp.wait_ge(s[f"out{i}"], 16 * (STEPS // 2))
                else:
                    @block.sync
                    def _(sp):
                        sp.dma_start(y[:], a["x_tiles"]).then_inc(s["x"], 16)
                        sp.wait_ge(s["x"], 16)

        def moments(v, ready, count, sem, k, y, parts, some, mv):
            n = UN * NODE_TILES
            v.wait_ge(ready, count)
            v.wait_ge(sem, (2 * n + 1) * k)
            for t in range(n):
                v.bn_stats(parts[:, t * 6:(t + 1) * 6], y[:, bass.ds((k * n + t) * C, C)]).then_inc(sem, 1)
            v.wait_ge(sem, (2 * n + 1) * k + n)
            v.nop(nofuse=True)
            for t in range(n):
                v.bn_aggr(some[:, 2 * t:2 * t + 2], parts[:, t * 6:(t + 1) * 6]).then_inc(sem, 1)
            v.wait_ge(sem, (2 * n + 1) * k + 2 * n)
            v.tensor_copy(mv[:, bass.ds(k * n * 2, n * 2)], some[:]).then_inc(sem, 1)

        def scales(v, act, go, done, sem_v, sem_a, mv, rstd, shift):
            mv3 = mv[:].rearrange("p (t m) -> p m t", m=2)
            if act is not None:
                act.activation(rstd[:], mv3[:, 1, :], ACT.Sqrt, bias=eps[:]).then_inc(sem_a, 1)
                return
            v.wait_ge(sem_a, 1)
            go(v.reciprocal(rstd[:], rstd[:]))
            done()
            go(v.scalar_tensor_tensor(out=shift[:], in0=mv3[:, 0, :], scalar=-1.0, in1=rstd[:], op0=ALU.mult, op1=ALU.mult))
            done()

        def fold(v, go, done, sqrt_in, sqrt_out, mean, ex2, gb):
            go(v.tensor_tensor(tmp[0:C, 2:3], mean, mean, ALU.mult))
            done()
            go(v.tensor_tensor(tmp[0:C, 3:4], ex2, tmp[0:C, 2:3], ALU.subtract))
            done()
            v.drain().then_inc(sqrt_in, 1)
            v.wait_ge(sqrt_out, 1)
            go(v.reciprocal(tmp[0:C, 6:7], tmp[0:C, 3:4]))
            done()
            go(v.tensor_tensor(tmp[0:C, 4:5], tmp[0:C, 6:7], gb[:, 0:1], ALU.mult))
            done()
            go(v.tensor_tensor(tmp[0:C, 5:6], mean, tmp[0:C, 4:5], ALU.mult))
            done()
            go(v.tensor_tensor(lift[:, C:C1], gb[:, 1:2], tmp[0:C, 5:6], ALU.subtract))
            done()

        def message_inputs(y, mv, nf):
            with ExitStack() as st:
                rstd = sb("m_rstd", [P, TILES], F32, st)
                shift = sb("m_shift", [P, TILES], F32, st)
                xs = [sb(f"m_xs{i}", [P, NODE_TILES * C], F32, st) for i in range(2)]
                xt = [sb(f"m_xt{i}", [C1, STEP], F32, st) for i in range(2)]
                slab_sq = sb("m_slab_sq", [C, S], F32, st)
                none = sb("m_none", [1, C], F32, st)
                rows_out = [sb(f"m_rows{i}", [P, 2, NODE_TILES * C], F32, st) for i in range(2)]
                ps = pools(st, xt=2, pq=2, nf=2, f=1)
                s = sems(st, *[f"m_{n}" for n in ("sqrt", "dve", "f_in", "f_out", "f_pe", "x", "xp", "xt", "wide", "nf", "pq",
                                                  "out0", "out1", "init", "clear", "y")])
                s = {n[2:]: x for n, x in s.items()}
                block = st.enter_context(nc.Block())

                def left(k, q):
                    return UN * k + max(0, q - 1)

                @block.gpsimd
                def _(gp):
                    gp.memset(sums[:], 0.0).then_inc(s["clear"], 1)
                    with gp.Fori(0, STEPS // UN) as k:
                        for q in range(UN):
                            gp.wait_ge(s["x"], NODE_TILES * (UN * k + q + 1))
                            gp.tensor_copy(y[:, bass.ds((k * UN + q) * NODE_TILES * C, NODE_TILES * C)],
                                           xs[q % 2][:]).then_inc(s["y"], 1)
                    gp.wait_ge(s["clear"], 1)
                    gp.wait_ge(s["y"], STEPS)

                @block.tensor
                def _(pe):
                    pe.wait_ge(s["f_in"], 2)
                    pe.matmul(ps["f"][0][0:C1, 0:C], lift[:], w_msg_e[:], start=True, stop=True).then_inc(s["f_pe"], 1)
                    pe.wait_ge(s["init"], 1)
                    with pe.Fori(0, STEPS // UN) as k:
                        for q in range(UN + 1):
                            if q < UN:
                                pe.wait_ge(s["x"], NODE_TILES * (UN * k + q + 1))
                                pe.wait_ge(s["xt"], left(k, q))
                                for t in range(NODE_TILES):
                                    mm = pe.transpose(ps["xt"][q % 2][0:C, t * P:(t + 1) * P],
                                                      xs[q % 2][:, t * C:(t + 1) * C], ident[:])
                                mm.then_inc(s["xp"], 1)
                            if q >= 1:
                                p = q - 1
                                pe.wait_ge(s["xt"], UN * k + p + 1)
                                pe.wait_ge(s["nf"], left(k, p))
                                pe.wait_ge(s["pq"], left(k, p))
                                for t in range(NODE_TILES):
                                    x_t = xt[p % 2][:, t * P:(t + 1) * P]
                                    pe.matmul(ps["pq"][p % 2][:, t * 2 * C:(t + 1) * 2 * C], x_t, w_wide[:, 0:2 * C],
                                              start=True, stop=True)
                                    mm = pe.matmul(ps["nf"][p % 2][:, t * C:(t + 1) * C], x_t, w_wide[:, 2 * C:3 * C],
                                                   start=True, stop=True)
                                mm.then_inc(s["wide"], 1)

                @block.scalar
                def _(act):
                    scales(None, act, None, None, None, s["sqrt"], mv, rstd, shift)
                    act.wait_ge(s["f_in"], 1)
                    act.activation(tmp[0:C, 3:4], tmp[0:C, 3:4], ACT.Sqrt, bias=eps[0:C, :]).then_inc(s["f_out"], 1)
                    with act.Fori(0, STEPS // UN) as k:
                        for q in range(UN + 2):
                            if 1 <= q <= UN:
                                p = q - 1
                                act.wait_ge(s["xp"], UN * k + p + 1)
                                act.wait_ge(s["wide"], left(k, p))
                                act.copy(xt[p % 2][0:C, :], ps["xt"][p % 2][0:C, 0:STEP]).then_inc(s["xt"], 1)
                            if q >= 2:
                                p = q - 2
                                act.wait_ge(s["wide"], UN * k + p + 1)
                                act.wait_ge(s[f"out{p % 2}"], (UN // 2 * k + p // 2) * 32)
                                act.copy(rows_out[p % 2][:].rearrange("p h (t c) -> p t h c", c=C),
                                         ps["pq"][p % 2][:, 0:NODE_TILES * 2 * C].rearrange("p (t h c) -> p t h c", h=2, c=C)
                                         ).then_inc(s["pq"], 1)

                @block.vector
                def _(v):
                    go, done = chain(v, s["dve"])
                    for i in range(2):
                        go(v.memset(xt[i][C:C1, :], 1.0))
                    go(v.memset(none[:], -3e38))
                    done()
                    mv3 = slab_mv[:].rearrange("p (s m) -> p m s", m=2)
                    go(v.tensor_tensor(slab_sq[:], mv3[:, 0, :], mv3[:, 0, :], ALU.mult))
                    done()
                    go(v.tensor_tensor(slab_sq[:], slab_sq[:], mv3[:, 1, :], ALU.add))
                    done()
                    go(v.tensor_reduce(tmp[0:C, 8:9], mv3[:, 0, :], AX_X, ALU.add))
                    go(v.tensor_reduce(tmp[0:C, 9:10], slab_sq[:], AX_X, ALU.add))
                    done()
                    go(v.tensor_scalar(tmp[0:C, 8:10], tmp[0:C, 8:10], float(T * P) / E, None, ALU.mult))
                    done()
                    fold(v, go, done, s["f_in"], s["f_out"], tmp[0:C, 8:9], tmp[0:C, 9:10], gb_edge)
                    v.drain().then_inc(s["f_in"], 1)
                    go(v.tensor_scalar(w_e1[:], w_msg_e[:], tmp[0:C, 4:5], None, ALU.mult))
                    v.wait_ge(s["f_pe"], 1)
                    go(v.tensor_tensor(w_wide[C:C1, C:2 * C], ps["f"][0][C:C1, 0:C], b_msg[C:C1, :], ALU.add))
                    done()
                    v.drain().then_inc(s["init"], 1)
                    scales(v, None, go, done, None, s["sqrt"], mv, rstd, shift)
                    with v.Fori(0, STEPS // UN) as k:
                        for q in range(UN + 2):
                            if q < UN:
                                v.wait_ge(s["xp"], left(k, q))
                                v.wait_ge(s["y"], left(k, q))
                                for t in range(NODE_TILES):
                                    tile = (k * UN + q) * NODE_TILES + t
                                    v.tensor_scalar(xs[q % 2][:, t * C:(t + 1) * C], y[:, bass.ds(tile * C, C)],
                                                    rstd[:, bass.ds(tile, 1)], shift[:, bass.ds(tile, 1)],
                                                    ALU.mult, ALU.add).then_inc(s["x"], 1)
                            if q >= 2:
                                p = q - 2
                                v.wait_ge(s["wide"], UN * k + p + 1)
                                v.tensor_scalar(nf[:, bass.ds((k * UN + p) * NODE_TILES * C, NODE_TILES * C)],
                                                ps["nf"][p % 2][:, 0:NODE_TILES * C], 0.0, None, ALU.max).then_inc(s["nf"], 1)
                @block.sync
                def _(sp):
                    with sp.Fori(0, STEPS // UN) as k:
                        for q in range(UN):
                            sp.wait_ge(s["pq"], UN * k + q + 1)
                            for h, table in enumerate((p_rows, q_rows)):
                                sp.dma_start(table[bass.ds((k * UN + q) * STEP, STEP), :].rearrange("(t p) c -> p t c", p=P),
                                             rows_out[q % 2][:, h, :].rearrange("p (t c) -> p t c", c=C)
                                             ).then_inc(s[f"out{q % 2}"], 16)
                    for i in range(2):
                        sp.wait_ge(s[f"out{i}"], 32 * (STEPS // 2))
                    sp.dma_start(p_rows[NPAD - 1:NPAD, :], none[:]).then_inc(s["out0"], 16)
                    sp.wait_ge(s["out0"], 32 * (STEPS // 2) + 16)

        def node_norm(y, nf):
            with ExitStack() as st:
                nf_sq = sb("b_sq", [P, TILES * C], F32, st)
                tot = sb("b_tot", [P, 2 * C], F32, st)
                mom = sb("b_mom", [P, 2 * C], F32, st)
                var = sb("b_var", [P, C], F32, st)
                ps = pools(st, tot=1)
                s = sems(st, "b_dve", "b_sqr", "b_go", "b_pe", "b_root")
                block = st.enter_context(nc.Block())
                full, part = divmod(N, P)

                @block.scalar
                def _(act):
                    act.wait_ge(s["b_go"], 1)
                    act.activation(nf_sq[:], nf[:], ACT.Square).then_inc(s["b_sqr"], 1)
                    act.wait_ge(s["b_go"], 3)
                    act.activation(var[:], var[:], ACT.Sqrt, bias=eps[:]).then_inc(s["b_root"], 1)

                @block.tensor
                def _(pe):
                    pe.wait_ge(s["b_go"], 2)
                    pe.matmul(ps["tot"][0][:, 0:2 * C], ones[:], tot[:], start=True, stop=True).then_inc(s["b_pe"], 1)

                @block.vector
                def _(v):
                    go, done = chain(v, s["b_dve"])
                    go(v.tensor_scalar(tmp[:, 0:1], node_col[:], float(part), None, ALU.is_lt))
                    done()
                    go(v.tensor_scalar(nf[:, full * C:(full + 1) * C], nf[:, full * C:(full + 1) * C], tmp[:, 0:1], None, ALU.mult))
                    if full + 1 < TILES:
                        go(v.memset(nf[:, (full + 1) * C:], 0.0))
                    done()
                    v.drain().then_inc(s["b_go"], 1)
                    go(v.tensor_reduce(tot[:, 0:C], nf[:].rearrange("p (t c) -> p c t", c=C), AX_X, ALU.add))
                    v.wait_ge(s["b_sqr"], 1)
                    go(v.tensor_reduce(tot[:, C:2 * C], nf_sq[:].rearrange("p (t c) -> p c t", c=C), AX_X, ALU.add))
                    done()
                    v.drain().then_inc(s["b_go"], 1)
                    v.wait_ge(s["b_pe"], 1)
                    go(v.tensor_scalar(mom[:], ps["tot"][0][:, 0:2 * C], 1.0 / N, None, ALU.mult))
                    done()
                    go(v.tensor_tensor(var[:], mom[:, 0:C], mom[:, 0:C], ALU.mult))
                    done()
                    go(v.tensor_tensor(var[:], mom[:, C:2 * C], var[:], ALU.subtract))
                    done()
                    v.drain().then_inc(s["b_go"], 1)
                    v.wait_ge(s["b_root"], 1)
                    go(v.reciprocal(var[:], var[:]))
                    done()
                    go(v.tensor_tensor(tot[:, 0:C], var[:], gb_node[:, 0:C], ALU.mult))
                    done()
                    go(v.tensor_tensor(var[:], mom[:, 0:C], tot[:, 0:C], ALU.mult))
                    done()
                    go(v.tensor_tensor(tot[:, C:2 * C], gb_node[:, C:2 * C], var[:], ALU.subtract))
                    nf3 = nf[:].rearrange("p (t c) -> p t c", c=C)
                    y3 = y[:].rearrange("p (t c) -> p t c", c=C)
                    go(v.tensor_tensor(nf3, nf3, tot[:, 0:C].unsqueeze(1).to_broadcast([P, TILES, C]), ALU.mult))
                    done()
                    go(v.tensor_tensor(y3, y3, tot[:, C:2 * C].unsqueeze(1).to_broadcast([P, TILES, C]), ALU.add))
                    done()
                    go(v.tensor_tensor(y[:], y[:], nf[:], ALU.add))
                    done()

        def finish(y, mv):
            with ExitStack() as st:
                rstd = sb("o_rstd", [P, TILES], F32, st)
                shift = sb("o_shift", [P, TILES], F32, st)
                part = [sb(f"o_sum{i}", [C1, STEP], F32, st) for i in range(2)]
                parts = sb("o_parts", [P, UN * NODE_TILES * 6], F32, st)
                some = sb("o_some", [P, UN * NODE_TILES * 2], F32, st)
                ps = pools(st, f=1, sq=1, y=2)
                s = sems(st, *[f"o_{n}" for n in ("dve", "f_in", "f_out", "f_pe", "sq", "w", "sum", "pe", "y", "st", "sqrt", "n0", "n1",
                                                  "go", "out")])
                s = {n[2:]: x for n, x in s.items()}
                block = st.enter_context(nc.Block())
                n = UN * NODE_TILES

                def left(k, q):
                    return UN * k + max(0, q - 1)

                @block.tensor
                def _(pe):
                    for i in range(CH):
                        mm = pe.matmul(ps["sq"][0][0:C, 0:1], sumsq[:, i * C:(i + 1) * C], ones[:, 0:1], start=(i == 0), stop=(i == CH - 1))
                    mm.then_inc(s["sq"], 1)
                    pe.wait_ge(s["f_in"], 2)
                    pe.matmul(ps["f"][0][0:C1, 0:C], lift[:], ident[0:C, 0:C], start=True, stop=True).then_inc(s["f_pe"], 1)
                    pe.wait_ge(s["w"], 1)
                    with pe.Fori(0, STEPS // UN) as k:
                        for q in range(UN):
                            pe.wait_ge(s["sum"], UN * k + q + 1)
                            pe.wait_ge(s["y"], left(k, q))
                            for t in range(NODE_TILES):
                                mm = pe.matmul(ps["y"][q % 2][:, t * C:(t + 1) * C], part[q % 2][:, t * P:(t + 1) * P], w_fin[:],
                                               start=True, stop=True)
                            mm.then_inc(s["pe"], 1)

                @block.scalar
                def _(act):
                    act.wait_ge(s["f_in"], 1)
                    act.activation(tmp[0:C, 3:4], tmp[0:C, 3:4], ACT.Sqrt, bias=eps[0:C, :]).then_inc(s["f_out"], 1)
                    with act.Fori(0, STEPS // UN) as k:
                        for q in range(UN):
                            act.wait_ge(s["pe"], left(k, q))
                            act.copy(part[q % 2][:], sums[:, bass.ds((k * UN + q) * STEP, STEP)]).then_inc(s["sum"], 1)
                    act.wait_ge(s["st"], 2 * TILES + STEPS // UN)
                    scales(None, act, None, None, None, s["sqrt"], mv, rstd, shift)
                    act.wait_ge(s["go"], 1)
                    with act.Fori(0, STEPS // UN) as k:
                        for t in range(1, n, 2):
                            tile = k * n + t
                            at = y[:, bass.ds(tile * C, C)]
                            act.activation(at, at, ACT.Identity, scale=rstd[:, bass.ds(tile, 1)],
                                           bias=shift[:, bass.ds(tile, 1)]).then_inc(s["n1"], 1)

                @block.vector
                def _(v):
                    go, done = chain(v, s["dve"])
                    go(v.tensor_reduce(tmp[0:C, 8:9], sums[0:C, :], AX_X, ALU.add))
                    done()
                    go(v.tensor_scalar(tmp[0:C, 9:10], tmp[0:C, 8:9], 1.0 / E, None, ALU.mult))
                    v.wait_ge(s["sq"], 1)
                    go(v.tensor_scalar(tmp[0:C, 10:11], ps["sq"][0][0:C, 0:1], 1.0 / E, None, ALU.mult))
                    done()
                    fold(v, go, done, s["f_in"], s["f_out"], tmp[0:C, 9:10], tmp[0:C, 10:11], gb_msg)
                    v.drain().then_inc(s["f_in"], 1)
                    go(v.tensor_scalar(w_fin[0:C, :], ident[0:C, 0:C], tmp[0:C, 4:5], None, ALU.mult))
                    v.wait_ge(s["f_pe"], 1)
                    go(v.tensor_copy(w_fin[C:C1, :], ps["f"][0][C:C1, 0:C]))
                    done()
                    v.drain().then_inc(s["w"], 1)
                    with v.Fori(0, STEPS // UN) as k:
                        for q in range(UN):
                            v.wait_ge(s["pe"], UN * k + q + 1)
                            at = y[:, bass.ds((k * UN + q) * NODE_TILES * C, NODE_TILES * C)]
                            v.tensor_tensor(at, at, ps["y"][q % 2][:, 0:NODE_TILES * C], ALU.add).then_inc(s["y"], 1)
                        moments(v, s["y"], UN * (k + 1), s["st"], k, y, parts, some, mv)
                    scales(v, None, go, done, None, s["sqrt"], mv, rstd, shift)
                    v.drain().then_inc(s["go"], 1)
                    with v.Fori(0, STEPS // UN) as k:
                        for t in range(0, n, 2):
                            tile = k * n + t
                            at = y[:, bass.ds(tile * C, C)]
                            v.tensor_scalar(at, at, rstd[:, bass.ds(tile, 1)], shift[:, bass.ds(tile, 1)],
                                            ALU.mult, ALU.add).then_inc(s["n0"], 1)

                @block.sync
                def _(sp):
                    with sp.Fori(0, STEPS // UN) as k:
                        sp.wait_ge(s["n0"], n // 2 * (k + 1))
                        sp.wait_ge(s["n1"], n // 2 * (k + 1))
                        sp.dma_start(out[bass.ds(k * n * P, n * P), :].rearrange("(t p) c -> p t c", p=P),
                                     y[:, bass.ds(k * n * C, n * C)].rearrange("p (t c) -> p t c", c=C)).then_inc(s["out"], 16)
                    sp.wait_ge(s["out"], 16 * (STEPS // UN))

        mv_x = sb("mv_x", [P, TILES * 2])
        edge_pass("conv0", a["x_rows"], split_edges=True)
        node_mlp(0)
        edge_pass("conv1", h1_rows, stats=True)
        y = sb("y", [P, TILES * C])
        node_mlp(1, y, mv_x)
        with ExitStack() as scope:
            nf = sb("nf", [P, TILES * C], F32, scope)
            message_inputs(y, mv_x, nf)
            node_norm(y, nf)
        edge_pass("last", p_rows, last=True)
        finish(y, mv_x)


def kernel(x, src, dst, edge_attr_4, edge_weight1, **w):
    import numpy as np
    import concourse.bacc as bacc
    from concourse.bass_utils import run_bass_kernel_spmd

    N, C = x.shape
    E = src.shape[0]
    S = slabs_of(E)
    EPAD = S * T * P
    NPAD = -(-N // (UN * NODE_TILES * P)) * UN * NODE_TILES * P
    f32 = np.float32

    def padded(v, n, fill):
        v = np.asarray(v)
        return np.concatenate([v, np.full((n - v.shape[0],) + v.shape[1:], fill, v.dtype)])

    def row(v):
        return np.asarray(v).reshape(1, -1)

    def col(v):
        return np.asarray(v).reshape(-1, 1)

    def parts_of(W, b):
        return np.tile(np.concatenate([W, W, W, b]), (3, 1))

    D = edge_attr_4.shape[1]
    rows = padded(x, NPAD, 0)
    src_p = padded(src, EPAD, NPAD - 1).reshape(S, T, P)
    dst_p = padded(dst, EPAD, -1).reshape(S, T, P)
    heads = dst_p[:, ::CH, 0]
    tail = np.zeros((3 * (3 * D + 1) + 1, R), f32)
    tail[3 * D] = -np.arange(R)
    tail[-1] = 1
    W_msg = np.asarray(w["L1_gnn_W_msg"])
    zero = np.zeros((1, C), f32)
    arrays = {
        "x_rows": rows,
        "x_tiles": rows.reshape(-1, P, C).transpose(1, 0, 2).reshape(P, -1),
        "x_cols": rows.T,
        "src_t": src_p.transpose(0, 2, 1),
        "dst_t": dst_p.transpose(2, 0, 1).reshape(P, S * T),
        "dst_n": dst_p.reshape(S, T * P),
        "heads": heads.reshape(1, -1),
        "heads_s": heads,
        "w_nat": padded(edge_weight1, EPAD, 0).reshape(1, P, -1),
        "ea_nat": padded(edge_attr_4, EPAD, 0).T.reshape(D, P, -1),
        "is_edge": (np.arange(EPAD) < E).astype(mybir.dt.np(BF16)).reshape(1, -1),
        "ident": np.eye(P, dtype=f32),
        "node_row": np.tile(np.arange(P, dtype=f32), (P, 1)),
        "node_col": np.arange(P, dtype=f32).reshape(P, 1),
        "first": np.tile(np.arange(0, NPAD, P, dtype=f32), (P, 1)),
        "w_hid0": parts_of(w["L0_gnn_W_l0"], row(w["L0_gnn_b_l0"])),
        "w_e0": np.concatenate([w["L0_gnn_W_l1"], row(w["L0_gnn_b_l1"])]),
        "w_hid1": parts_of(w["L1_gnn_W_edge"], row(w["L1_gnn_b_edge"])),
        "pick0": np.repeat(np.eye(3, dtype=f32), 4, axis=0),
        "pick1": np.repeat(np.eye(3, dtype=f32), 3 * D + 1, axis=0),
        "tail": tail,
        "w_msg_e": W_msg[2 * C:],
        "b_msg": row(w["L1_gnn_b_msg"]),
        "w_wide": np.concatenate([np.concatenate([W_msg[:C], W_msg[C:2 * C], w["L1_gnn_W_node"]], axis=1),
                                  np.concatenate([zero, zero, row(w["L1_gnn_b_node"])], axis=1)]),
        "gb_edge": np.concatenate([col(w["L1_gnn_g_edge"]), col(w["L1_gnn_beta_edge"])], axis=1),
        "gb_msg": np.concatenate([col(w["L1_gnn_g_msg"]), col(w["L1_gnn_beta_msg"])], axis=1),
        "gb_node": np.concatenate([row(w["L1_gnn_g_node"]), row(w["L1_gnn_beta_node"])], axis=1),
    }
    for l in range(2):
        for i in range(2):
            arrays[f"w_conv{l}_{i}"] = np.concatenate([w[f"L0_gnn_W{l}{i}"], row(w[f"L0_gnn_b{l}{i}"])])
            arrays[f"b_conv{l}_{i}"] = col(w[f"L0_gnn_b{l}{i}"])
    arrays = {f"in_{n}": np.ascontiguousarray(v) for n, v in arrays.items()}

    nc = bacc.Bacc("TRN2", target_bir_lowering=False, num_devices=1)
    aps = {n: nc.dram_tensor(n, v.shape, mybir.dt.from_np(v.dtype), kind="ExternalInput").ap() for n, v in arrays.items()}
    out = nc.dram_tensor("out", (NPAD, C), F32, kind="ExternalOutput").ap()
    gnn_kernel(nc, {n[3:]: v for n, v in aps.items()} | {"edges": E, "nodes": N}, out)
    r = run_bass_kernel_spmd(nc, [arrays], core_ids=[0])
    return r.results[0]["out"][:N]
```

```python
from contextlib import ExitStack

import concourse.bass as bass
from concourse import mybir

F32 = mybir.dt.float32
BF16 = mybir.dt.bfloat16
I32 = mybir.dt.int32
ALU = mybir.AluOpType
ACT = mybir.ActivationFunctionType
AX_X = mybir.AxisListType.X

P = 128
T = 26
W = 112
R = 32
CH = 4
CHUNKS = [(t, min(CH, T - t)) for t in range(0, T, CH)]
NC_ = len(CHUNKS)
U = 2
Q = U * NC_
NODE_TILES = 2
UN = 10
EPS = 1e-5


def slabs_of(edges):
    return -(-edges // (T * P * U)) * U


GROUPS = [(0, (NC_ + 1) // 2 - 1), ((NC_ + 1) // 2, NC_ - 1)]


def group_tiles(g):
    first, last = GROUPS[g]
    return CHUNKS[first][0], sum(CHUNKS[last])


def need(eng, sem, count):
    if not isinstance(count, int) or count > 0:
        eng.wait_ge(sem, count)


def repeat(eng, n, body):
    body(0)
    if n > 1:
        with eng.Fori(1, n) as k:
            body(k)


def staged(eng, iters, width, plan, ahead=None):
    def body(k):
        if ahead:
            ahead(k)
        for q in range(width):
            for lag, stage in plan:
                if q >= lag:
                    stage(k, q - lag)
                elif not isinstance(k, int):
                    stage(k - 1, q - lag + width)
    repeat(eng, iters, body)
    for q in range(max(lag for lag, _ in plan)):
        for lag, stage in plan:
            if q < lag:
                stage(iters - 1, width + q - lag)


def chunk(q):
    t0, nt = CHUNKS[q % NC_]
    return q // NC_, q % NC_, t0, nt


def gnn_kernel(nc, a, out):
    NPAD, C = a["x_rows"].shape
    N = a["nodes"]
    E = a["edges"]
    S = slabs_of(E)
    ITERS = S // U
    STEP = NODE_TILES * P
    STEPS = NPAD // STEP
    TILES = NPAD // P
    EPAD = S * T * P
    C1 = C + 1
    D = a["ea_nat"].shape[0]
    KW = a["w_hid0"].shape[0]
    KE = a["w_hid1"].shape[0]
    HEADS = S * NC_
    COLS = EPAD // P
    PIECE = COLS // ITERS
    assert STEPS % UN == 0 and COLS % ITERS == 0 and S <= P and N < NPAD and C + R <= P

    ctx = ExitStack()
    with ctx:
        def sb(name, shape, dt=F32, where=ctx):
            return where.enter_context(nc.sbuf_tensor(name, shape, dt))

        stage = [0]

        def pools(where, **banks):
            stage[0] += 1
            return {n: [where.enter_context(nc.psum_tensor(f"ps{stage[0]}_{n}{i}", [P, 512], F32)) for i in range(k)]
                    for n, k in banks.items()}

        class Sems(dict):
            def __init__(self, where, block):
                self.where, self.block = where, block

            def __missing__(self, n):
                self[n] = self.where.enter_context(nc.semaphore(f"{self.block}_{n}"))
                return self[n]

        sums = sb("sums", [C1, NPAD])
        rel = sb("rel", [P, S * T])
        head_i = sb("head_i", [1, HEADS], I32)
        base_i = sb("base_i", [1, S], I32)
        base_all = sb("base_all", [P, S])
        fits = sb("fits", [1, 1], I32)
        ident = sb("ident", [P, P])
        node_row = sb("node_row", [P, P])
        first = sb("first", [P, TILES])
        ones = sb("ones", [P, P])
        eps = sb("eps", [P, 1])
        w_hid0 = sb("w_hid0", [KW, C], BF16)
        w_hid1 = sb("w_hid1", [KE + 1, C + R], BF16)
        w_e0 = sb("w_e0", [C1, C])
        w_e1 = sb("w_e1", [C, C])
        w_conv = [[sb(f"w_conv{l}_{i}", [C1, C]) for i in range(2)] for l in range(2)]
        b_conv = [[sb(f"b_conv{l}_{i}", [C, 1]) for i in range(2)] for l in range(2)]
        w_wide = sb("w_wide", [C1, 3 * C])
        w_msg_e = sb("w_msg_e", [C, C])
        b_msg = sb("b_msg", [C1, C])
        gb_edge = sb("gb_edge", [C, 2])
        gb_msg = sb("gb_msg", [C, 2])
        gb_node = sb("gb_node", [P, 2 * C])
        w_fin = sb("w_fin", [C + 2, C])
        node_g = sb("node_g", [P, C])
        node_b = sb("node_b", [P, C])
        is_node = sb("is_node", [P, TILES])
        sumsq = sb("sumsq", [P, CH * C])
        slab_mv = sb("slab_mv", [C, S * 2])
        tmp = sb("tmp", [P, 16])
        lift = sb("lift", [C, C + 2])

        h1_rows = nc.dram_tensor("h1_rows", (NPAD, C), F32, kind="Internal").ap()
        p_rows = nc.dram_tensor("p_rows", (NPAD, C), F32, kind="Internal").ap()
        q_rows = nc.dram_tensor("q_rows", (NPAD, C), F32, kind="Internal").ap()
        w_parts = nc.dram_tensor("w_parts", (4, EPAD), BF16, kind="Internal").ap()
        ea_parts = nc.dram_tensor("ea_parts", (3 * D + 1, EPAD), BF16, kind="Internal").ap()
        near = nc.dram_tensor("near", (S, T * P), BF16, kind="Internal").ap()

        def chain(eng, sem):
            count = [0]

            def go(ins):
                count[0] += 1
                ins.then_inc(sem, 1)
                return count[0]

            def done():
                eng.wait_ge(sem, count[0])
            return go, done

        def split(go, done, v, x, parts):
            for i, part in enumerate(parts):
                go(v.tensor_copy(part, x))
                done()
                if i < 2:
                    go(v.tensor_tensor(x, x, part, ALU.subtract))
                    done()

        with ExitStack() as st:
            dst_i = sb("dst_i", [P, S * T], I32, st)
            dst_n = sb("dst_n", [S, T * P], I32, st)
            near_f = sb("near_f", [S, T * P], F32, st)
            near_b = sb("near_b", [S, T * P], BF16, st)
            inside = sb("inside", [P, T * P], F32, st)
            heads = sb("heads", [1, HEADS], I32, st)
            heads_s = sb("heads_s", [S, NC_], I32, st)
            head_s = sb("head_s", [S, NC_], F32, st)
            head_f = sb("head_f", [1, HEADS], F32, st)
            base_f = sb("base_f", [1, S], F32, st)
            ps = pools(st, base=1, count=1)
            s = Sems(st, "setup")
            loads = [(ident, a["ident"]), (node_row, a["node_row"]), (first, a["first"]), (is_node, a["is_node"]),
                     (w_e0, a["w_e0"]),
                     (w_msg_e, a["w_msg_e"]), (b_msg[C:C1, :], a["b_msg"]), (gb_edge, a["gb_edge"]),
                     (gb_msg, a["gb_msg"]), (w_wide, a["w_wide"]), (sums[0:C, :], a["x_cols"]),
                     (gb_node, a["gb_node"].to_broadcast([P, 2 * C]))]
            for l in range(2):
                for i in range(2):
                    loads += [(w_conv[l][i], a[f"w_conv{l}_{i}"]), (b_conv[l][i], a[f"b_conv{l}_{i}"])]
            block = st.enter_context(nc.Block())

            @block.sync
            def _(sp):
                sp.dma_start(heads[:], a["heads"]).then_inc(s["heads"], 16)
                sp.dma_start(heads_s[:], a["heads_s"]).then_inc(s["heads"], 16)
                sp.dma_start(dst_i[:], a["dst_t"]).then_inc(s["dst"], 16)
                sp.dma_start(dst_n[:], a["dst_n"]).then_inc(s["near"], 16)
                for to, src in loads:
                    sp.dma_start(to[:] if not isinstance(to, bass.AP) else to, src).then_inc(s["const"], 16)
                sp.wait_ge(s["const"], 16 * len(loads))
                sp.wait_ge(s["near"], 32)
                sp.dma_start(near, near_b[:]).then_inc(s["nearout"], 16)
                sp.wait_ge(s["nearout"], 16)

            @block.scalar
            def _(act):
                act.dma_start(w_parts[3:4, :], a["is_edge"]).then_inc(s["ones"], 16)
                act.dma_start(ea_parts[3 * D:3 * D + 1, :], a["is_edge"]).then_inc(s["ones"], 16)
                act.wait_ge(s["ones"], 32)

            @block.tensor
            def _(pe):
                pe.wait_ge(s["base"], 1)
                pe.matmul(ps["base"][0][:, 0:S], ones[0:1, :], base_f[:], start=True, stop=True).then_inc(s["pe"], 1)
                pe.wait_ge(s["cnt"], 1)
                pe.matmul(ps["count"][0][:, 0:2], ones[:], tmp[:, 0:2], start=True, stop=True).then_inc(s["pe"], 1)

            @block.vector
            def _(v):
                go, done = chain(v, s["dve"])
                go(v.memset(ones[:], 1.0))
                go(v.memset(eps[:], EPS))
                go(v.memset(lift[:], 0.0))
                go(v.memset(sumsq[:], 0.0))
                go(v.memset(tmp[:], 0.0))
                v.wait_ge(s["heads"], 32)
                go(v.tensor_scalar(base_f[:], heads[:].rearrange("p (s c) -> p s c", c=NC_)[:, :, 0],
                                   float(N - W), 0.0, ALU.min, ALU.max))
                go(v.tensor_scalar(head_f[:], heads[:], float(N - R), 0.0, ALU.min, ALU.max))
                go(v.tensor_scalar(head_s[:], heads_s[:], float(N - R), 0.0, ALU.min, ALU.max))
                done()
                v.drain().then_inc(s["base"], 1)
                go(v.tensor_copy(base_i[:], base_f[:]))
                go(v.tensor_copy(head_i[:], head_f[:]))
                v.wait_ge(s["dst"], 16)
                go(v.tensor_copy(rel[:], dst_i[:]))
                v.wait_ge(s["pe"], 1)
                go(v.tensor_copy(base_all[:], ps["base"][0][:, 0:S]))
                done()
                rel3 = rel[:].rearrange("p (s t) -> p s t", t=T)
                go(v.tensor_tensor(rel3, rel3, base_all[:].unsqueeze(2).to_broadcast([P, S, T]), ALU.subtract))
                done()
                seen = inside[:, 0:S * T]
                go(v.tensor_scalar(seen, rel[:], 0.0, None, ALU.is_ge))
                done()
                go(v.scalar_tensor_tensor(out=seen, in0=rel[:], scalar=float(W), in1=seen,
                                          op0=ALU.is_lt, op1=ALU.mult, accum_out=tmp[:, 0:1]))
                v.wait_ge(s["near"], 16)
                for c, (t0, nt) in enumerate(CHUNKS):
                    go(v.tensor_scalar(near_f[:, t0 * P:(t0 + nt) * P], dst_n[:, t0 * P:(t0 + nt) * P],
                                       head_s[:, c:c + 1], None, ALU.subtract))
                done()
                go(v.tensor_scalar(inside[0:S, :], near_f[:], 0.0, None, ALU.is_ge))
                v.tensor_copy(near_b[:], near_f[:]).then_inc(s["near"], 16)
                done()
                go(v.scalar_tensor_tensor(out=inside[0:S, :], in0=near_f[:], scalar=float(R), in1=inside[0:S, :],
                                          op0=ALU.is_lt, op1=ALU.mult, accum_out=tmp[0:S, 1:2]))
                done()
                v.drain().then_inc(s["cnt"], 1)
                v.wait_ge(s["pe"], 2)
                go(v.tensor_scalar(tmp[0:1, 2:3], ps["count"][0][0:1, 0:1], ps["count"][0][0:1, 1:2], float(2 * E),
                                   ALU.add, ALU.is_equal))
                done()
                go(v.tensor_copy(fits[:], tmp[0:1, 2:3]))
                done()

        def edge_pass(name, table, split_edges=False, stats=False, last=False):
            K = KE + 1 if last else KW
            HC = C + R if last else C
            M = C1 if last else C
            with ExitStack() as st:
                idx = [sb(f"{name}_idx{j}", [P, T], I32, st) for j in range(U)]
                got = [sb(f"{name}_got{j}", [P, T * C], F32, st) for j in range(U)]
                row = [sb(f"{name}_row{j}", [K, T * P], BF16, st) for j in range(U)]
                hid = [sb(f"{name}_hid{i}", [P, CH * P], F32, st) for i in range(2)]
                msg = [sb(f"{name}_msg{i}", [P, CH * C1], F32, st) for i in range(2)]
                hot = [sb(f"{name}_hot{i}", [P, CH * P], F32, st) for i in range(2)]
                dst = sb(f"{name}_dst", [P, T], F32, st)
                off = sb(f"{name}_off", [P, CH], F32, st)
                if last:
                    w_q = [sb(f"{name}_w_q{j}", [P, NC_ * C], F32, st) for j in range(U)]
                    sq = [sb(f"{name}_sq{i}", [P, CH * C], F32, st) for i in range(2)]
                    q_idx = sb(f"{name}_q_idx", [P, T], I32, st)
                if stats:
                    srow = [sb(f"{name}_srow{j}", [KE, T * P], BF16, st) for j in range(U)]
                    feat = [sb(f"{name}_feat{i}", [C, CH * P], F32, st) for i in range(2)]
                    parts = sb(f"{name}_parts", [C, NC_ * 6], F32, st)
                    mv1 = sb(f"{name}_mv1", [C, 2], F32, st)
                if split_edges:
                    w_f = sb(f"{name}_w_f", [P, COLS], F32, st)
                    w_p = [sb(f"{name}_w_p{i}", [P, COLS], BF16, st) for i in range(3)]
                    e_f = sb(f"{name}_e_f", [P, D * PIECE], F32, st)
                    e_p = sb(f"{name}_e_p", [P, 3 * D * PIECE], BF16, st)
                    hid_f = [sb(f"hid_f{i}", [k, C], F32, st) for i, k in enumerate((KW, KE))]
                    pick = [sb(f"pick{i}", [k, 3], F32, st) for i, k in enumerate((KW, KE))]
                    hid_p = [sb(f"hid_p{i}", [KE, C], BF16, st) for i in range(3)]
                    hid_t = sb("hid_t", [KE, C], F32, st)
                    tail_f = sb("tail_f", [KE + 1, R], F32, st)
                    hid_loads = [(hid_f[0], a["w_hid0"]), (hid_f[1], a["w_hid1"]), (pick[0], a["pick0"]),
                                 (pick[1], a["pick1"]), (tail_f, a["tail"])]
                ps = pools(st, hid=2, pre=2, win=2, **(dict(feat=2) if stats else {}))
                s = Sems(st, name)
                block = st.enter_context(nc.Block())

                def left(k, q):
                    return Q * k + q - 1

                def load_rows(sp, j, slab):
                    src, n = (ea_parts, 3 * D + 1) if last else (w_parts, 4)
                    at = bass.ds(slab * (T * P), T * P)
                    for i in range(3):
                        sp.dma_start(row[j][i * n:(i + 1) * n, :], src[:, at]).then_inc(s[f"row{j}"], 16)
                    if last:
                        sp.dma_start(row[j][KE:KE + 1, :], near[bass.ds(slab, 1), :]).then_inc(s[f"row{j}"], 16)
                    if stats:
                        for i in range(3):
                            n = 3 * D + 1
                            sp.dma_start(srow[j][i * n:(i + 1) * n, :], ea_parts[:, at]).then_inc(s[f"srow{j}"], 16)
                ROWS = 16 * (4 if last else 3)

                def load_idx(sp, j, slab):
                    sp.dma_start(idx[j][:], a["src_t"][bass.ds(slab, 1)].rearrange("s p t -> (s p) t")).then_inc(s[f"idx{j}"], 16)

                def hidden(pe, j, q, b, n, free):
                    t0, nt = CHUNKS[q % NC_]
                    need(pe, s["rhid"], free)
                    if last:
                        need(pe, s["hot_t"], free)
                    pe.matmul(ps["hid"][b][0:HC, 0:nt * P], (w_hid1 if last else w_hid0)[:], row[j][:, t0 * P:(t0 + nt) * P],
                              start=True, stop=True).then_inc(s["hid"], 1)

                def features(pe, j, q, b, n, free):
                    t0, nt = CHUNKS[q % NC_]
                    need(pe, s["rf"], free)
                    pe.matmul(ps["feat"][b][0:C, 0:nt * P], w_hid1[0:KE, 0:C], srow[j][:, t0 * P:(t0 + nt) * P],
                              start=True, stop=True).then_inc(s["f"], 1)

                def relu_hidden(act, q, b, n, free):
                    nt = CHUNKS[q % NC_][1]
                    act.wait_ge(s["hid"], n + 1)
                    need(act, s["pre"], free)
                    act.activation(hid[b][0:C, 0:nt * P], ps["hid"][b][0:C, 0:nt * P], ACT.Relu).then_inc(s["rhid"], 1)

                def relu_features(act, q, b, n, free):
                    nt = CHUNKS[q % NC_][1]
                    act.wait_ge(s["f"], n + 1)
                    need(act, s["bn"], free)
                    act.activation(feat[b][:, 0:nt * P], ps["feat"][b][0:C, 0:nt * P], ACT.Relu).then_inc(s["rf"], 1)

                def relu_message(act, j, q, b, n, free):
                    t0, nt = CHUNKS[q % NC_]
                    m3 = msg[b][:].rearrange("p (t c) -> p t c", c=C1)[:, 0:nt, 0:C]
                    act.wait_ge(s["add"], n + 1)
                    need(act, s["seg"], free)
                    act.activation(m3, got[j][:, t0 * C:(t0 + nt) * C].rearrange("p (t c) -> p t c", c=C),
                                   ACT.Relu).then_inc(s["msg"], 1)

                def square_message(act, q, b, n, sq_free):
                    nt = CHUNKS[q % NC_][1]
                    m3 = msg[b][:].rearrange("p (t c) -> p t c", c=C1)[:, 0:nt, 0:C]
                    act.wait_ge(s["msg"], n + 1)
                    need(act, s["sumsq"], sq_free)
                    act.activation(sq[b][:, 0:nt * C].rearrange("p (t c) -> p t c", c=C), m3,
                                   ACT.Square).then_inc(s["sq"], 1)

                def batch_statistics(v, slab, q, b, n):
                    nt = CHUNKS[q % NC_][1]
                    c = q % NC_
                    v.wait_ge(s["rf"], n + 1)
                    if c == 0:
                        need(v, s["flush"], slab)
                    v.bn_stats(parts[:, c * 6:(c + 1) * 6], feat[b][:, 0:nt * P]).then_inc(s["bn"], 1)
                    if c == NC_ - 1:
                        v.wait_ge(s["bn"], n + 1)
                        need(v, s["keep"], slab)
                        v.nop(nofuse=True)
                        v.bn_aggr(mv1[:], parts[:]).then_inc(s["flush"], 1)
                        v.wait_ge(s["flush"], slab + 1)
                        v.tensor_copy(slab_mv[:, bass.ds(slab * 2, 2)], mv1[:]).then_inc(s["keep"], 1)

                def add_gathered(v, j, q, b, n, inc=True):
                    t0, nt = CHUNKS[q % NC_]
                    v.wait_ge(s["pre"], n + 1)
                    at = got[j][:, t0 * C:(t0 + nt) * C]
                    ins = v.tensor_tensor(at, at, ps["pre"][b][:, 0:nt * C], ALU.add)
                    return ins.then_inc(s["add"], 1) if inc else ins

                def add_squares(v, q, b, n):
                    nt = CHUNKS[q % NC_][1]
                    v.wait_ge(s["sq"], n + 1)
                    need(v, s["sumsq"], n)
                    v.tensor_tensor(sumsq[:, 0:nt * C], sumsq[:, 0:nt * C], sq[b][:, 0:nt * C], ALU.add).then_inc(s["sumsq"], 1)

                def prepare(v):
                    for i in range(2):
                        v.memset(hid[i][64:P, :], 1.0)
                        v.memset(msg[i][:], 1.0)
                    if last:
                        for j in range(U):
                            v.tensor_copy(w_q[j][0:C, :].rearrange("p (k c) -> p k c", c=C),
                                          w_e1[:].unsqueeze(1).to_broadcast([C, NC_, C]))
                    if split_edges:
                        go, done = chain(v, s["wcut"])
                        v.wait_ge(s["wf"], 16)
                        split(go, done, v, w_f[:], [x[:] for x in w_p])
                        go(v.memset(w_hid1[:], 0.0))
                        go(v.memset(sums[C:C1, :], 0.0))
                        v.wait_ge(s["hf"], 16 * len(hid_loads))
                        for x, m, to in ((hid_f[0], pick[0], w_hid0[:]), (hid_f[1], pick[1], w_hid1[0:KE, 0:C])):
                            K = x.shape[0]
                            split(go, done, v, x[:], [h[0:K, :] for h in hid_p])
                            go(v.tensor_scalar(hid_t[0:K, :], hid_p[0][0:K, :], m[:, 0:1], None, ALU.mult))
                            done()
                            go(v.scalar_tensor_tensor(out=hid_t[0:K, :], in0=hid_p[1][0:K, :], scalar=m[:, 1:2],
                                                      in1=hid_t[0:K, :], op0=ALU.mult, op1=ALU.add))
                            done()
                            go(v.scalar_tensor_tensor(out=to, in0=hid_p[2][0:K, :], scalar=m[:, 2:3], in1=hid_t[0:K, :],
                                                      op0=ALU.mult, op1=ALU.add))
                            done()
                        go(v.tensor_copy(w_hid1[:, C:C + R], tail_f[:]))
                        done()
                    v.drain().then_inc(s["init"], 1)

                def sync_windows(sp):
                    def free(sem, k, j, c):
                        if not isinstance(k, int):
                            sp.wait_ge(s[sem], Q * (k - 1) + NC_ * j + c + 1)
                            sp.nop(nofuse=True)

                    def slab_idx(k, j):
                        free("add", k, j, GROUPS[-1][0])
                        load_idx(sp, j, k * U + j)

                    def slab_rows(k, j):
                        free("hid", k, j, NC_ - 1)
                        if stats:
                            free("f", k, j, NC_ - 1)
                        load_rows(sp, j, k * U + j)
                        if last:
                            free("pre", k, j, NC_ - 1)
                            for c in range(NC_):
                                h = sp.value_load(head_i[0:1, bass.ds((k * U + j) * NC_ + c, 1)], min_val=0, max_val=N - R)
                                sp.dma_start(w_q[j][C:C + R, c * C:(c + 1) * C], q_rows[bass.ds(h, R), :]).then_inc(s[f"q{j}"], 16)

                    def body(k):
                        if isinstance(k, int):
                            for j in range(U):
                                slab_idx(k, j)
                        if split_edges:
                            load_piece(sp, k)
                            if isinstance(k, int):
                                sp.wait_ge(s["wout"], 48)
                        for j in range(U):
                            if not isinstance(k, int):
                                slab_idx(k, j)
                            slab_rows(k, j)
                        if split_edges:
                            store_parts(sp, k)
                    repeat(sp, ITERS, body)
                    if split_edges:
                        sp.wait_ge(s["eout"], 48 * ITERS)

                def load_piece(sp, k):
                    if not isinstance(k, int):
                        sp.wait_ge(s["estep"], k)
                        sp.nop(nofuse=True)
                    sp.dma_start(e_f[:].rearrange("p (d i) -> p d i", d=D),
                                 a["ea_nat"][:, :, bass.ds(k * PIECE, PIECE)].rearrange("d p i -> p d i")).then_inc(s["ef"], 16)

                def store_parts(sp, k):
                    sp.wait_ge(s["estep"], k + 1)
                    sp.nop(nofuse=True)
                    for i in range(3):
                        sp.dma_start(ea_parts[i * D:(i + 1) * D, :].rearrange("d (p i) -> p d i", p=P)[:, :, bass.ds(k * PIECE, PIECE)],
                                     e_p[:, i * D * PIECE:(i + 1) * D * PIECE].rearrange("p (d i) -> p d i", d=D)
                                     ).then_inc(s["eout"], 16)

                def split_piece(v, k):
                    v.wait_ge(s["ef"], 16 * (k + 1))
                    need(v, s["eout"], 48 * k)
                    n = D * PIECE
                    for i in range(3):
                        part = e_p[:, i * n:(i + 1) * n]
                        ins = v.tensor_copy(part, e_f[:])
                        ins.then_inc(s["estep"] if i == 2 else s["ecut"], 1)
                        if i < 2:
                            v.wait_ge(s["ecut"], 4 * k + 2 * i + 1)
                            v.tensor_tensor(e_f[:], e_f[:], part, ALU.subtract).then_inc(s["ecut"], 1)
                            v.wait_ge(s["ecut"], 4 * k + 2 * i + 2)

                def gpsimd_windows(gp):
                    def body(k):
                        for j in range(U):
                            for g, (_, end) in enumerate(GROUPS):
                                if not isinstance(k, int):
                                    gp.wait_ge(s["msg"], Q * (k - 1) + NC_ * j + end + 1)
                                if g == 0:
                                    gp.wait_ge(s[f"idx{j}"], 16 * (k + 1))
                                gp.nop(nofuse=True)
                                for t in range(*group_tiles(g)):
                                    gp.indirect_dma_start(got[j][:, t * C:(t + 1) * C], None, table,
                                                          bass.IndirectOffsetOnAxis(idx[j][:, t:t + 1], 0)
                                                          ).then_inc(s[f"got{j}{g}"], 16)
                    repeat(gp, ITERS, body)

                def tensor_windows(pe):
                    def hidden_rows(k, q):
                        j, c, _, _ = chunk(q)
                        if c == 0:
                            pe.wait_ge(s[f"row{j}"], ROWS * (k + 1))
                        hidden(pe, j, q, q % 2, Q * k + q, left(k, q))
                        if stats:
                            if c == 0:
                                pe.wait_ge(s[f"srow{j}"], 48 * (k + 1))
                            features(pe, j, q, q % 2, Q * k + q, left(k, q))

                    def pre(k, q):
                        j, c, t0, nt = chunk(q)
                        pe.wait_ge(s["rhid"], Q * k + q + 1)
                        need(pe, s["add"], left(k, q))
                        if last:
                            pe.wait_ge(s["hot_t"], Q * k + q + 1)
                            if c == 0:
                                pe.wait_ge(s[f"q{j}"], 16 * NC_ * (k + 1))
                        for t in range(nt):
                            mm = pe.matmul(ps["pre"][q % 2][:, t * C:(t + 1) * C], hid[q % 2][0:P if last else C1, t * P:(t + 1) * P],
                                           w_q[j][:, c * C:(c + 1) * C] if last else w_e0[:], start=True, stop=True)
                        mm.then_inc(s["pre"], 1)

                    def segment(k, q):
                        j, c, t0, nt = chunk(q)
                        if c == 0:
                            need(pe, s[f"win{j}"], k)
                        pe.wait_ge(s["msg"], Q * k + q + 1)
                        pe.wait_ge(s["hot"], Q * k + q + 1)
                        for t in range(nt):
                            mm = pe.matmul(ps["win"][j][0:M, 0:W], msg[q % 2][:, t * C1:t * C1 + M],
                                           hot[q % 2][:, t * W:(t + 1) * W],
                                           start=(t0 + t == 0), stop=(t0 + t == T - 1))
                        mm.then_inc(s["seg"], 1)

                    staged(pe, ITERS, Q, [(0, hidden_rows), (1, pre), (2, segment)])

                def scalar_windows(act):
                    plan = [(0, lambda k, q: relu_hidden(act, q, q % 2, Q * k + q, left(k, q)))]
                    if stats:
                        plan += [(0, lambda k, q: relu_features(act, q, q % 2, Q * k + q, left(k, q)))]
                    plan += [(1, lambda k, q: relu_message(act, chunk(q)[0], q, q % 2, Q * k + q, left(k, q)))]
                    if last:
                        plan += [(1, lambda k, q: square_message(act, q, q % 2, Q * k + q, left(k, q)))]
                    staged(act, ITERS, Q, plan)

                def vector_windows(v):
                    def near_rows(k, q):
                        nt = chunk(q)[3]
                        v.wait_ge(s["hid"], Q * k + q + 1)
                        need(v, s["pre"], left(k, q))
                        v.tensor_scalar(hid[q % 2][C:C + R, 0:nt * P], ps["hid"][q % 2][C:C + R, 0:nt * P],
                                        0.0, None, ALU.is_equal).then_inc(s["hot_t"], 1)

                    def add_window(k, q):
                        j, c, _, _ = chunk(q)
                        if c < NC_ - 1:
                            return
                        b = v.value_load(base_i[0:1, bass.ds(k * U + j, 1)], min_val=0, max_val=N - W)
                        v.wait_ge(s["seg"], Q * k + q + 1)
                        need(v, s[f"win{1 - j}"], k + j)
                        at = sums[0:M, bass.ds(b, W)]
                        v.tensor_tensor(at, at, ps["win"][j][0:M, 0:W], ALU.add).then_inc(s[f"win{j}"], 1)

                    def one_hot(k, q):
                        j, _, t0, nt = chunk(q)
                        need(v, s["seg"], left(k, q))
                        v.tensor_tensor(hot[q % 2][:, 0:nt * W].rearrange("p (t w) -> p t w", w=W),
                                        node_row[:, 0:W].unsqueeze(1).to_broadcast([P, nt, W]),
                                        rel[:, bass.ds((k * U + j) * T + t0, nt)].unsqueeze(2).to_broadcast([P, nt, W]),
                                        ALU.is_equal).then_inc(s["hot"], 1)

                    def add_rows(k, q):
                        j, c, _, _ = chunk(q)
                        for g, (start, _) in enumerate(GROUPS):
                            if c == start:
                                t0, t1 = group_tiles(g)
                                v.wait_ge(s[f"got{j}{g}"], 16 * (t1 - t0) * (k + 1))
                        add_gathered(v, j, q, q % 2, Q * k + q)

                    plan = [(0, near_rows)] if last else []
                    plan += [(3, add_window), (0, one_hot)]
                    if stats:
                        plan += [(0, lambda k, q: batch_statistics(v, k * U + chunk(q)[0], q, q % 2, Q * k + q))]
                    plan += [(1, add_rows)]
                    if last:
                        plan += [(2, lambda k, q: add_squares(v, q, q % 2, Q * k + q))]
                    staged(v, ITERS, Q, plan, ahead=(lambda k: split_piece(v, k)) if split_edges else None)

                NW = TILES

                def sync_general(sp):
                    if split_edges:
                        sp.wait_ge(s["wout"], 48)

                        def piece(k):
                            load_piece(sp, k)
                            store_parts(sp, k)
                        repeat(sp, ITERS, piece)
                        sp.wait_ge(s["eout"], 48 * ITERS)

                    def body(k):
                        if not isinstance(k, int):
                            sp.wait_ge(s["slab"], k)
                            sp.nop(nofuse=True)
                        load_idx(sp, 0, k)
                        load_rows(sp, 0, k)
                    repeat(sp, S, body)

                def gpsimd_general(gp):
                    def body(k):
                        need(gp, s["slab"], k)
                        if last:
                            gp.wait_ge(s["qidx"], k + 1)
                        gp.wait_ge(s["idx0"], 16 * (k + 1))
                        gp.nop(nofuse=True)
                        for t in range(T):
                            gp.indirect_dma_start(got[0][:, t * C:(t + 1) * C], None, table,
                                                  bass.IndirectOffsetOnAxis(idx[0][:, t:t + 1], 0)).then_inc(s["got00"], 16)
                            if last:
                                gp.indirect_dma_start(got[1][:, t * C:(t + 1) * C], None, q_rows,
                                                      bass.IndirectOffsetOnAxis(q_idx[:, t:t + 1], 0)).then_inc(s["got10"], 16)
                    repeat(gp, S, body)

                def tensor_general(pe):
                    def body(k):
                        pe.wait_ge(s["row0"], ROWS * (k + 1))
                        if stats:
                            pe.wait_ge(s["srow0"], 48 * (k + 1))
                        for c, (t0, nt) in enumerate(CHUNKS):
                            n = k * NC_ + c
                            hidden(pe, 0, c, 0, n, n)
                            if stats:
                                features(pe, 0, c, 0, n, n)
                            pe.wait_ge(s["rhid"], n + 1)
                            need(pe, s["add"], n)
                            for t in range(nt):
                                mm = pe.matmul(ps["pre"][0][:, t * C:(t + 1) * C], hid[0][0:C if last else C1, t * P:(t + 1) * P],
                                               (w_e1 if last else w_e0)[:], start=True, stop=True)
                            mm.then_inc(s["pre"], 1)
                            pe.wait_ge(s["msg"], n + 1)
                            pe.nop(nofuse=True)
                            with pe.Fori(0, NW) as w:
                                pe.wait_ge(s["hot"], n * NW + w + 1)
                                for t in range(nt):
                                    mm = pe.matmul(ps["win"][0][0:M, 0:P], msg[0][:, t * C1:t * C1 + M],
                                                   hot[0][:, t * P:(t + 1) * P], start=(t == 0), stop=(t == nt - 1))
                                mm.then_inc(s["win1"], 1)
                            pe.drain().then_inc(s["seg"], 1)
                    repeat(pe, S, body)

                def scalar_general(act):
                    def body(k):
                        for c in range(NC_):
                            n = k * NC_ + c
                            relu_hidden(act, c, 0, n, n)
                            if stats:
                                relu_features(act, c, 0, n, n)
                            relu_message(act, 0, c, 0, n, n)
                            if last:
                                square_message(act, c, 0, n, n)
                    repeat(act, S, body)

                def vector_general(v):
                    if split_edges:
                        repeat(v, ITERS, lambda k: split_piece(v, k))

                    def body(k):
                        need(v, s["slab"], k)
                        v.tensor_scalar(dst[:], rel[:, bass.ds(k * T, T)], base_all[:, bass.ds(k, 1)], None,
                                        ALU.add).then_inc(s["dst"], 1)
                        v.wait_ge(s["dst"], k + 1)
                        if last:
                            v.tensor_scalar(q_idx[:], dst[:], 0.0, None, ALU.max).then_inc(s["qidx"], 1)
                        for c, (t0, nt) in enumerate(CHUNKS):
                            n = k * NC_ + c
                            if last:
                                v.wait_ge(s["hid"], n + 1)
                                v.sem_inc(s["hot_t"], 1)
                            if stats:
                                batch_statistics(v, k, c, 0, n)
                            if c == 0:
                                v.wait_ge(s["got00"], 16 * T * (k + 1))
                            if last:
                                if c == 0:
                                    v.wait_ge(s["got10"], 16 * T * (k + 1))
                                at = got[0][:, t0 * C:(t0 + nt) * C]
                                v.tensor_tensor(at, at, got[1][:, t0 * C:(t0 + nt) * C], ALU.add).then_inc(s["qadd"], 1)
                                v.wait_ge(s["qadd"], n + 1)
                            add_gathered(v, 0, c, 0, n)
                            with v.Fori(0, NW) as w:
                                v.tensor_scalar(off[:, 0:nt], dst[:, t0:t0 + nt], first[:, bass.ds(w, 1)], None,
                                                ALU.subtract).then_inc(s["off"], 1)
                                v.wait_ge(s["off"], n * NW + w + 1)
                                v.tensor_tensor(hot[0][:, 0:nt * P].rearrange("p (t w) -> p t w", w=P),
                                                node_row[:].unsqueeze(1).to_broadcast([P, nt, P]),
                                                off[:, 0:nt].unsqueeze(2).to_broadcast([P, nt, P]),
                                                ALU.is_equal).then_inc(s["hot"], 1)
                                v.wait_ge(s["win1"], n * NW + w + 1)
                                at = sums[0:M, bass.ds(w * P, P)]
                                v.tensor_tensor(at, at, ps["win"][0][0:M, 0:P], ALU.add).then_inc(s["win0"], 1)
                                v.wait_ge(s["win0"], n * NW + w + 1)
                            if last:
                                add_squares(v, c, 0, n)
                        v.drain().then_inc(s["slab"], 1)
                    repeat(v, S, body)

                def both(eng, windows, general):
                    flag = eng.value_load(fits[:], min_val=0, max_val=1)
                    with eng.If(flag == 1):
                        windows(eng)
                    with eng.Else():
                        general(eng)

                @block.sync
                def _(sp):
                    if split_edges:
                        sp.dma_start(w_f[:], a["w_nat"].rearrange("o p i -> (o p) i")).then_inc(s["wf"], 16)
                        for to, src in hid_loads:
                            sp.dma_start(to[:], src).then_inc(s["hf"], 16)
                    both(sp, sync_windows, sync_general)

                @block.gpsimd
                def _(gp):
                    both(gp, gpsimd_windows, gpsimd_general)

                @block.tensor
                def _(pe):
                    pe.wait_ge(s["init"], 1)
                    both(pe, tensor_windows, tensor_general)

                @block.scalar
                def _(act):
                    if split_edges:
                        act.wait_ge(s["wcut"], 5)
                        for i in range(3):
                            act.dma_start(w_parts[i:i + 1, :].rearrange("o (p i) -> (o p) i", p=P), w_p[i][:]).then_inc(s["wout"], 16)
                    act.wait_ge(s["init"], 1)
                    both(act, scalar_windows, scalar_general)

                @block.vector
                def _(v):
                    prepare(v)
                    both(v, vector_windows, vector_general)

        def node_mlp(l, y=None, mv=None):
            with ExitStack() as st:
                z = [sb(f"n{l}_z{i}", [C1, STEP], F32, st) for i in range(2)]
                ps = pools(st, a=2, b=2, c=2)
                s = Sems(st, f"mlp{l}")
                if l == 0:
                    cols = [sb(f"n0_cols{i}", [C, STEP], F32, st) for i in range(2)]
                    rows_out = [sb(f"n0_rows{i}", [P, NODE_TILES * C], F32, st) for i in range(2)]
                else:
                    parts = sb("n1_parts", [P, UN * NODE_TILES * 6], F32, st)
                    some = sb("n1_some", [P, UN * NODE_TILES * 2], F32, st)
                block = st.enter_context(nc.Block())

                def at_step(k, q):
                    return bass.ds((k * UN + q) * STEP, STEP)

                @block.tensor
                def _(pe):
                    def first_layer(k, q):
                        need(pe, s["z"], UN * k + q - 1)
                        pe.matmul(ps["a"][q % 2][0:C, 0:STEP], w_conv[l][0][0:C, :], sums[0:C, at_step(k, q)],
                                  start=True, stop=True).then_inc(s["a"], 1)

                    def second_cols(k, q):
                        pe.wait_ge(s["z"], UN * k + q + 1)
                        need(pe, s["col"], UN * k + q - 1)
                        pe.matmul(ps["c"][q % 2][0:C, 0:STEP], w_conv[l][1][0:C, :], z[q % 2][0:C, :],
                                  start=True, stop=True).then_inc(s["c"], 1)

                    def turn(k, q):
                        pe.wait_ge(s["col"], UN * k + q + 1)
                        need(pe, s["row"], UN * k + q - 1)
                        for t in range(NODE_TILES):
                            mm = pe.transpose(ps["b"][q % 2][:, t * C:(t + 1) * C], cols[q % 2][:, t * P:(t + 1) * P],
                                              ident[0:C, 0:C])
                        mm.then_inc(s["b"], 1)

                    def second_rows(k, q):
                        pe.wait_ge(s["z"], UN * k + q + 1)
                        need(pe, s["row"], UN * k + q - 1)
                        for t in range(NODE_TILES):
                            mm = pe.matmul(ps["b"][q % 2][:, t * C:(t + 1) * C], z[q % 2][:, t * P:(t + 1) * P],
                                           w_conv[l][1][:], start=True, stop=True)
                        mm.then_inc(s["b"], 1)

                    pe.wait_ge(s["init"], 1)
                    staged(pe, STEPS // UN, UN,
                           [(0, first_layer)] + ([(1, second_cols), (2, turn)] if l == 0 else [(1, second_rows)]))

                @block.scalar
                def _(act):
                    def relu_first(k, q):
                        act.wait_ge(s["a"], UN * k + q + 1)
                        need(act, s["c"] if l == 0 else s["b"], UN * k + q - 1)
                        act.activation(z[q % 2][0:C, :], ps["a"][q % 2][0:C, 0:STEP], ACT.Relu,
                                       bias=b_conv[l][0][:]).then_inc(s["z"], 1)

                    def relu_second(k, q):
                        act.wait_ge(s["c"], UN * k + q + 1)
                        need(act, s["b"], UN * k + q - 1)
                        need(act, s["sum"], UN * k + q - 1)
                        act.activation(cols[q % 2][:], ps["c"][q % 2][0:C, 0:STEP], ACT.Relu,
                                       bias=b_conv[l][1][:]).then_inc(s["col"], 1)

                    staged(act, STEPS // UN, UN, [(0, relu_first)] + ([(1, relu_second)] if l == 0 else []))

                @block.vector
                def _(v):
                    def rows_of(k, q):
                        v.wait_ge(s["b"], UN * k + q + 1)
                        need(v, s[f"out{q % 2}"], (UN // 2 * k + q // 2) * 16)
                        v.tensor_copy(rows_out[q % 2][:], ps["b"][q % 2][:, 0:NODE_TILES * C]).then_inc(s["row"], 1)

                    def add_residual(k, q):
                        v.wait_ge(s["b"], UN * k + q + 1)
                        at = y[:, bass.ds((k * UN + q) * NODE_TILES * C, NODE_TILES * C)]
                        v.scalar_tensor_tensor(out=at, in0=ps["b"][q % 2][:, 0:NODE_TILES * C], scalar=0.0, in1=at,
                                               op0=ALU.max, op1=ALU.add).then_inc(s["row"], 1)
                        if q == UN - 1:
                            moments(v, s["row"], UN * (k + 1), s["st"], k, y, parts, some, mv)

                    for i in range(2):
                        v.memset(z[i][C:C1, :], 1.0)
                    v.drain().then_inc(s["init"], 1)
                    if l == 1:
                        v.wait_ge(s["x"], 16)
                    staged(v, STEPS // UN, UN, [(0, rows_of if l == 0 else add_residual)])

                if l == 0:
                    @block.gpsimd
                    def _(gp):
                        def keep(k, q):
                            gp.wait_ge(s["col"], UN * k + q + 1)
                            gp.tensor_copy(sums[0:C, at_step(k, q)], cols[q % 2][:]).then_inc(s["sum"], 1)
                        staged(gp, STEPS // UN, UN, [(0, keep)])
                        gp.wait_ge(s["sum"], STEPS)

                    @block.sync
                    def _(sp):
                        def store(k, q):
                            sp.wait_ge(s["row"], UN * k + q + 1)
                            sp.nop(nofuse=True)
                            sp.dma_start(h1_rows[at_step(k, q), :].rearrange("(t p) c -> p t c", p=P),
                                         rows_out[q % 2][:].rearrange("p (t c) -> p t c", c=C)).then_inc(s[f"out{q % 2}"], 16)
                        staged(sp, STEPS // UN, UN, [(0, store)])
                        for i in range(2):
                            sp.wait_ge(s[f"out{i}"], 16 * (STEPS // 2))
                else:
                    @block.sync
                    def _(sp):
                        sp.dma_start(y[:], a["x_tiles"]).then_inc(s["x"], 16)
                        sp.wait_ge(s["x"], 16)

        def moments(v, ready, count, sem, k, y, parts, some, mv):
            n = UN * NODE_TILES
            v.wait_ge(ready, count)
            need(v, sem, (2 * n + 1) * k)
            for t in range(n):
                v.bn_stats(parts[:, t * 6:(t + 1) * 6], y[:, bass.ds((k * n + t) * C, C)]).then_inc(sem, 1)
            v.wait_ge(sem, (2 * n + 1) * k + n)
            v.nop(nofuse=True)
            for t in range(n):
                v.bn_aggr(some[:, 2 * t:2 * t + 2], parts[:, t * 6:(t + 1) * 6]).then_inc(sem, 1)
            v.wait_ge(sem, (2 * n + 1) * k + 2 * n)
            v.tensor_copy(mv[:, bass.ds(k * n * 2, n * 2)], some[:]).then_inc(sem, 1)

        def root(act, sem, mv, rstd):
            act.activation(rstd[:], mv[:].rearrange("p (t m) -> p m t", m=2)[:, 1, :], ACT.Sqrt, bias=eps[:]).then_inc(sem, 1)

        def scales(v, go, done, sem, mv, rstd, shift):
            v.wait_ge(sem, 1)
            go(v.reciprocal(rstd[:], rstd[:]))
            done()
            go(v.scalar_tensor_tensor(out=shift[:], in0=mv[:].rearrange("p (t m) -> p m t", m=2)[:, 0, :], scalar=-1.0,
                                      in1=rstd[:], op0=ALU.mult, op1=ALU.mult))
            done()

        def fold(v, go, done, sqrt_in, sqrt_out, mean, ex2, gb):
            go(v.tensor_tensor(tmp[0:C, 2:3], mean, mean, ALU.mult))
            done()
            go(v.tensor_tensor(tmp[0:C, 3:4], ex2, tmp[0:C, 2:3], ALU.subtract))
            done()
            v.drain().then_inc(sqrt_in, 1)
            v.wait_ge(sqrt_out, 1)
            go(v.reciprocal(tmp[0:C, 6:7], tmp[0:C, 3:4]))
            done()
            go(v.tensor_tensor(tmp[0:C, 4:5], tmp[0:C, 6:7], gb[:, 0:1], ALU.mult))
            done()
            go(v.tensor_tensor(tmp[0:C, 5:6], mean, tmp[0:C, 4:5], ALU.mult))
            done()
            go(v.tensor_tensor(lift[:, C:C1], gb[:, 1:2], tmp[0:C, 5:6], ALU.subtract))
            done()

        def message_inputs(y, mv, nf):
            with ExitStack() as st:
                rstd = sb("m_rstd", [P, TILES], F32, st)
                shift = sb("m_shift", [P, TILES], F32, st)
                xs = [sb(f"m_xs{i}", [P, NODE_TILES * C], F32, st) for i in range(2)]
                xt = [sb(f"m_xt{i}", [C1, STEP], F32, st) for i in range(2)]
                nf_sq = [sb(f"m_nf_sq{i}", [P, NODE_TILES * C], F32, st) for i in range(2)]
                acc = [sb(f"m_acc{i}", [P, NODE_TILES * C], F32, st) for i in range(2)]
                tot = sb("m_tot", [P, 2 * C], F32, st)
                mom = sb("m_mom", [P, 2 * C], F32, st)
                var = sb("m_var", [P, C], F32, st)
                slab_sq = sb("m_slab_sq", [C, S], F32, st)
                none = sb("m_none", [1, C], F32, st)
                rows_out = [sb(f"m_rows{i}", [P, 2, NODE_TILES * C], F32, st) for i in range(2)]
                ps = pools(st, xt=2, pq=2, nf=2, f=1, tot=1)
                s = Sems(st, "inputs")
                block = st.enter_context(nc.Block())

                def nodes(k, q):
                    return bass.ds((k * UN + q) * NODE_TILES * C, NODE_TILES * C)

                @block.gpsimd
                def _(gp):
                    def keep(k, q):
                        gp.wait_ge(s["x"], NODE_TILES * (UN * k + q + 1))
                        gp.tensor_copy(y[:, nodes(k, q)], xs[q % 2][:]).then_inc(s["y"], 1)
                    gp.memset(sums[:], 0.0).then_inc(s["clear"], 1)
                    staged(gp, STEPS // UN, UN, [(0, keep)])
                    gp.wait_ge(s["clear"], 1)
                    gp.wait_ge(s["y"], STEPS)

                @block.tensor
                def _(pe):
                    def turn(k, q):
                        pe.wait_ge(s["x"], NODE_TILES * (UN * k + q + 1))
                        need(pe, s["xt"], UN * k + q - 1)
                        for t in range(NODE_TILES):
                            mm = pe.transpose(ps["xt"][q % 2][0:C, t * P:(t + 1) * P], xs[q % 2][:, t * C:(t + 1) * C], ident[:])
                        mm.then_inc(s["xp"], 1)

                    def products(k, q):
                        pe.wait_ge(s["xt"], UN * k + q + 1)
                        need(pe, s["nf"], (UN * k + q - 1) * NODE_TILES)
                        need(pe, s["pq"], UN * k + q - 1)
                        for t in range(NODE_TILES):
                            x_t = xt[q % 2][:, t * P:(t + 1) * P]
                            pe.matmul(ps["pq"][q % 2][:, t * 2 * C:(t + 1) * 2 * C], x_t, w_wide[:, 0:2 * C],
                                      start=True, stop=True)
                            mm = pe.matmul(ps["nf"][q % 2][:, t * C:(t + 1) * C], x_t, w_wide[:, 2 * C:3 * C],
                                           start=True, stop=True)
                        mm.then_inc(s["wide"], 1)

                    pe.wait_ge(s["f_in"], 2)
                    pe.matmul(ps["f"][0][0:C1, 0:C], lift[:, 0:C1], w_msg_e[:], start=True, stop=True).then_inc(s["f_pe"], 1)
                    pe.wait_ge(s["init"], 1)
                    staged(pe, STEPS // UN, UN, [(0, turn), (1, products)])
                    pe.wait_ge(s["t_in"], 1)
                    pe.matmul(ps["tot"][0][:, 0:2 * C], ones[:], tot[:], start=True, stop=True).then_inc(s["t_pe"], 1)

                @block.scalar
                def _(act):
                    def copy_turned(k, q):
                        act.wait_ge(s["xp"], UN * k + q + 1)
                        need(act, s["wide"], UN * k + q - 1)
                        act.copy(xt[q % 2][0:C, :], ps["xt"][q % 2][0:C, 0:STEP]).then_inc(s["xt"], 1)

                    def copy_products(k, q):
                        act.wait_ge(s["wide"], UN * k + q + 1)
                        need(act, s[f"out{q % 2}"], (UN // 2 * k + q // 2) * 32)
                        act.copy(rows_out[q % 2][:].rearrange("p h (t c) -> p t h c", c=C),
                                 ps["pq"][q % 2][:, 0:NODE_TILES * 2 * C].rearrange("p (t h c) -> p t h c", h=2, c=C)
                                 ).then_inc(s["pq"], 1)

                    def square(k, q):
                        act.wait_ge(s["nf"], NODE_TILES * (UN * k + q + 1))
                        need(act, s["acc1"], UN * k + q - 1)
                        act.activation(nf_sq[q % 2][:], nf[:, nodes(k, q)], ACT.Square).then_inc(s["nsq"], 1)

                    root(act, s["sqrt"], mv, rstd)
                    act.wait_ge(s["f_in"], 1)
                    act.activation(tmp[0:C, 3:4], tmp[0:C, 3:4], ACT.Sqrt, bias=eps[0:C, :]).then_inc(s["f_out"], 1)
                    staged(act, STEPS // UN, UN, [(0, copy_turned), (1, copy_products), (2, square)])
                    act.wait_ge(s["t_in"], 2)
                    act.activation(var[:], var[:], ACT.Sqrt, bias=eps[:]).then_inc(s["root"], 1)

                @block.vector
                def _(v):
                    def normalize(k, q):
                        need(v, s["xp"], UN * k + q - 1)
                        need(v, s["y"], UN * k + q - 1)
                        for t in range(NODE_TILES):
                            tile = (k * UN + q) * NODE_TILES + t
                            v.tensor_scalar(xs[q % 2][:, t * C:(t + 1) * C], y[:, bass.ds(tile * C, C)],
                                            rstd[:, bass.ds(tile, 1)], shift[:, bass.ds(tile, 1)],
                                            ALU.mult, ALU.add).then_inc(s["x"], 1)

                    def features(k, q):
                        v.wait_ge(s["wide"], UN * k + q + 1)
                        for t in range(NODE_TILES):
                            tile = (k * UN + q) * NODE_TILES + t
                            v.tensor_scalar(nf[:, bass.ds(tile * C, C)], ps["nf"][q % 2][:, t * C:(t + 1) * C],
                                            0.0, is_node[:, bass.ds(tile, 1)], ALU.max, ALU.mult).then_inc(s["nf"], 1)

                    def gather_moments(k, q):
                        n = UN * k + q
                        v.wait_ge(s["nf"], NODE_TILES * (n + 1))
                        need(v, s["acc0"], n)
                        v.tensor_tensor(acc[0][:], acc[0][:], nf[:, nodes(k, q)], ALU.add).then_inc(s["acc0"], 1)
                        v.wait_ge(s["nsq"], n + 1)
                        need(v, s["acc1"], n)
                        v.tensor_tensor(acc[1][:], acc[1][:], nf_sq[q % 2][:], ALU.add).then_inc(s["acc1"], 1)

                    go, done = chain(v, s["dve"])
                    for i in range(2):
                        go(v.memset(xt[i][C:C1, :], 1.0))
                        go(v.memset(acc[i][:], 0.0))
                    go(v.memset(none[:], -3e38))
                    mv3 = slab_mv[:].rearrange("p (s m) -> p m s", m=2)
                    go(v.tensor_tensor(slab_sq[:], mv3[:, 0, :], mv3[:, 0, :], ALU.mult))
                    done()
                    go(v.tensor_tensor(slab_sq[:], slab_sq[:], mv3[:, 1, :], ALU.add))
                    done()
                    go(v.tensor_reduce(tmp[0:C, 8:9], mv3[:, 0, :], AX_X, ALU.add))
                    go(v.tensor_reduce(tmp[0:C, 9:10], slab_sq[:], AX_X, ALU.add))
                    done()
                    go(v.tensor_scalar(tmp[0:C, 8:10], tmp[0:C, 8:10], float(T * P) / E, None, ALU.mult))
                    done()
                    fold(v, go, done, s["f_in"], s["f_out"], tmp[0:C, 8:9], tmp[0:C, 9:10], gb_edge)
                    v.drain().then_inc(s["f_in"], 1)
                    go(v.tensor_scalar(w_e1[:], w_msg_e[:], tmp[0:C, 4:5], None, ALU.mult))
                    v.wait_ge(s["f_pe"], 1)
                    go(v.tensor_tensor(w_wide[C:C1, C:2 * C], ps["f"][0][C:C1, 0:C], b_msg[C:C1, :], ALU.add))
                    done()
                    v.drain().then_inc(s["init"], 1)
                    scales(v, go, done, s["sqrt"], mv, rstd, shift)
                    staged(v, STEPS // UN, UN, [(0, normalize), (2, features), (3, gather_moments)])
                    v.wait_ge(s["acc0"], STEPS)
                    v.wait_ge(s["acc1"], STEPS)
                    for i in range(2):
                        go(v.tensor_tensor(tot[:, i * C:(i + 1) * C], acc[i][:, 0:C], acc[i][:, C:2 * C], ALU.add))
                    done()
                    v.drain().then_inc(s["t_in"], 1)
                    v.wait_ge(s["t_pe"], 1)
                    go(v.tensor_scalar(mom[:], ps["tot"][0][:, 0:2 * C], 1.0 / N, None, ALU.mult))
                    done()
                    go(v.tensor_tensor(var[:], mom[:, 0:C], mom[:, 0:C], ALU.mult))
                    done()
                    go(v.tensor_tensor(var[:], mom[:, C:2 * C], var[:], ALU.subtract))
                    done()
                    v.drain().then_inc(s["t_in"], 1)
                    v.wait_ge(s["root"], 1)
                    go(v.reciprocal(var[:], var[:]))
                    done()
                    go(v.tensor_tensor(node_g[:], var[:], gb_node[:, 0:C], ALU.mult))
                    done()
                    go(v.tensor_tensor(var[:], mom[:, 0:C], node_g[:], ALU.mult))
                    done()
                    go(v.tensor_tensor(node_b[:], gb_node[:, C:2 * C], var[:], ALU.subtract))
                    done()

                @block.sync
                def _(sp):
                    def store(k, q):
                        sp.wait_ge(s["pq"], UN * k + q + 1)
                        sp.nop(nofuse=True)
                        for h, table in enumerate((p_rows, q_rows)):
                            sp.dma_start(table[bass.ds((k * UN + q) * STEP, STEP), :].rearrange("(t p) c -> p t c", p=P),
                                         rows_out[q % 2][:, h, :].rearrange("p (t c) -> p t c", c=C)
                                         ).then_inc(s[f"out{q % 2}"], 16)
                    staged(sp, STEPS // UN, UN, [(0, store)])
                    for i in range(2):
                        sp.wait_ge(s[f"out{i}"], 32 * (STEPS // 2))
                    sp.dma_start(p_rows[NPAD - 1:NPAD, :], none[:]).then_inc(s["out0"], 16)
                    sp.wait_ge(s["out0"], 32 * (STEPS // 2) + 16)

        def finish(y, nf, mv):
            with ExitStack() as st:
                rstd = sb("o_rstd", [P, TILES], F32, st)
                shift = sb("o_shift", [P, TILES], F32, st)
                part = [sb(f"o_sum{i}", [C + 2, STEP], F32, st) for i in range(2)]
                one_b = sb("o_one_b", [1, C + 2], F32, st)
                parts = sb("o_parts", [P, UN * NODE_TILES * 6], F32, st)
                some = sb("o_some", [P, UN * NODE_TILES * 2], F32, st)
                ps = pools(st, f=1, sq=1, y=2)
                s = Sems(st, "finish")
                block = st.enter_context(nc.Block())
                n = UN * NODE_TILES
                iters = STEPS // UN

                @block.gpsimd
                def _(gp):
                    def scale(k):
                        at = nf[:, bass.ds(k * n * C, n * C)]
                        at3 = at.rearrange("p (t c) -> p t c", c=C)
                        gp.tensor_tensor(at3, at3, node_g[:].unsqueeze(1).to_broadcast([P, n, C]), ALU.mult).then_inc(s["nf"], 1)
                        gp.wait_ge(s["nf"], k + 1)
                        y_at = y[:, bass.ds(k * n * C, n * C)]
                        gp.tensor_tensor(y_at, y_at, at, ALU.add).then_inc(s["y2"], 1)
                    repeat(gp, iters, scale)

                @block.tensor
                def _(pe):
                    def add_up(k, q):
                        pe.wait_ge(s["sum"], UN * k + q + 1)
                        need(pe, s["y"], UN * k + q - 1)
                        for t in range(NODE_TILES):
                            mm = pe.matmul(ps["y"][q % 2][:, t * C:(t + 1) * C], part[q % 2][:, t * P:(t + 1) * P], w_fin[:],
                                           start=True, stop=True)
                        mm.then_inc(s["pe"], 1)

                    for i in range(CH):
                        mm = pe.matmul(ps["sq"][0][0:C, 0:1], sumsq[:, i * C:(i + 1) * C], ones[:, 0:1],
                                       start=(i == 0), stop=(i == CH - 1))
                    mm.then_inc(s["sq"], 1)
                    pe.wait_ge(s["f_in"], 2)
                    pe.matmul(ps["f"][0][0:C + 2, 0:C], lift[:], ident[0:C, 0:C], start=True, stop=False)
                    pe.matmul(ps["f"][0][0:C + 2, 0:C], one_b[:], node_b[0:1, :], start=False, stop=True).then_inc(s["f_pe"], 1)
                    pe.wait_ge(s["w"], 1)
                    staged(pe, iters, UN, [(0, add_up)])

                @block.scalar
                def _(act):
                    def copy_sums(k, q):
                        need(act, s["pe"], UN * k + q - 1)
                        act.copy(part[q % 2][0:C1, :], sums[:, bass.ds((k * UN + q) * STEP, STEP)]).then_inc(s["sum"], 1)

                    def normalize(k):
                        for t in range(1, n, 2):
                            tile = k * n + t
                            at = y[:, bass.ds(tile * C, C)]
                            act.activation(at, at, ACT.Identity, scale=rstd[:, bass.ds(tile, 1)],
                                           bias=shift[:, bass.ds(tile, 1)]).then_inc(s["n1"], 1)

                    act.wait_ge(s["f_in"], 1)
                    act.activation(tmp[0:C, 3:4], tmp[0:C, 3:4], ACT.Sqrt, bias=eps[0:C, :]).then_inc(s["f_out"], 1)
                    act.wait_ge(s["init"], 1)
                    staged(act, iters, UN, [(0, copy_sums)])
                    act.wait_ge(s["st"], (2 * n + 1) * iters)
                    root(act, s["sqrt"], mv, rstd)
                    act.wait_ge(s["go"], 1)
                    repeat(act, iters, normalize)

                @block.vector
                def _(v):
                    def add_products(k, q):
                        if q == 0:
                            v.wait_ge(s["y2"], k + 1)
                        v.wait_ge(s["pe"], UN * k + q + 1)
                        at = y[:, bass.ds((k * UN + q) * NODE_TILES * C, NODE_TILES * C)]
                        v.tensor_tensor(at, at, ps["y"][q % 2][:, 0:NODE_TILES * C], ALU.add).then_inc(s["y"], 1)
                        if q == UN - 1:
                            moments(v, s["y"], UN * (k + 1), s["st"], k, y, parts, some, mv)

                    def normalize(k):
                        for t in range(0, n, 2):
                            tile = k * n + t
                            at = y[:, bass.ds(tile * C, C)]
                            v.tensor_scalar(at, at, rstd[:, bass.ds(tile, 1)], shift[:, bass.ds(tile, 1)],
                                            ALU.mult, ALU.add).then_inc(s["n0"], 1)

                    go, done = chain(v, s["dve"])
                    go(v.tensor_reduce(tmp[0:C, 8:9], sums[0:C, :], AX_X, ALU.add))
                    for i in range(2):
                        go(v.memset(part[i][C:C + 2, :], 1.0))
                    go(v.memset(one_b[:], 0.0))
                    done()
                    v.drain().then_inc(s["init"], 1)
                    go(v.memset(one_b[:, C1:C + 2], 1.0))
                    go(v.tensor_scalar(tmp[0:C, 9:10], tmp[0:C, 8:9], 1.0 / E, None, ALU.mult))
                    v.wait_ge(s["sq"], 1)
                    go(v.tensor_scalar(tmp[0:C, 10:11], ps["sq"][0][0:C, 0:1], 1.0 / E, None, ALU.mult))
                    done()
                    fold(v, go, done, s["f_in"], s["f_out"], tmp[0:C, 9:10], tmp[0:C, 10:11], gb_msg)
                    v.drain().then_inc(s["f_in"], 1)
                    go(v.tensor_scalar(w_fin[0:C, :], ident[0:C, 0:C], tmp[0:C, 4:5], None, ALU.mult))
                    v.wait_ge(s["f_pe"], 1)
                    go(v.tensor_copy(w_fin[C:C + 2, :], ps["f"][0][C:C + 2, 0:C]))
                    done()
                    v.drain().then_inc(s["w"], 1)
                    staged(v, iters, UN, [(0, add_products)])
                    scales(v, go, done, s["sqrt"], mv, rstd, shift)
                    v.drain().then_inc(s["go"], 1)
                    repeat(v, iters, normalize)

                @block.sync
                def _(sp):
                    def store(k):
                        sp.wait_ge(s["n0"], n // 2 * (k + 1))
                        sp.wait_ge(s["n1"], n // 2 * (k + 1))
                        sp.nop(nofuse=True)
                        sp.dma_start(out[bass.ds(k * n * P, n * P), :].rearrange("(t p) c -> p t c", p=P),
                                     y[:, bass.ds(k * n * C, n * C)].rearrange("p (t c) -> p t c", c=C)).then_inc(s["out"], 16)
                    repeat(sp, iters, store)
                    sp.wait_ge(s["out"], 16 * iters)

        mv_x = sb("mv_x", [P, TILES * 2])
        edge_pass("conv0", a["x_rows"], split_edges=True)
        node_mlp(0)
        edge_pass("conv1", h1_rows, stats=True)
        y = sb("y", [P, TILES * C])
        node_mlp(1, y, mv_x)
        nf = sb("nf", [P, TILES * C])
        message_inputs(y, mv_x, nf)
        edge_pass("last", p_rows, last=True)
        finish(y, nf, mv_x)


def kernel(x, src, dst, edge_attr_4, edge_weight1, **w):
    import numpy as np
    import concourse.bacc as bacc
    from concourse.bass_utils import run_bass_kernel_spmd

    N, C = x.shape
    E = src.shape[0]
    S = slabs_of(E)
    EPAD = S * T * P
    NPAD = -(-N // (UN * NODE_TILES * P)) * UN * NODE_TILES * P
    f32 = np.float32

    def padded(v, n, fill):
        v = np.asarray(v)
        return np.concatenate([v, np.full((n - v.shape[0],) + v.shape[1:], fill, v.dtype)])

    def row(v):
        return np.asarray(v).reshape(1, -1)

    def col(v):
        return np.asarray(v).reshape(-1, 1)

    def parts_of(W, b):
        return np.tile(np.concatenate([W, W, W, b]), (3, 1))

    D = edge_attr_4.shape[1]
    rows = padded(x, NPAD, 0)
    src_p = padded(src, EPAD, NPAD - 1).reshape(S, T, P)
    dst_p = padded(dst, EPAD, -1).reshape(S, T, P)
    heads = dst_p[:, ::CH, 0]
    tail = np.zeros((3 * (3 * D + 1) + 1, R), f32)
    tail[3 * D] = -np.arange(R)
    tail[-1] = 1
    W_msg = np.asarray(w["L1_gnn_W_msg"])
    zero = np.zeros((1, C), f32)
    arrays = {
        "x_rows": rows,
        "x_tiles": rows.reshape(-1, P, C).transpose(1, 0, 2).reshape(P, -1),
        "x_cols": rows.T,
        "src_t": src_p.transpose(0, 2, 1),
        "dst_t": dst_p.transpose(2, 0, 1).reshape(P, S * T),
        "dst_n": dst_p.reshape(S, T * P),
        "heads": heads.reshape(1, -1),
        "heads_s": heads,
        "w_nat": padded(edge_weight1, EPAD, 0).reshape(1, P, -1),
        "ea_nat": padded(edge_attr_4, EPAD, 0).T.reshape(D, P, -1),
        "is_edge": (np.arange(EPAD) < E).astype(mybir.dt.np(BF16)).reshape(1, -1),
        "ident": np.eye(P, dtype=f32),
        "node_row": np.tile(np.arange(P, dtype=f32), (P, 1)),
        "is_node": (np.arange(NPAD) < N).astype(f32).reshape(-1, P).T,
        "first": np.tile(np.arange(0, NPAD, P, dtype=f32), (P, 1)),
        "w_hid0": parts_of(w["L0_gnn_W_l0"], row(w["L0_gnn_b_l0"])),
        "w_e0": np.concatenate([w["L0_gnn_W_l1"], row(w["L0_gnn_b_l1"])]),
        "w_hid1": parts_of(w["L1_gnn_W_edge"], row(w["L1_gnn_b_edge"])),
        "pick0": np.repeat(np.eye(3, dtype=f32), 4, axis=0),
        "pick1": np.repeat(np.eye(3, dtype=f32), 3 * D + 1, axis=0),
        "tail": tail,
        "w_msg_e": W_msg[2 * C:],
        "b_msg": row(w["L1_gnn_b_msg"]),
        "w_wide": np.concatenate([np.concatenate([W_msg[:C], W_msg[C:2 * C], w["L1_gnn_W_node"]], axis=1),
                                  np.concatenate([zero, zero, row(w["L1_gnn_b_node"])], axis=1)]),
        "gb_edge": np.concatenate([col(w["L1_gnn_g_edge"]), col(w["L1_gnn_beta_edge"])], axis=1),
        "gb_msg": np.concatenate([col(w["L1_gnn_g_msg"]), col(w["L1_gnn_beta_msg"])], axis=1),
        "gb_node": np.concatenate([row(w["L1_gnn_g_node"]), row(w["L1_gnn_beta_node"])], axis=1),
    }
    for l in range(2):
        for i in range(2):
            arrays[f"w_conv{l}_{i}"] = np.concatenate([w[f"L0_gnn_W{l}{i}"], row(w[f"L0_gnn_b{l}{i}"])])
            arrays[f"b_conv{l}_{i}"] = col(w[f"L0_gnn_b{l}{i}"])
    arrays = {f"in_{n}": np.ascontiguousarray(v) for n, v in arrays.items()}

    nc = bacc.Bacc("TRN2", target_bir_lowering=False, num_devices=1)
    aps = {n: nc.dram_tensor(n, v.shape, mybir.dt.from_np(v.dtype), kind="ExternalInput").ap() for n, v in arrays.items()}
    out = nc.dram_tensor("out", (NPAD, C), F32, kind="ExternalOutput").ap()
    gnn_kernel(nc, {n[3:]: v for n, v in aps.items()} | {"edges": E, "nodes": N}, out)
    r = run_bass_kernel_spmd(nc, [arrays], core_ids=[0])
    return r.results[0]["out"][:N]
```

```python
from contextlib import ExitStack

import concourse.bass as bass
from concourse import mybir

F32 = mybir.dt.float32
BF16 = mybir.dt.bfloat16
I32 = mybir.dt.int32
ALU = mybir.AluOpType
ACT = mybir.ActivationFunctionType
AX_X = mybir.AxisListType.X

P = 128
T = 26
W = 112
R = 32
CH = 4
CHUNKS = [(t, min(CH, T - t)) for t in range(0, T, CH)]
NC_ = len(CHUNKS)
U = 2
Q = U * NC_
NODE_TILES = 2
UN = 10
EPS = 1e-5


def slabs_of(edges):
    return -(-edges // (T * P * U)) * U


def inner_steps(n, npad, slabs):
    iters, step = slabs // U, NODE_TILES * P
    return max(min((n * (iters - 1) // iters - P) // step, npad // step, iters - 1), 0)


GROUPS = [(0, (NC_ + 1) // 2 - 1), ((NC_ + 1) // 2, NC_ - 1)]


def group_tiles(g):
    first, last = GROUPS[g]
    return CHUNKS[first][0], sum(CHUNKS[last])


def need(eng, sem, count):
    if not isinstance(count, int) or count > 0:
        eng.wait_ge(sem, count)


def opening(k):
    return isinstance(k, int) and k == 0


def repeat(eng, n, body):
    body(0)
    if n > 1:
        with eng.Fori(1, n) as k:
            body(k)


def phases(eng, iters, start, body):
    body(0, 0)
    for lo, hi, late in ((1, start, 0), (start, min(start + 1, iters), 1), (start + 1, iters, 2)):
        if lo < hi:
            with eng.Fori(lo, hi) as k:
                body(k, late)


class Marks:
    def __init__(self, sem, *names):
        self.sem, self.names = sem, names

    def of(self, ins):
        ins.then_inc(self.sem, 1)

    def wait(self, eng, name, i):
        eng.wait_ge(self.sem, len(self.names) * i + self.names.index(name) + 1)


def staged(eng, iters, width, plan, ahead=None, start=None, side=()):
    def beside(k, late, q):
        for place, stage in side:
            if late > 0 and place == q:
                stage(k - start)
            if late > 1 and place == q + width:
                stage(k - start - 1)

    def body(k, late):
        if ahead:
            ahead(k)
        for q in range(width):
            beside(k, late, q)
            for lag, stage in plan:
                if q >= lag:
                    stage(k, q - lag)
                elif not opening(k):
                    stage(k - 1, q - lag + width)
    phases(eng, iters, iters if start is None else start, body)
    for place, stage in side:
        if place >= width and start < iters:
            stage(iters - 1 - start)
    for q in range(max(lag for lag, _ in plan)):
        for lag, stage in plan:
            if q < lag:
                stage(iters - 1, width + q - lag)


def chunk(q):
    t0, nt = CHUNKS[q % NC_]
    return q // NC_, q % NC_, t0, nt


def gnn_kernel(nc, a, out):
    NPAD, C = a["x_rows"].shape
    N = a["nodes"]
    E = a["edges"]
    S = slabs_of(E)
    ITERS = S // U
    STEP = NODE_TILES * P
    STEPS = NPAD // STEP
    TILES = NPAD // P
    EPAD = S * T * P
    C1 = C + 1
    D = a["ea_nat"].shape[0]
    KW = a["w_hid0"].shape[0]
    KE = a["w_hid1"].shape[0]
    HEADS = S * NC_
    COLS = EPAD // P
    FIRST = ITERS - inner_steps(N, NPAD, S)
    PIECE = COLS // ITERS
    assert STEPS % UN == 0 and COLS % ITERS == 0 and S <= P and N < NPAD and C + R <= P

    ctx = ExitStack()
    with ctx:
        def sb(name, shape, dt=F32, where=ctx):
            return where.enter_context(nc.sbuf_tensor(name, shape, dt))

        stage = [0]

        def pools(where, **banks):
            stage[0] += 1
            return {n: [where.enter_context(nc.psum_tensor(f"ps{stage[0]}_{n}{i}", [P, 512], F32)) for i in range(k)]
                    for n, k in banks.items()}

        class Sems(dict):
            def __init__(self, where, block):
                self.where, self.block = where, block

            def __missing__(self, n):
                self[n] = self.where.enter_context(nc.semaphore(f"{self.block}_{n}"))
                return self[n]

        sums = sb("sums", [C1, NPAD])
        rel = sb("rel", [P, S * T])
        head_i = sb("head_i", [1, HEADS], I32)
        base_i = sb("base_i", [1, S], I32)
        base_all = sb("base_all", [P, S])
        fits = sb("fits", [1, 1], I32)
        ident = sb("ident", [P, P])
        node_row = sb("node_row", [P, P])
        first = sb("first", [P, TILES])
        ones = sb("ones", [P, P])
        eps = sb("eps", [P, 1])
        w_hid0 = sb("w_hid0", [KW, C], BF16)
        w_hid0_64 = sb("w_hid0_64", [64 + KW, C], BF16)
        w_hid0_at = w_hid0_64[64:64 + KW, :]
        w_hid1 = sb("w_hid1", [KE + 1, C + R], BF16)
        w_e0 = sb("w_e0", [C1, C])
        w_e1 = sb("w_e1", [C, C])
        w_conv = [[sb(f"w_conv{l}_{i}", [C1, C]) for i in range(2)] for l in range(2)]
        b_conv = [[sb(f"b_conv{l}_{i}", [C, 1]) for i in range(2)] for l in range(2)]
        w_wide = sb("w_wide", [C1, 3 * C])
        w_msg_e = sb("w_msg_e", [C, C])
        b_msg = sb("b_msg", [1, C])
        c_all = sb("c_all", [P, C])
        acc = [sb(f"acc{i}", [P, NODE_TILES * C]) for i in range(2)]
        gb_edge = sb("gb_edge", [C, 2])
        gb_msg = sb("gb_msg", [C, 2])
        gb_node = sb("gb_node", [P, 2 * C])
        w_fin = sb("w_fin", [C + 2, C])
        node_g = sb("node_g", [P, C])
        node_b = sb("node_b", [P, C])
        is_node = sb("is_node", [P, TILES])
        sumsq = sb("sumsq", [P, CH * C])
        slab_mv = sb("slab_mv", [C, S * 2])
        tmp = sb("tmp", [P, 16])
        lift = sb("lift", [C, C + 2])

        h1_rows = nc.dram_tensor("h1_rows", (NPAD, C), F32, kind="Internal").ap()
        p_rows = nc.dram_tensor("p_rows", (NPAD, C), F32, kind="Internal").ap()
        q_rows = nc.dram_tensor("q_rows", (NPAD, C), F32, kind="Internal").ap()
        w_parts = nc.dram_tensor("w_parts", (4, EPAD), BF16, kind="Internal").ap()
        ea_parts = nc.dram_tensor("ea_parts", (3 * D + 1, EPAD), BF16, kind="Internal").ap()
        nf_rows = nc.dram_tensor("nf_rows", (NPAD, C), F32, kind="Internal").ap()
        w_hid0_rows = nc.dram_tensor("w_hid0_rows", (KW, C), BF16, kind="Internal").ap()
        near = nc.dram_tensor("near", (S, T * P), BF16, kind="Internal").ap()

        def chain(eng, sem):
            count = [0]

            def go(ins):
                count[0] += 1
                ins.then_inc(sem, 1)
                return count[0]

            def done():
                eng.wait_ge(sem, count[0])
            return go, done

        def split(go, done, v, x, parts):
            for i, part in enumerate(parts):
                go(v.tensor_copy(part, x))
                done()
                if i < 2:
                    go(v.tensor_tensor(x, x, part, ALU.subtract))
                    done()

        with ExitStack() as st:
            dst_i = sb("dst_i", [P, S * T], I32, st)
            dst_n = sb("dst_n", [S, T * P], I32, st)
            near_f = sb("near_f", [S, T * P], F32, st)
            near_b = sb("near_b", [S, T * P], BF16, st)
            inside = sb("inside", [P, T * P], F32, st)
            heads = sb("heads", [1, HEADS], I32, st)
            heads_s = sb("heads_s", [S, NC_], I32, st)
            head_s = sb("head_s", [S, NC_], F32, st)
            head_f = sb("head_f", [1, HEADS], F32, st)
            base_f = sb("base_f", [1, S], F32, st)
            due = sb("due", [1, S], F32, st)
            ahead = sb("ahead", [1, S], F32, st)
            ps = pools(st, base=1, count=1)
            s = Sems(st, "setup")
            loads = [(ident, a["ident"]), (node_row, a["node_row"]), (first, a["first"]), (is_node, a["is_node"]),
                     (w_e0, a["w_e0"]),
                     (w_msg_e, a["w_msg_e"]), (b_msg, a["b_msg"]), (gb_edge, a["gb_edge"]),
                     (gb_msg, a["gb_msg"]), (w_wide, a["w_wide"]), (sums[0:C, :], a["x_cols"]),
                     (gb_node, a["gb_node"].to_broadcast([P, 2 * C]))]
            for l in range(2):
                for i in range(2):
                    loads += [(w_conv[l][i], a[f"w_conv{l}_{i}"]), (b_conv[l][i], a[f"b_conv{l}_{i}"])]
            block = st.enter_context(nc.Block())

            @block.sync
            def _(sp):
                sp.dma_start(heads[:], a["heads"]).then_inc(s["heads"], 16)
                sp.dma_start(heads_s[:], a["heads_s"]).then_inc(s["heads"], 16)
                sp.dma_start(due[:], a["due"]).then_inc(s["heads"], 16)
                sp.dma_start(dst_i[:], a["dst_t"]).then_inc(s["dst"], 16)
                sp.dma_start(dst_n[:], a["dst_n"]).then_inc(s["near"], 16)
                for to, src in loads:
                    sp.dma_start(to[:] if not isinstance(to, bass.AP) else to, src).then_inc(s["const"], 16)
                sp.wait_ge(s["const"], 16 * len(loads))
                sp.wait_ge(s["near"], 32)
                sp.dma_start(near, near_b[:]).then_inc(s["nearout"], 16)
                sp.wait_ge(s["nearout"], 16)

            @block.scalar
            def _(act):
                act.dma_start(w_parts[3:4, :], a["is_edge"]).then_inc(s["ones"], 16)
                act.dma_start(ea_parts[3 * D:3 * D + 1, :], a["is_edge"]).then_inc(s["ones"], 16)
                act.wait_ge(s["ones"], 32)

            @block.tensor
            def _(pe):
                pe.wait_ge(s["base"], 1)
                pe.matmul(ps["base"][0][:, 0:S], ones[0:1, :], base_f[:], start=True, stop=True).then_inc(s["pe"], 1)
                pe.wait_ge(s["cnt"], 1)
                pe.matmul(ps["count"][0][:, 0:2], ones[:], tmp[:, 0:2], start=True, stop=True).then_inc(s["pe"], 1)

            @block.vector
            def _(v):
                go, done = chain(v, s["dve"])
                go(v.memset(ones[:], 1.0))
                go(v.memset(eps[:], EPS))
                go(v.memset(lift[:], 0.0))
                go(v.memset(sumsq[:], 0.0))
                go(v.memset(tmp[:], 0.0))
                v.wait_ge(s["heads"], 48)
                go(v.tensor_scalar(base_f[:], heads[:].rearrange("p (s c) -> p s c", c=NC_)[:, :, 0],
                                   float(N - W), 0.0, ALU.min, ALU.max))
                go(v.tensor_scalar(head_f[:], heads[:], float(N - R), 0.0, ALU.min, ALU.max))
                go(v.tensor_scalar(head_s[:], heads_s[:], float(N - R), 0.0, ALU.min, ALU.max))
                done()
                v.drain().then_inc(s["base"], 1)
                go(v.tensor_copy(base_i[:], base_f[:]))
                go(v.tensor_copy(head_i[:], head_f[:]))
                v.wait_ge(s["dst"], 16)
                go(v.tensor_copy(rel[:], dst_i[:]))
                go(v.tensor_tensor(ahead[:], base_f[:], due[:], ALU.subtract))
                done()
                go(v.scalar_tensor_tensor(out=ahead[:], in0=ahead[:], scalar=0.0, in1=ones[0:1, 0:S],
                                          op0=ALU.is_ge, op1=ALU.mult, accum_out=tmp[0:1, 3:4]))
                v.wait_ge(s["pe"], 1)
                go(v.tensor_copy(base_all[:], ps["base"][0][:, 0:S]))
                done()
                rel3 = rel[:].rearrange("p (s t) -> p s t", t=T)
                go(v.tensor_tensor(rel3, rel3, base_all[:].unsqueeze(2).to_broadcast([P, S, T]), ALU.subtract))
                done()
                seen = inside[:, 0:S * T]
                go(v.tensor_scalar(seen, rel[:], 0.0, None, ALU.is_ge))
                done()
                go(v.scalar_tensor_tensor(out=seen, in0=rel[:], scalar=float(W), in1=seen,
                                          op0=ALU.is_lt, op1=ALU.mult, accum_out=tmp[:, 0:1]))
                v.wait_ge(s["near"], 16)
                for c, (t0, nt) in enumerate(CHUNKS):
                    go(v.tensor_scalar(near_f[:, t0 * P:(t0 + nt) * P], dst_n[:, t0 * P:(t0 + nt) * P],
                                       head_s[:, c:c + 1], None, ALU.subtract))
                done()
                go(v.tensor_scalar(inside[0:S, :], near_f[:], 0.0, None, ALU.is_ge))
                v.tensor_copy(near_b[:], near_f[:]).then_inc(s["near"], 16)
                done()
                go(v.scalar_tensor_tensor(out=inside[0:S, :], in0=near_f[:], scalar=float(R), in1=inside[0:S, :],
                                          op0=ALU.is_lt, op1=ALU.mult, accum_out=tmp[0:S, 1:2]))
                done()
                v.drain().then_inc(s["cnt"], 1)
                v.wait_ge(s["pe"], 2)
                go(v.tensor_scalar(tmp[0:1, 2:3], ps["count"][0][0:1, 0:1], ps["count"][0][0:1, 1:2], float(2 * E),
                                   ALU.add, ALU.is_equal))
                done()
                go(v.tensor_scalar(tmp[0:1, 2:3], tmp[0:1, 3:4], float(S), tmp[0:1, 2:3], ALU.is_equal, ALU.mult))
                done()
                go(v.tensor_copy(fits[:], tmp[0:1, 2:3]))
                done()

        def edge_pass(name, table, y=None, split_edges=False, stats=False, last=False):
            K = KE + 1 if last else KW
            HC = C + R if last else C
            M = C1 if last else C
            with ExitStack() as st:
                idx = [sb(f"{name}_idx{j}", [P, T], I32, st) for j in range(U)]
                got = [sb(f"{name}_got{j}", [P, T * C], F32, st) for j in range(U)]
                AT = 64 if stats else 0
                row = [sb(f"{name}_row{j}", [AT + K, T * P], BF16, st) for j in range(U)]
                hid = [sb(f"{name}_hid{i}", [P, CH * P], F32, st) for i in range(2)]
                msg = [sb(f"{name}_msg{i}", [P, CH * C], F32, st) for i in range(2)]
                rem = [sb(f"{name}_rem{i}", [P, CH * C], F32, st) for i in range(2)]
                part0 = [sb(f"{name}_part0_{i}", [P, CH * C1], BF16, st) for i in range(NC_)]
                part1 = [sb(f"{name}_part1_{i}", [P, CH * C1], BF16, st) for i in range(2)]
                part2 = [sb(f"{name}_part2_{i}", [P, CH * C1], BF16, st) for i in range(2)]
                hot = [sb(f"{name}_hot{i}", [P, CH * P], BF16, st) for i in range(2)]
                dst = sb(f"{name}_dst", [P, T], F32, st)
                off = sb(f"{name}_off", [P, CH], F32, st)
                if last:
                    w_q = [sb(f"{name}_w_q{j}", [P, NC_ * C], F32, st) for j in range(U)]
                    sq = [sb(f"{name}_sq{i}", [P, CH * C], F32, st) for i in range(2)]
                    spread = sb("spread", [C, P], F32, st)
                    slab_sq = sb("slab_sq", [C, S], F32, st)
                    tot = sb("tot", [P, 2 * C], F32, st)
                    mom = sb("mom", [P, 2 * C], F32, st)
                    var = sb("var", [P, C], F32, st)
                    nf_in = sb("nf_in", [P, NODE_TILES * C], F32, st)
                    q_idx = sb(f"{name}_q_idx", [P, T], I32, st)
                if stats:
                    srow = [row[j][0:KE, :] for j in range(U)]
                    feat = [sb(f"{name}_feat{i}", [C, CH * P], F32, st) for i in range(2)]
                    parts = sb(f"{name}_parts", [C, NC_ * 6], F32, st)
                    mv1 = sb(f"{name}_mv1", [C, 2], F32, st)
                    xs = sb("xs", [P, NODE_TILES * C], F32, st)
                    xt = sb("xt", [C1, STEP], F32, st)
                    parts_y = sb("parts_y", [P, NODE_TILES * 6], F32, st)
                    mv_y = sb("mv_y", [P, NODE_TILES * 2], F32, st)
                    rstd = sb("rstd", [P, NODE_TILES], F32, st)
                    shift = sb("shift", [P, NODE_TILES], F32, st)
                    nf = sb("nf", [P, NODE_TILES * C], F32, st)
                    nf_sq = sb("nf_sq", [P, NODE_TILES * C], F32, st)
                    zeros = sb("zeros", [C, STEP], F32, st)
                    none = sb("none", [1, C], F32, st)
                    rows_out = sb("pq_out", [P, 2, NODE_TILES * C], F32, st)
                if not last:
                    z = sb(f"{name}_z", [C1, STEP], F32, st)
                if split_edges:
                    cols = sb("cols", [C, STEP], F32, st)
                    rows_out = sb("h1_out", [P, NODE_TILES * C], F32, st)
                    w_f = sb(f"{name}_w_f", [P, COLS], F32, st)
                    w_p = [sb(f"{name}_w_p{i}", [P, COLS], BF16, st) for i in range(3)]
                    e_f = sb(f"{name}_e_f", [P, D * PIECE], F32, st)
                    e_p = sb(f"{name}_e_p", [P, 3 * D * PIECE], BF16, st)
                    hid_f = [sb(f"hid_f{i}", [k, C], F32, st) for i, k in enumerate((KW, KE))]
                    pick = [sb(f"pick{i}", [k, 3], F32, st) for i, k in enumerate((KW, KE))]
                    hid_p = [sb(f"hid_p{i}", [KE, C], BF16, st) for i in range(3)]
                    hid_t = sb("hid_t", [KE, C], F32, st)
                    tail_f = sb("tail_f", [KE + 1, R], F32, st)
                    hid_loads = [(hid_f[0], a["w_hid0"]), (hid_f[1], a["w_hid1"]), (pick[0], a["pick0"]),
                                 (pick[1], a["pick1"]), (tail_f, a["tail"])]
                ps = pools(st, hid=2, pre=2, win=2, **(dict(feat=1, node=1) if stats else dict(f=1, tot=1) if last else dict(node=1)))
                s = Sems(st, name)
                block = st.enter_context(nc.Block())

                def left(k, q):
                    return Q * k + q - 1

                def load_rows(sp, j, slab):
                    src, n = (ea_parts, 3 * D + 1) if last else (w_parts, 4)
                    at = bass.ds(slab * (T * P), T * P)
                    for i in range(3):
                        sp.dma_start(row[j][AT + i * n:AT + (i + 1) * n, :], src[:, at]).then_inc(s[f"row{j}"], 16)
                    if last:
                        sp.dma_start(row[j][KE:KE + 1, :], near[bass.ds(slab, 1), :]).then_inc(s[f"row{j}"], 16)
                    if stats:
                        for i in range(3):
                            n = 3 * D + 1
                            sp.dma_start(srow[j][i * n:(i + 1) * n, :], ea_parts[:, at]).then_inc(s[f"srow{j}"], 16)
                ROWS = 16 * (4 if last else 3)

                def load_idx(sp, j, slab):
                    sp.dma_start(idx[j][:], a["src_t"][bass.ds(slab, 1)].rearrange("s p t -> (s p) t")).then_inc(s[f"idx{j}"], 16)

                w_hid = w_hid1 if last else w_hid0_at if stats else w_hid0

                def hidden(pe, j, q, b, n, free):
                    t0, nt = CHUNKS[q % NC_]
                    need(pe, s["rhid"], free)
                    if last:
                        need(pe, s["hot_t"], free)
                    pe.matmul(ps["hid"][b][0:HC, 0:nt * P], w_hid[:], row[j][AT:AT + K, t0 * P:(t0 + nt) * P],
                              start=True, stop=True).then_inc(s["hid"], 1)

                def features(pe, j, q, b, n, free):
                    t0, nt = CHUNKS[q % NC_]
                    need(pe, s["rf"], n)
                    pe.matmul(ps["feat"][0][0:C, 0:nt * P], w_hid1[0:KE, 0:C], srow[j][:, t0 * P:(t0 + nt) * P],
                              start=True, stop=True).then_inc(s["f"], 1)

                def relu_hidden(act, q, b, n, free):
                    nt = CHUNKS[q % NC_][1]
                    act.wait_ge(s["hid"], n + 1)
                    need(act, s["pre"], free)
                    act.activation(hid[b][0:C, 0:nt * P], ps["hid"][b][0:C, 0:nt * P], ACT.Relu).then_inc(s["rhid"], 1)

                def relu_features(act, q, b, n, free):
                    nt = CHUNKS[q % NC_][1]
                    act.wait_ge(s["f"], n + 1)
                    need(act, s["bn"], free)
                    act.activation(feat[b][:, 0:nt * P], ps["feat"][0][0:C, 0:nt * P], ACT.Relu).then_inc(s["rf"], 1)

                def tiles_of(x, nt, stride):
                    return x[:].rearrange("p (t c) -> p t c", c=stride)[:, 0:nt, 0:C]

                def relu_message(act, j, q, b, n, free, part_free):
                    t0, nt = CHUNKS[q % NC_]
                    m3 = got[j][:, t0 * C:(t0 + nt) * C].rearrange("p (t c) -> p t c", c=C)
                    act.wait_ge(s["add"], n + 1)
                    need(act, s["rem"], free)
                    act.activation(tiles_of(msg[b], nt, C), m3, ACT.Relu).then_inc(s["msg"], 1)
                    need(act, s["seg"], part_free)
                    act.activation(tiles_of(part0[q % NC_], nt, C1), m3, ACT.Relu).then_inc(s["part0"], 1)

                def subtract_first(v, q, b, n, free):
                    nt = CHUNKS[q % NC_][1]
                    v.wait_ge(s["part0"], n + 1)
                    need(v, s["part2"], free)
                    v.tensor_tensor(tiles_of(rem[b], nt, C), tiles_of(msg[b], nt, C), tiles_of(part0[q % NC_], nt, C1),
                                    ALU.subtract).then_inc(s["rem"], 1)

                def second_part(act, q, b, n, free):
                    nt = CHUNKS[q % NC_][1]
                    act.wait_ge(s["rem"], n + 1)
                    need(act, s["seg"], free)
                    act.copy(tiles_of(part1[b], nt, C1), tiles_of(rem[b], nt, C)).then_inc(s["part1"], 1)

                def third_part(v, q, b, n, free):
                    nt = CHUNKS[q % NC_][1]
                    v.wait_ge(s["part1"], n + 1)
                    need(v, s["seg"], free)
                    v.tensor_tensor(tiles_of(part2[b], nt, C1), tiles_of(rem[b], nt, C), tiles_of(part1[b], nt, C1),
                                    ALU.subtract).then_inc(s["part2"], 1)

                def sum_window(pe, bank, hot_b, width, parts, t, start, stop):
                    for i, part in enumerate(parts):
                        mm = pe.matmul(bank[0:M, 0:width], part[:, t * C1:t * C1 + M], hot_b[:, t * width:(t + 1) * width],
                                       start=start and i == 0, stop=stop and i == 2)
                    return mm

                def square_message(act, q, b, n, sq_free):
                    nt = CHUNKS[q % NC_][1]
                    act.wait_ge(s["msg"], n + 1)
                    need(act, s["sumsq"], sq_free)
                    act.activation(tiles_of(sq[b], nt, C), tiles_of(msg[b], nt, C), ACT.Square).then_inc(s["sq"], 1)

                def batch_statistics(v, slab, q, b, n):
                    nt = CHUNKS[q % NC_][1]
                    c = q % NC_
                    v.wait_ge(s["rf"], n + 1)
                    if c == 0:
                        need(v, s["flush"], slab)
                    v.bn_stats(parts[:, c * 6:(c + 1) * 6], feat[b][:, 0:nt * P]).then_inc(s["bn"], 1)
                    if c == NC_ - 1:
                        v.wait_ge(s["bn"], n + 1)
                        need(v, s["keep"], slab)
                        v.nop(nofuse=True)
                        v.bn_aggr(mv1[:], parts[:]).then_inc(s["flush"], 1)
                        v.wait_ge(s["flush"], slab + 1)
                        v.tensor_copy(slab_mv[:, bass.ds(slab * 2, 2)], mv1[:]).then_inc(s["keep"], 1)

                def add_gathered(v, j, q, b, n, inc=True):
                    t0, nt = CHUNKS[q % NC_]
                    v.wait_ge(s["pre"], n + 1)
                    at = got[j][:, t0 * C:(t0 + nt) * C]
                    ins = v.tensor_tensor(at, at, ps["pre"][b][:, 0:nt * C], ALU.add)
                    return ins.then_inc(s["add"], 1) if inc else ins

                def add_squares(v, q, b, n):
                    nt = CHUNKS[q % NC_][1]
                    v.wait_ge(s["sq"], n + 1)
                    need(v, s["sumsq"], n)
                    v.tensor_tensor(sumsq[:, 0:nt * C], sumsq[:, 0:nt * C], sq[b][:, 0:nt * C], ALU.add).then_inc(s["sumsq"], 1)

                def prepare(v):
                    for i in range(2):
                        v.memset(hid[i][64:P, :], 1.0)
                        v.memset(part1[i][:], 0.0)
                        v.memset(part2[i][:], 0.0)
                    for x in part0:
                        v.memset(x[:], 1.0)
                    if stats:
                        go, done = chain(v, s["zero"])
                        go(v.memset(z[C:C1, :], 1.0))
                        go(v.memset(xt[C:C1, :], 1.0))
                        go(v.memset(none[:], -3e38))
                        go(v.memset(zeros[:], 0.0))
                        for x in acc:
                            go(v.memset(x[:], 0.0))
                        done()
                    if last:
                        fold_edges(v)
                        norm_nodes(v)
                        for j in range(U):
                            v.tensor_copy(w_q[j][0:C, :].rearrange("p (k c) -> p k c", c=C),
                                          w_e1[:].unsqueeze(1).to_broadcast([C, NC_, C]))
                    if split_edges:
                        go, done = chain(v, s["wcut"])
                        v.wait_ge(s["wf"], 16)
                        split(go, done, v, w_f[:], [x[:] for x in w_p])
                        go(v.memset(w_hid1[:], 0.0))
                        go(v.memset(sums[C:C1, :], 0.0))
                        v.wait_ge(s["hf"], 16 * len(hid_loads))
                        for x, m, to in ((hid_f[0], pick[0], w_hid0[:]), (hid_f[1], pick[1], w_hid1[0:KE, 0:C])):
                            K = x.shape[0]
                            split(go, done, v, x[:], [h[0:K, :] for h in hid_p])
                            go(v.tensor_scalar(hid_t[0:K, :], hid_p[0][0:K, :], m[:, 0:1], None, ALU.mult))
                            done()
                            go(v.scalar_tensor_tensor(out=hid_t[0:K, :], in0=hid_p[1][0:K, :], scalar=m[:, 1:2],
                                                      in1=hid_t[0:K, :], op0=ALU.mult, op1=ALU.add))
                            done()
                            go(v.scalar_tensor_tensor(out=to, in0=hid_p[2][0:K, :], scalar=m[:, 2:3], in1=hid_t[0:K, :],
                                                      op0=ALU.mult, op1=ALU.add))
                            done()
                        go(v.tensor_copy(w_hid1[:, C:C + R], tail_f[:]))
                        done()
                    v.drain().then_inc(s["init"], 1)
                    v.sem_inc(s["step"], 1)

                def fold_edges(v):
                    go, done = chain(v, s["fold"])
                    mv3 = slab_mv[:].rearrange("p (s m) -> p m s", m=2)
                    go(v.tensor_tensor(slab_sq[:], mv3[:, 0, :], mv3[:, 0, :], ALU.mult))
                    done()
                    go(v.tensor_tensor(slab_sq[:], slab_sq[:], mv3[:, 1, :], ALU.add))
                    done()
                    go(v.tensor_reduce(tmp[0:C, 8:9], mv3[:, 0, :], AX_X, ALU.add))
                    go(v.tensor_reduce(tmp[0:C, 9:10], slab_sq[:], AX_X, ALU.add))
                    done()
                    go(v.tensor_scalar(tmp[0:C, 8:10], tmp[0:C, 8:10], float(T * P) / E, None, ALU.mult))
                    done()
                    fold(v, go, done, s["f_in"], s["f_out"], tmp[0:C, 8:9], tmp[0:C, 9:10], gb_edge)
                    go(v.tensor_copy(spread[:], lift[:, C:C1].to_broadcast([C, P])))
                    done()
                    v.drain().then_inc(s["f_in"], 1)
                    go(v.tensor_scalar(w_e1[:], w_msg_e[:], tmp[0:C, 4:5], None, ALU.mult))
                    v.wait_ge(s["f_pe"], 1)
                    go(v.tensor_copy(c_all[:], ps["f"][0][:, 0:C]))
                    done()

                def norm_nodes(v):
                    go, done = chain(v, s["norm"])
                    for i in range(2):
                        go(v.tensor_tensor(tot[:, i * C:(i + 1) * C], acc[i][:, 0:C], acc[i][:, C:2 * C], ALU.add))
                    done()
                    v.drain().then_inc(s["t_in"], 1)
                    v.wait_ge(s["t_pe"], 1)
                    go(v.tensor_scalar(mom[:], ps["tot"][0][:, 0:2 * C], 1.0 / N, None, ALU.mult))
                    done()
                    go(v.tensor_tensor(var[:], mom[:, 0:C], mom[:, 0:C], ALU.mult))
                    done()
                    go(v.tensor_tensor(var[:], mom[:, C:2 * C], var[:], ALU.subtract))
                    done()
                    v.drain().then_inc(s["t_in"], 1)
                    v.wait_ge(s["root"], 1)
                    go(v.reciprocal(var[:], var[:]))
                    done()
                    go(v.tensor_tensor(node_g[:], var[:], gb_node[:, 0:C], ALU.mult))
                    done()
                    go(v.tensor_tensor(var[:], mom[:, 0:C], node_g[:], ALU.mult))
                    done()
                    go(v.tensor_tensor(node_b[:], gb_node[:, C:2 * C], var[:], ALU.subtract))
                    done()

                START = max(1, ITERS - STEPS) if last else FIRST
                l = 1 if stats else 0
                on_pe = Marks(s["n_pe"], *(("a", "b", "turn") if split_edges else ("a", "b", "turn", "pq", "nf")))
                on_act = Marks(s["n_act"], *(("z", "cols", "sums") if split_edges else ("z", "clear", "root", "y", "xt", "pq", "sq")))
                on_dve = Marks(s["n_dve"], *(("rows",) if split_edges else ("scaled", "added") if last else
                                             ("y", "stat0", "stat1", "aggr0", "aggr1", "recip", "shift", "x0", "x1",
                                              "nf0", "nf1", "acc0", "acc1")))
                def node_cols(i):
                    return bass.ds(i * STEP, STEP)

                def node_y(i):
                    return y[:, bass.ds(i * (NODE_TILES * C), NODE_TILES * C)]

                def store_rows(act, i, table, tile):
                    act.dma_start(table[node_cols(i), :].rearrange("(t p) c -> p t c", p=P),
                                  tile.rearrange("p (t c) -> p t c", c=C)).then_inc(s["n_out"], 16)

                def load_features(sp, i):
                    sp.wait_ge(s["step"], i + 1)
                    sp.nop(nofuse=True)
                    sp.dma_start(nf_in[:].rearrange("p (t c) -> p t c", c=C),
                                 nf_rows[node_cols(i), :].rearrange("(t p) c -> p t c", p=P)).then_inc(s["n_in"], 16)

                def first_layer(i):
                    nc.tensor.wait_ge(s["step"], i + 1)
                    on_pe.of(nc.tensor.matmul(ps["node"][0][0:C, 0:STEP], w_conv[l][0][0:C, :], sums[0:C, node_cols(i)],
                                              start=True, stop=True))

                def second_cols(i):
                    on_act.wait(nc.tensor, "z", i)
                    on_pe.of(nc.tensor.matmul(ps["node"][0][0:C, 0:STEP], w_conv[l][1][0:C, :], z[0:C, :], start=True, stop=True))

                def turn_cols(i):
                    on_act.wait(nc.tensor, "sums", i)
                    for t in range(NODE_TILES):
                        mm = nc.tensor.transpose(ps["node"][0][:, t * C:(t + 1) * C], cols[:, t * P:(t + 1) * P], ident[0:C, 0:C])
                    on_pe.of(mm)

                def second_rows(i):
                    on_act.wait(nc.tensor, "z", i)
                    for t in range(NODE_TILES):
                        mm = nc.tensor.matmul(ps["node"][0][:, t * C:(t + 1) * C], z[:, t * P:(t + 1) * P], w_conv[l][1][:],
                                              start=True, stop=True)
                    on_pe.of(mm)

                def turn_x2(i):
                    on_dve.wait(nc.tensor, "x1", i)
                    for t in range(NODE_TILES):
                        mm = nc.tensor.transpose(ps["node"][0][0:C, t * P:(t + 1) * P], xs[:, t * C:(t + 1) * C], ident[:])
                    on_pe.of(mm)

                def message_products(i):
                    on_act.wait(nc.tensor, "xt", i)
                    for t in range(NODE_TILES):
                        mm = nc.tensor.matmul(ps["node"][0][:, t * 2 * C:(t + 1) * 2 * C], xt[:, t * P:(t + 1) * P],
                                              w_wide[:, 0:2 * C], start=True, stop=True)
                    on_pe.of(mm)

                def node_products(i):
                    on_act.wait(nc.tensor, "pq", i)
                    for t in range(NODE_TILES):
                        mm = nc.tensor.matmul(ps["node"][0][:, t * C:(t + 1) * C], xt[:, t * P:(t + 1) * P],
                                              w_wide[:, 2 * C:3 * C], start=True, stop=True)
                    on_pe.of(mm)

                def relu_z(i):
                    on_pe.wait(nc.scalar, "a", i)
                    on_act.of(nc.scalar.activation(z[0:C, :], ps["node"][0][0:C, 0:STEP], ACT.Relu, bias=b_conv[l][0][:]))

                def clear_sums(i):
                    on_act.of(nc.scalar.copy(sums[0:C, node_cols(i)], zeros[:]))

                def relu_cols(i):
                    on_pe.wait(nc.scalar, "b", i)
                    for to in (cols[:], sums[0:C, node_cols(i)]):
                        on_act.of(nc.scalar.activation(to, ps["node"][0][0:C, 0:STEP], ACT.Relu, bias=b_conv[l][1][:]))

                def store_h1(i):
                    on_dve.wait(nc.scalar, "rows", i)
                    nc.scalar.nop(nofuse=True)
                    store_rows(nc.scalar, i, h1_rows, rows_out[:])

                def root_y(i):
                    on_dve.wait(nc.scalar, "aggr1", i)
                    on_act.of(nc.scalar.activation(rstd[:], mv_y[:].rearrange("p (t m) -> p m t", m=2)[:, 1, :], ACT.Sqrt, bias=eps[:]))

                def copy_x2(i):
                    on_dve.wait(nc.scalar, "x1", i)
                    on_act.of(nc.scalar.copy(node_y(i), xs[:]))
                    on_pe.wait(nc.scalar, "turn", i)
                    on_act.of(nc.scalar.copy(xt[0:C, :], ps["node"][0][0:C, 0:STEP]))

                def store_pq(i):
                    on_pe.wait(nc.scalar, "pq", i)
                    on_act.of(nc.scalar.copy(rows_out[:].rearrange("p h (t c) -> p t h c", c=C),
                                             ps["node"][0][:, 0:NODE_TILES * 2 * C].rearrange("p (t h c) -> p t h c", h=2, c=C)))
                    on_act.wait(nc.scalar, "pq", i)
                    nc.scalar.nop(nofuse=True)
                    store_rows(nc.scalar, i, p_rows, rows_out[:, 0, :])
                    store_rows(nc.scalar, i, q_rows, rows_out[:, 1, :])

                def square_nf(i):
                    on_dve.wait(nc.scalar, "nf1", i)
                    on_act.of(nc.scalar.activation(nf_sq[:], nf[:], ACT.Square))
                    nc.scalar.nop(nofuse=True)
                    store_rows(nc.scalar, i, nf_rows, nf[:])

                def copy_rows(i):
                    on_pe.wait(nc.vector, "turn", i)
                    on_dve.of(nc.vector.tensor_copy(rows_out[:], ps["node"][0][:, 0:NODE_TILES * C]))

                def residual(i):
                    v = nc.vector
                    v.wait_ge(s["x"], 16)
                    on_pe.wait(v, "b", i)
                    on_dve.of(v.scalar_tensor_tensor(out=node_y(i), in0=ps["node"][0][:, 0:NODE_TILES * C], scalar=0.0,
                                                     in1=node_y(i), op0=ALU.max, op1=ALU.add))
                    on_dve.wait(v, "y", i)
                    for t in range(NODE_TILES):
                        on_dve.of(v.bn_stats(parts_y[:, t * 6:(t + 1) * 6], y[:, bass.ds((i * NODE_TILES + t) * C, C)]))
                    on_dve.wait(v, "stat1", i)
                    v.nop(nofuse=True)
                    for t in range(NODE_TILES):
                        on_dve.of(v.bn_aggr(mv_y[:, 2 * t:2 * t + 2], parts_y[:, t * 6:(t + 1) * 6]))

                def layer_norm(i):
                    v = nc.vector
                    on_act.wait(v, "root", i)
                    on_dve.of(v.reciprocal(rstd[:], rstd[:]))
                    on_dve.wait(v, "recip", i)
                    on_dve.of(v.scalar_tensor_tensor(out=shift[:], in0=mv_y[:].rearrange("p (t m) -> p m t", m=2)[:, 0, :],
                                                     scalar=-1.0, in1=rstd[:], op0=ALU.mult, op1=ALU.mult))
                    on_dve.wait(v, "shift", i)
                    for t in range(NODE_TILES):
                        on_dve.of(v.tensor_scalar(xs[:, t * C:(t + 1) * C], y[:, bass.ds((i * NODE_TILES + t) * C, C)],
                                                  rstd[:, t:t + 1], shift[:, t:t + 1], ALU.mult, ALU.add))

                def relu_nf(i):
                    v = nc.vector
                    on_pe.wait(v, "nf", i)
                    for t in range(NODE_TILES):
                        on_dve.of(v.tensor_scalar(nf[:, t * C:(t + 1) * C], ps["node"][0][:, t * C:(t + 1) * C],
                                                  0.0, is_node[:, bass.ds(i * NODE_TILES + t, 1)], ALU.max, ALU.mult))

                def add_nf(i):
                    v = nc.vector
                    on_dve.wait(v, "nf1", i)
                    on_dve.of(v.tensor_tensor(acc[0][:], acc[0][:], nf[:], ALU.add))
                    on_act.wait(v, "sq", i)
                    on_dve.of(v.tensor_tensor(acc[1][:], acc[1][:], nf_sq[:], ALU.add))

                def end_step(i):
                    v = nc.vector
                    on_dve.wait(v, "rows" if split_edges else "acc1", i)
                    v.wait_ge(s["n_out"], (16 if split_edges else 48) * (i + 1))
                    v.sem_inc(s["step"], 1)

                def add_features(i):
                    v = nc.vector
                    v.wait_ge(s["n_in"], 16 * (i + 1))
                    at = nf_in[:].rearrange("p (t c) -> p t c", c=C)
                    on_dve.of(v.tensor_tensor(at, at, node_g[:].unsqueeze(1).to_broadcast([P, NODE_TILES, C]), ALU.mult))
                    on_dve.wait(v, "scaled", i)
                    on_dve.of(v.tensor_tensor(node_y(i), node_y(i), nf_in[:], ALU.add))
                    on_dve.wait(v, "added", i)
                    v.sem_inc(s["step"], 1)

                def node_stages(eng):
                    if last:
                        return [(3, add_features)] if eng is nc.vector else []
                    if split_edges:
                        return {nc.tensor: [(4, first_layer), (6, second_cols), (8, turn_cols)],
                                nc.scalar: [(5, relu_z), (7, relu_cols), (10, store_h1)],
                                nc.vector: [(9, copy_rows), (13, end_step)]}[eng]
                    return {nc.tensor: [(4, first_layer), (6, second_rows), (10, turn_x2), (12, message_products), (Q, node_products)],
                            nc.scalar: [(5, relu_z), (5, clear_sums), (8, root_y), (11, copy_x2), (13, store_pq), (Q + 2, square_nf)],
                            nc.vector: [(7, residual), (9, layer_norm), (Q + 1, relu_nf), (Q + 3, add_nf), (Q + 3, end_step)]}[eng]

                def node_steps(eng, lo, summed):
                    if eng is nc.sync:
                        if last:
                            if lo < STEPS:
                                with eng.Fori(lo, STEPS) as i:
                                    load_features(eng, i)
                        return
                    if eng is nc.gpsimd:
                        return
                    stages = node_stages(eng)
                    if eng is nc.tensor and not last:
                        for sem, count in summed:
                            eng.wait_ge(sem, count)
                        eng.nop(nofuse=True)
                    if stages and lo < STEPS:
                        with eng.Fori(lo, STEPS) as i:
                            for _, stage in stages:
                                stage(i)

                def sync_windows(sp):
                    def free(sem, k, j, c):
                        if not opening(k):
                            sp.wait_ge(s[sem], Q * (k - 1) + NC_ * j + c + 1)
                            sp.nop(nofuse=True)

                    def slab_idx(k, j):
                        free("add", k, j, GROUPS[-1][0])
                        load_idx(sp, j, k * U + j)

                    def slab_rows(k, j):
                        free("hid", k, j, NC_ - 1)
                        if stats:
                            free("f", k, j, NC_ - 1)
                        load_rows(sp, j, k * U + j)
                        if last:
                            free("pre", k, j, NC_ - 1)
                            for c in range(NC_):
                                h = sp.value_load(head_i[0:1, bass.ds((k * U + j) * NC_ + c, 1)], min_val=0, max_val=N - R)
                                sp.dma_start(w_q[j][C:C + R, c * C:(c + 1) * C], q_rows[bass.ds(h, R), :]).then_inc(s[f"q{j}"], 16)

                    def body(k, late):
                        if late and last:
                            load_features(sp, k - START)
                        if opening(k):
                            for j in range(U):
                                slab_idx(k, j)
                        if split_edges:
                            load_piece(sp, k)
                            if opening(k):
                                sp.wait_ge(s["wout"], 48)
                        for j in range(U):
                            if not opening(k):
                                slab_idx(k, j)
                            slab_rows(k, j)
                        if split_edges:
                            store_parts(sp, k)
                    phases(sp, ITERS, START, body)
                    if split_edges:
                        sp.wait_ge(s["init"], 1)
                        sp.dma_start(w_hid0_rows, w_hid0[:]).then_inc(s["whid"], 16)
                        sp.wait_ge(s["whid"], 16)
                        sp.wait_ge(s["eout"], 48 * ITERS)

                def load_piece(sp, k):
                    if not opening(k):
                        sp.wait_ge(s["estep"], k)
                        sp.nop(nofuse=True)
                    sp.dma_start(e_f[:].rearrange("p (d i) -> p d i", d=D),
                                 a["ea_nat"][:, :, bass.ds(k * PIECE, PIECE)].rearrange("d p i -> p d i")).then_inc(s["ef"], 16)

                def store_parts(sp, k):
                    sp.wait_ge(s["estep"], k + 1)
                    sp.nop(nofuse=True)
                    for i in range(3):
                        sp.dma_start(ea_parts[i * D:(i + 1) * D, :].rearrange("d (p i) -> p d i", p=P)[:, :, bass.ds(k * PIECE, PIECE)],
                                     e_p[:, i * D * PIECE:(i + 1) * D * PIECE].rearrange("p (d i) -> p d i", d=D)
                                     ).then_inc(s["eout"], 16)

                def split_piece(v, k):
                    v.wait_ge(s["ef"], 16 * (k + 1))
                    need(v, s["eout"], 48 * k)
                    n = D * PIECE
                    for i in range(3):
                        part = e_p[:, i * n:(i + 1) * n]
                        ins = v.tensor_copy(part, e_f[:])
                        ins.then_inc(s["estep"] if i == 2 else s["ecut"], 1)
                        if i < 2:
                            v.wait_ge(s["ecut"], 4 * k + 2 * i + 1)
                            v.tensor_tensor(e_f[:], e_f[:], part, ALU.subtract).then_inc(s["ecut"], 1)
                            v.wait_ge(s["ecut"], 4 * k + 2 * i + 2)

                def gpsimd_windows(gp):
                    def body(k):
                        for j in range(U):
                            for g, (_, end) in enumerate(GROUPS):
                                if not opening(k):
                                    gp.wait_ge(s["part0"], Q * (k - 1) + NC_ * j + end + 1)
                                if g == 0:
                                    gp.wait_ge(s[f"idx{j}"], 16 * (k + 1))
                                gp.nop(nofuse=True)
                                for t in range(*group_tiles(g)):
                                    gp.indirect_dma_start(got[j][:, t * C:(t + 1) * C], None, table,
                                                          bass.IndirectOffsetOnAxis(idx[j][:, t:t + 1], 0)
                                                          ).then_inc(s[f"got{j}{g}"], 16)
                    repeat(gp, ITERS, body)

                def tensor_windows(pe):
                    def hidden_rows(k, q):
                        j, c, _, _ = chunk(q)
                        if c == 0:
                            pe.wait_ge(s[f"row{j}"], ROWS * (k + 1))
                        hidden(pe, j, q, q % 2, Q * k + q, left(k, q))
                        if stats:
                            if c == 0:
                                pe.wait_ge(s[f"srow{j}"], 48 * (k + 1))
                            features(pe, j, q, q % 2, Q * k + q, left(k, q))

                    def pre(k, q):
                        j, c, t0, nt = chunk(q)
                        pe.wait_ge(s["rhid"], Q * k + q + 1)
                        need(pe, s["add"], left(k, q))
                        if last:
                            pe.wait_ge(s["hot_t"], Q * k + q + 1)
                            if c == 0:
                                pe.wait_ge(s[f"qc{j}"], k + 1)
                        for t in range(nt):
                            mm = pe.matmul(ps["pre"][q % 2][:, t * C:(t + 1) * C], hid[q % 2][0:P if last else C1, t * P:(t + 1) * P],
                                           w_q[j][:, c * C:(c + 1) * C] if last else w_e0[:], start=True, stop=True)
                        mm.then_inc(s["pre"], 1)

                    def segment(k, q):
                        j, c, t0, nt = chunk(q)
                        if c == 0:
                            need(pe, s[f"win{j}"], k)
                        pe.wait_ge(s["part2"], Q * k + q + 1)
                        pe.wait_ge(s["hot"], Q * k + q + 1)
                        for t in range(nt):
                            mm = sum_window(pe, ps["win"][j], hot[q % 2], W, (part0[q % NC_], part1[q % 2], part2[q % 2]), t,
                                            t0 + t == 0, t0 + t == T - 1)
                        mm.then_inc(s["seg"], 1)

                    def summed(i):
                        for j in range(U):
                            pe.wait_ge(s[f"win{j}"], i + START)

                    staged(pe, ITERS, Q, [(0, hidden_rows), (1, pre), (3, segment)],
                           start=START, side=([] if last else [(4, summed)]) + node_stages(pe))

                def scalar_windows(act):
                    plan = [(0, lambda k, q: relu_hidden(act, q, q % 2, Q * k + q, left(k, q)))]
                    if stats:
                        plan += [(0, lambda k, q: relu_features(act, q, q % 2, Q * k + q, left(k, q)))]
                    def message(k, q):
                        part_free = Q * k + q - NC_ + 1
                        relu_message(act, chunk(q)[0], q, q % 2, Q * k + q, left(k, q), part_free)

                    plan += [(1, message)]
                    if last:
                        plan += [(1, lambda k, q: square_message(act, q, q % 2, Q * k + q, left(k, q)))]
                    plan += [(2, lambda k, q: second_part(act, q, q % 2, Q * k + q, left(k, q)))]
                    staged(act, ITERS, Q, plan, start=START, side=node_stages(act))

                def vector_windows(v):
                    def near_rows(k, q):
                        nt = chunk(q)[3]
                        v.wait_ge(s["hid"], Q * k + q + 1)
                        need(v, s["pre"], left(k, q))
                        v.tensor_scalar(hid[q % 2][C:C + R, 0:nt * P], ps["hid"][q % 2][C:C + R, 0:nt * P],
                                        0.0, None, ALU.is_equal).then_inc(s["hot_t"], 1)

                    def add_window(k, q):
                        j, c, _, _ = chunk(q)
                        if c < NC_ - 1:
                            return
                        b = v.value_load(base_i[0:1, bass.ds(k * U + j, 1)], min_val=0, max_val=N - W)
                        v.wait_ge(s["seg"], Q * k + q + 1)
                        need(v, s[f"win{1 - j}"], k + j)
                        at = sums[0:M, bass.ds(b, W)]
                        v.tensor_tensor(at, at, ps["win"][j][0:M, 0:W], ALU.add).then_inc(s[f"win{j}"], 1)

                    def one_hot(k, q):
                        j, _, t0, nt = chunk(q)
                        need(v, s["seg"], left(k, q))
                        v.tensor_tensor(hot[q % 2][:, 0:nt * W].rearrange("p (t w) -> p t w", w=W),
                                        node_row[:, 0:W].unsqueeze(1).to_broadcast([P, nt, W]),
                                        rel[:, bass.ds((k * U + j) * T + t0, nt)].unsqueeze(2).to_broadcast([P, nt, W]),
                                        ALU.is_equal).then_inc(s["hot"], 1)

                    def add_rows(k, q):
                        j, c, _, _ = chunk(q)
                        for g, (start, _) in enumerate(GROUPS):
                            if c == start:
                                t0, t1 = group_tiles(g)
                                v.wait_ge(s[f"got{j}{g}"], 16 * (t1 - t0) * (k + 1))
                        add_gathered(v, j, q, q % 2, Q * k + q)

                    def add_constants(k, q):
                        j, c, _, _ = chunk(q)
                        if c == 0:
                            v.wait_ge(s[f"q{j}"], 16 * NC_ * (k + 1))
                            at = w_q[j][C:C + R, :].rearrange("p (k c) -> p k c", c=C)
                            v.tensor_tensor(at, at, c_all[C:C + R, :].unsqueeze(1).to_broadcast([R, NC_, C]),
                                            ALU.add).then_inc(s[f"qc{j}"], 1)

                    plan = [(0, near_rows), (0, add_constants)] if last else []
                    plan += [(2, lambda k, q: subtract_first(v, q, q % 2, Q * k + q, left(k, q))),
                             (3, lambda k, q: third_part(v, q, q % 2, Q * k + q, left(k, q))),
                             (4, add_window), (2, one_hot)]
                    if stats:
                        plan += [(0, lambda k, q: batch_statistics(v, k * U + chunk(q)[0], q, q % 2, Q * k + q))]
                    plan += [(1, add_rows)]
                    if last:
                        plan += [(2, lambda k, q: add_squares(v, q, q % 2, Q * k + q))]
                    staged(v, ITERS, Q, plan, ahead=(lambda k: split_piece(v, k)) if split_edges else None,
                           start=START, side=node_stages(v))

                NW = TILES

                def sync_general(sp):
                    if split_edges:
                        sp.wait_ge(s["wout"], 48)

                        def piece(k):
                            load_piece(sp, k)
                            store_parts(sp, k)
                        repeat(sp, ITERS, piece)
                        sp.wait_ge(s["init"], 1)
                        sp.dma_start(w_hid0_rows, w_hid0[:]).then_inc(s["whid"], 16)
                        sp.wait_ge(s["whid"], 16)
                        sp.wait_ge(s["eout"], 48 * ITERS)

                    def body(k):
                        if not opening(k):
                            sp.wait_ge(s["slab"], k)
                            sp.nop(nofuse=True)
                        load_idx(sp, 0, k)
                        load_rows(sp, 0, k)
                    repeat(sp, S, body)

                def gpsimd_general(gp):
                    def body(k):
                        need(gp, s["slab"], k)
                        if last:
                            gp.wait_ge(s["qidx"], k + 1)
                        gp.wait_ge(s["idx0"], 16 * (k + 1))
                        gp.nop(nofuse=True)
                        for t in range(T):
                            gp.indirect_dma_start(got[0][:, t * C:(t + 1) * C], None, table,
                                                  bass.IndirectOffsetOnAxis(idx[0][:, t:t + 1], 0)).then_inc(s["got00"], 16)
                            if last:
                                gp.indirect_dma_start(got[1][:, t * C:(t + 1) * C], None, q_rows,
                                                      bass.IndirectOffsetOnAxis(q_idx[:, t:t + 1], 0)).then_inc(s["got10"], 16)
                    repeat(gp, S, body)

                def tensor_general(pe):
                    def body(k):
                        pe.wait_ge(s["row0"], ROWS * (k + 1))
                        if stats:
                            pe.wait_ge(s["srow0"], 48 * (k + 1))
                        for c, (t0, nt) in enumerate(CHUNKS):
                            n = k * NC_ + c
                            hidden(pe, 0, c, 0, n, n)
                            if stats:
                                features(pe, 0, c, 0, n, n)
                            pe.wait_ge(s["rhid"], n + 1)
                            need(pe, s["add"], n)
                            for t in range(nt):
                                mm = pe.matmul(ps["pre"][0][:, t * C:(t + 1) * C], hid[0][0:C if last else C1, t * P:(t + 1) * P],
                                               (w_e1 if last else w_e0)[:], start=True, stop=True)
                            mm.then_inc(s["pre"], 1)
                            pe.wait_ge(s["part2"], n + 1)
                            pe.nop(nofuse=True)
                            with pe.Fori(0, NW) as w:
                                pe.wait_ge(s["hot"], n * NW + w + 1)
                                for t in range(nt):
                                    mm = sum_window(pe, ps["win"][0], hot[0], P, (part0[c], part1[0], part2[0]), t,
                                                    t == 0, t == nt - 1)
                                mm.then_inc(s["win1"], 1)
                            pe.drain().then_inc(s["seg"], 1)
                    repeat(pe, S, body)

                def scalar_general(act):
                    def body(k):
                        for c in range(NC_):
                            n = k * NC_ + c
                            relu_hidden(act, c, 0, n, n)
                            if stats:
                                relu_features(act, c, 0, n, n)
                            relu_message(act, 0, c, 0, n, n, n)
                            second_part(act, c, 0, n, n)
                            if last:
                                square_message(act, c, 0, n, n)
                    repeat(act, S, body)

                def vector_general(v):
                    if split_edges:
                        repeat(v, ITERS, lambda k: split_piece(v, k))

                    def body(k):
                        need(v, s["slab"], k)
                        v.tensor_scalar(dst[:], rel[:, bass.ds(k * T, T)], base_all[:, bass.ds(k, 1)], None,
                                        ALU.add).then_inc(s["dst"], 1)
                        v.wait_ge(s["dst"], k + 1)
                        if last:
                            v.tensor_scalar(q_idx[:], dst[:], 0.0, None, ALU.max).then_inc(s["qidx"], 1)
                        for c, (t0, nt) in enumerate(CHUNKS):
                            n = k * NC_ + c
                            if last:
                                v.wait_ge(s["hid"], n + 1)
                                v.sem_inc(s["hot_t"], 1)
                            if stats:
                                batch_statistics(v, k, c, 0, n)
                            if c == 0:
                                v.wait_ge(s["got00"], 16 * T * (k + 1))
                            if last:
                                if c == 0:
                                    v.wait_ge(s["got10"], 16 * T * (k + 1))
                                at = got[0][:, t0 * C:(t0 + nt) * C]
                                v.tensor_tensor(at, at, got[1][:, t0 * C:(t0 + nt) * C], ALU.add).then_inc(s["qadd"], 1)
                                v.wait_ge(s["qadd"], 2 * n + 1)
                                at3 = at.rearrange("p (t c) -> p t c", c=C)
                                v.tensor_tensor(at3, at3, c_all[:].unsqueeze(1).to_broadcast([P, nt, C]), ALU.add).then_inc(s["qadd"], 1)
                                v.wait_ge(s["qadd"], 2 * n + 2)
                            add_gathered(v, 0, c, 0, n)
                            subtract_first(v, c, 0, n, n)
                            third_part(v, c, 0, n, n)
                            with v.Fori(0, NW) as w:
                                v.tensor_scalar(off[:, 0:nt], dst[:, t0:t0 + nt], first[:, bass.ds(w, 1)], None,
                                                ALU.subtract).then_inc(s["off"], 1)
                                v.wait_ge(s["off"], n * NW + w + 1)
                                v.tensor_tensor(hot[0][:, 0:nt * P].rearrange("p (t w) -> p t w", w=P),
                                                node_row[:].unsqueeze(1).to_broadcast([P, nt, P]),
                                                off[:, 0:nt].unsqueeze(2).to_broadcast([P, nt, P]),
                                                ALU.is_equal).then_inc(s["hot"], 1)
                                v.wait_ge(s["win1"], n * NW + w + 1)
                                at = sums[0:M, bass.ds(w * P, P)]
                                v.tensor_tensor(at, at, ps["win"][0][0:M, 0:P], ALU.add).then_inc(s["win0"], 1)
                                v.wait_ge(s["win0"], n * NW + w + 1)
                            if last:
                                add_squares(v, c, 0, n)
                        v.drain().then_inc(s["slab"], 1)
                    repeat(v, S, body)

                def both(eng, windows, general):
                    flag = eng.value_load(fits[:], min_val=0, max_val=1)
                    with eng.If(flag == 1):
                        windows(eng)
                        node_steps(eng, ITERS - START, [(s[f"win{j}"], ITERS) for j in range(U)])
                    with eng.Else():
                        general(eng)
                        node_steps(eng, 0, [(s["slab"], S)])

                @block.sync
                def _(sp):
                    if split_edges:
                        sp.dma_start(w_f[:], a["w_nat"].rearrange("o p i -> (o p) i")).then_inc(s["wf"], 16)
                        for to, src in hid_loads:
                            sp.dma_start(to[:], src).then_inc(s["hf"], 16)
                    if stats:
                        sp.dma_start(y[:], a["x_tiles"]).then_inc(s["x"], 16)
                        sp.dma_start(w_hid0_at, w_hid0_rows).then_inc(s["whid"], 16)
                        sp.wait_ge(s["whid"], 16)
                        sp.nop(nofuse=True)
                    both(sp, sync_windows, sync_general)
                    if stats:
                        sp.wait_ge(s["step"], STEPS + 1)
                        sp.dma_start(p_rows[NPAD - 1:NPAD, :], none[:]).then_inc(s["pad"], 16)
                        sp.wait_ge(s["pad"], 16)

                @block.gpsimd
                def _(gp):
                    both(gp, gpsimd_windows, gpsimd_general)

                @block.tensor
                def _(pe):
                    if last:
                        pe.wait_ge(s["f_in"], 2)
                        pe.matmul(ps["f"][0][:, 0:C], spread[:], w_msg_e[:], start=True, stop=False)
                        pe.matmul(ps["f"][0][:, 0:C], ones[0:1, :], b_msg[:], start=False, stop=True).then_inc(s["f_pe"], 1)
                        pe.wait_ge(s["t_in"], 1)
                        pe.matmul(ps["tot"][0][:, 0:2 * C], ones[:], tot[:], start=True, stop=True).then_inc(s["t_pe"], 1)
                    pe.wait_ge(s["init"], 1)
                    if stats:
                        pe.wait_ge(s["whid"], 16)
                    pe.nop(nofuse=True)
                    both(pe, tensor_windows, tensor_general)

                @block.scalar
                def _(act):
                    if split_edges:
                        act.wait_ge(s["wcut"], 5)
                        for i in range(3):
                            act.dma_start(w_parts[i:i + 1, :].rearrange("o (p i) -> (o p) i", p=P), w_p[i][:]).then_inc(s["wout"], 16)
                    if last:
                        act.wait_ge(s["f_in"], 1)
                        act.activation(tmp[0:C, 3:4], tmp[0:C, 3:4], ACT.Sqrt, bias=eps[0:C, :]).then_inc(s["f_out"], 1)
                        act.wait_ge(s["t_in"], 2)
                        act.activation(var[:], var[:], ACT.Sqrt, bias=eps[:]).then_inc(s["root"], 1)
                    act.wait_ge(s["init"], 1)
                    both(act, scalar_windows, scalar_general)

                @block.vector
                def _(v):
                    prepare(v)
                    both(v, vector_windows, vector_general)

        def moments(v, ready, count, sem, k, y, parts, some, mv):
            n = UN * NODE_TILES
            v.wait_ge(ready, count)
            need(v, sem, (2 * n + 1) * k)
            for t in range(n):
                v.bn_stats(parts[:, t * 6:(t + 1) * 6], y[:, bass.ds((k * n + t) * C, C)]).then_inc(sem, 1)
            v.wait_ge(sem, (2 * n + 1) * k + n)
            v.nop(nofuse=True)
            for t in range(n):
                v.bn_aggr(some[:, 2 * t:2 * t + 2], parts[:, t * 6:(t + 1) * 6]).then_inc(sem, 1)
            v.wait_ge(sem, (2 * n + 1) * k + 2 * n)
            v.tensor_copy(mv[:, bass.ds(k * n * 2, n * 2)], some[:]).then_inc(sem, 1)

        def root(act, sem, mv, rstd):
            act.activation(rstd[:], mv[:].rearrange("p (t m) -> p m t", m=2)[:, 1, :], ACT.Sqrt, bias=eps[:]).then_inc(sem, 1)

        def scales(v, go, done, sem, mv, rstd, shift):
            v.wait_ge(sem, 1)
            go(v.reciprocal(rstd[:], rstd[:]))
            done()
            go(v.scalar_tensor_tensor(out=shift[:], in0=mv[:].rearrange("p (t m) -> p m t", m=2)[:, 0, :], scalar=-1.0,
                                      in1=rstd[:], op0=ALU.mult, op1=ALU.mult))
            done()

        def fold(v, go, done, sqrt_in, sqrt_out, mean, ex2, gb):
            go(v.tensor_tensor(tmp[0:C, 2:3], mean, mean, ALU.mult))
            done()
            go(v.tensor_tensor(tmp[0:C, 3:4], ex2, tmp[0:C, 2:3], ALU.subtract))
            done()
            v.drain().then_inc(sqrt_in, 1)
            v.wait_ge(sqrt_out, 1)
            go(v.reciprocal(tmp[0:C, 6:7], tmp[0:C, 3:4]))
            done()
            go(v.tensor_tensor(tmp[0:C, 4:5], tmp[0:C, 6:7], gb[:, 0:1], ALU.mult))
            done()
            go(v.tensor_tensor(tmp[0:C, 5:6], mean, tmp[0:C, 4:5], ALU.mult))
            done()
            go(v.tensor_tensor(lift[:, C:C1], gb[:, 1:2], tmp[0:C, 5:6], ALU.subtract))
            done()

        def finish(y, mv):
            with ExitStack() as st:
                rstd = sb("o_rstd", [P, TILES], F32, st)
                shift = sb("o_shift", [P, TILES], F32, st)
                part = [sb(f"o_sum{i}", [C + 2, STEP], F32, st) for i in range(2)]
                one_b = sb("o_one_b", [1, C + 2], F32, st)
                parts = sb("o_parts", [P, UN * NODE_TILES * 6], F32, st)
                some = sb("o_some", [P, UN * NODE_TILES * 2], F32, st)
                ps = pools(st, f=1, sq=1, y=2)
                s = Sems(st, "finish")
                block = st.enter_context(nc.Block())
                n = UN * NODE_TILES
                iters = STEPS // UN

                @block.tensor
                def _(pe):
                    def add_up(k, q):
                        pe.wait_ge(s["sum"], UN * k + q + 1)
                        need(pe, s["y"], UN * k + q - 1)
                        for t in range(NODE_TILES):
                            mm = pe.matmul(ps["y"][q % 2][:, t * C:(t + 1) * C], part[q % 2][:, t * P:(t + 1) * P], w_fin[:],
                                           start=True, stop=True)
                        mm.then_inc(s["pe"], 1)

                    for i in range(CH):
                        mm = pe.matmul(ps["sq"][0][0:C, 0:1], sumsq[:, i * C:(i + 1) * C], ones[:, 0:1],
                                       start=(i == 0), stop=(i == CH - 1))
                    mm.then_inc(s["sq"], 1)
                    pe.wait_ge(s["f_in"], 2)
                    pe.matmul(ps["f"][0][0:C + 2, 0:C], lift[:], ident[0:C, 0:C], start=True, stop=False)
                    pe.matmul(ps["f"][0][0:C + 2, 0:C], one_b[:], node_b[0:1, :], start=False, stop=True).then_inc(s["f_pe"], 1)
                    pe.wait_ge(s["w"], 1)
                    staged(pe, iters, UN, [(0, add_up)])

                @block.scalar
                def _(act):
                    def copy_sums(k, q):
                        need(act, s["pe"], UN * k + q - 1)
                        act.copy(part[q % 2][0:C1, :], sums[:, bass.ds((k * UN + q) * STEP, STEP)]).then_inc(s["sum"], 1)

                    def normalize(k):
                        for t in range(1, n, 2):
                            tile = k * n + t
                            at = y[:, bass.ds(tile * C, C)]
                            act.activation(at, at, ACT.Identity, scale=rstd[:, bass.ds(tile, 1)],
                                           bias=shift[:, bass.ds(tile, 1)]).then_inc(s["n1"], 1)

                    act.wait_ge(s["f_in"], 1)
                    act.activation(tmp[0:C, 3:4], tmp[0:C, 3:4], ACT.Sqrt, bias=eps[0:C, :]).then_inc(s["f_out"], 1)
                    act.wait_ge(s["init"], 1)
                    staged(act, iters, UN, [(0, copy_sums)])
                    act.wait_ge(s["st"], (2 * n + 1) * iters)
                    root(act, s["sqrt"], mv, rstd)
                    act.wait_ge(s["go"], 1)
                    repeat(act, iters, normalize)

                @block.vector
                def _(v):
                    def add_products(k, q):
                        v.wait_ge(s["pe"], UN * k + q + 1)
                        at = y[:, bass.ds((k * UN + q) * NODE_TILES * C, NODE_TILES * C)]
                        v.tensor_tensor(at, at, ps["y"][q % 2][:, 0:NODE_TILES * C], ALU.add).then_inc(s["y"], 1)
                        if q == UN - 1:
                            moments(v, s["y"], UN * (k + 1), s["st"], k, y, parts, some, mv)

                    def normalize(k):
                        for t in range(0, n, 2):
                            tile = k * n + t
                            at = y[:, bass.ds(tile * C, C)]
                            v.tensor_scalar(at, at, rstd[:, bass.ds(tile, 1)], shift[:, bass.ds(tile, 1)],
                                            ALU.mult, ALU.add).then_inc(s["n0"], 1)

                    go, done = chain(v, s["dve"])
                    go(v.tensor_reduce(tmp[0:C, 8:9], sums[0:C, :], AX_X, ALU.add))
                    for i in range(2):
                        go(v.memset(part[i][C:C + 2, :], 1.0))
                    go(v.memset(one_b[:], 0.0))
                    done()
                    v.drain().then_inc(s["init"], 1)
                    go(v.memset(one_b[:, C1:C + 2], 1.0))
                    go(v.tensor_scalar(tmp[0:C, 9:10], tmp[0:C, 8:9], 1.0 / E, None, ALU.mult))
                    v.wait_ge(s["sq"], 1)
                    go(v.tensor_scalar(tmp[0:C, 10:11], ps["sq"][0][0:C, 0:1], 1.0 / E, None, ALU.mult))
                    done()
                    fold(v, go, done, s["f_in"], s["f_out"], tmp[0:C, 9:10], tmp[0:C, 10:11], gb_msg)
                    v.drain().then_inc(s["f_in"], 1)
                    go(v.tensor_scalar(w_fin[0:C, :], ident[0:C, 0:C], tmp[0:C, 4:5], None, ALU.mult))
                    v.wait_ge(s["f_pe"], 1)
                    go(v.tensor_copy(w_fin[C:C + 2, :], ps["f"][0][C:C + 2, 0:C]))
                    done()
                    v.drain().then_inc(s["w"], 1)
                    staged(v, iters, UN, [(0, add_products)])
                    scales(v, go, done, s["sqrt"], mv, rstd, shift)
                    v.drain().then_inc(s["go"], 1)
                    repeat(v, iters, normalize)

                @block.sync
                def _(sp):
                    def store(k):
                        sp.wait_ge(s["n0"], n // 2 * (k + 1))
                        sp.wait_ge(s["n1"], n // 2 * (k + 1))
                        sp.nop(nofuse=True)
                        sp.dma_start(out[bass.ds(k * n * P, n * P), :].rearrange("(t p) c -> p t c", p=P),
                                     y[:, bass.ds(k * n * C, n * C)].rearrange("p (t c) -> p t c", c=C)).then_inc(s["out"], 16)
                    repeat(sp, iters, store)
                    sp.wait_ge(s["out"], 16 * iters)

        edge_pass("conv0", a["x_rows"], split_edges=True)
        y = sb("y", [P, TILES * C])
        edge_pass("conv1", h1_rows, y, stats=True)
        edge_pass("last", p_rows, y, last=True)
        finish(y, sb("mv_y2", [P, TILES * 2]))


def kernel(x, src, dst, edge_attr_4, edge_weight1, **w):
    import numpy as np
    import concourse.bacc as bacc
    from concourse.bass_utils import run_bass_kernel_spmd

    N, C = x.shape
    E = src.shape[0]
    S = slabs_of(E)
    EPAD = S * T * P
    NPAD = -(-N // (UN * NODE_TILES * P)) * UN * NODE_TILES * P
    f32 = np.float32

    def padded(v, n, fill):
        v = np.asarray(v)
        return np.concatenate([v, np.full((n - v.shape[0],) + v.shape[1:], fill, v.dtype)])

    def row(v):
        return np.asarray(v).reshape(1, -1)

    def col(v):
        return np.asarray(v).reshape(-1, 1)

    def parts_of(W, b):
        return np.tile(np.concatenate([W, W, W, b]), (3, 1))

    D = edge_attr_4.shape[1]
    rows = padded(x, NPAD, 0)
    src_p = padded(src, EPAD, NPAD - 1).reshape(S, T, P)
    dst_p = padded(dst, EPAD, -1).reshape(S, T, P)
    heads = dst_p[:, ::CH, 0]
    first_iter = S // U - inner_steps(N, NPAD, S)
    due = ((np.arange(S) // U - first_iter + 1) * NODE_TILES * P).astype(f32).reshape(1, -1)
    tail = np.zeros((3 * (3 * D + 1) + 1, R), f32)
    tail[3 * D] = -np.arange(R)
    tail[-1] = 1
    W_msg = np.asarray(w["L1_gnn_W_msg"])
    zero = np.zeros((1, C), f32)
    arrays = {
        "x_rows": rows,
        "x_tiles": rows.reshape(-1, P, C).transpose(1, 0, 2).reshape(P, -1),
        "x_cols": rows.T,
        "src_t": src_p.transpose(0, 2, 1),
        "dst_t": dst_p.transpose(2, 0, 1).reshape(P, S * T),
        "dst_n": dst_p.reshape(S, T * P),
        "heads": heads.reshape(1, -1),
        "heads_s": heads,
        "due": due,
        "w_nat": padded(edge_weight1, EPAD, 0).reshape(1, P, -1),
        "ea_nat": padded(edge_attr_4, EPAD, 0).T.reshape(D, P, -1),
        "is_edge": (np.arange(EPAD) < E).astype(mybir.dt.np(BF16)).reshape(1, -1),
        "ident": np.eye(P, dtype=f32),
        "node_row": np.tile(np.arange(P, dtype=f32), (P, 1)),
        "is_node": (np.arange(NPAD) < N).astype(f32).reshape(-1, P).T,
        "first": np.tile(np.arange(0, NPAD, P, dtype=f32), (P, 1)),
        "w_hid0": parts_of(w["L0_gnn_W_l0"], row(w["L0_gnn_b_l0"])),
        "w_e0": np.concatenate([w["L0_gnn_W_l1"], row(w["L0_gnn_b_l1"])]),
        "w_hid1": parts_of(w["L1_gnn_W_edge"], row(w["L1_gnn_b_edge"])),
        "pick0": np.repeat(np.eye(3, dtype=f32), 4, axis=0),
        "pick1": np.repeat(np.eye(3, dtype=f32), 3 * D + 1, axis=0),
        "tail": tail,
        "w_msg_e": W_msg[2 * C:],
        "b_msg": row(w["L1_gnn_b_msg"]),
        "w_wide": np.concatenate([np.concatenate([W_msg[:C], W_msg[C:2 * C], w["L1_gnn_W_node"]], axis=1),
                                  np.concatenate([zero, zero, row(w["L1_gnn_b_node"])], axis=1)]),
        "gb_edge": np.concatenate([col(w["L1_gnn_g_edge"]), col(w["L1_gnn_beta_edge"])], axis=1),
        "gb_msg": np.concatenate([col(w["L1_gnn_g_msg"]), col(w["L1_gnn_beta_msg"])], axis=1),
        "gb_node": np.concatenate([row(w["L1_gnn_g_node"]), row(w["L1_gnn_beta_node"])], axis=1),
    }
    for l in range(2):
        for i in range(2):
            arrays[f"w_conv{l}_{i}"] = np.concatenate([w[f"L0_gnn_W{l}{i}"], row(w[f"L0_gnn_b{l}{i}"])])
            arrays[f"b_conv{l}_{i}"] = col(w[f"L0_gnn_b{l}{i}"])
    arrays = {f"in_{n}": np.ascontiguousarray(v) for n, v in arrays.items()}

    nc = bacc.Bacc("TRN2", target_bir_lowering=False, num_devices=1)
    aps = {n: nc.dram_tensor(n, v.shape, mybir.dt.from_np(v.dtype), kind="ExternalInput").ap() for n, v in arrays.items()}
    out = nc.dram_tensor("out", (NPAD, C), F32, kind="ExternalOutput").ap()
    gnn_kernel(nc, {n[3:]: v for n, v in aps.items()} | {"edges": E, "nodes": N}, out)
    r = run_bass_kernel_spmd(nc, [arrays], core_ids=[0])
    return r.results[0]["out"][:N]
```
